# Optimizing a Trainium2 kernel written in Bass

```python
import numpy as np
import jax
import jax.numpy as jnp

def _softmax(x, axis=-1):
    return jax.nn.softmax(x, axis=axis)

def _gelu(x):
    return jax.nn.gelu(x, approximate=True)

def _silu(x):
    return jax.nn.silu(x)

def _sigmoid(x):
    return jax.nn.sigmoid(x)

def _layernorm(x, axis=-1, eps=1e-05):
    m = jnp.mean(x, axis=axis, keepdims=True)
    v = jnp.var(x, axis=axis, keepdims=True)
    return (x - m) / jnp.sqrt(v + eps)

def _scatter_add(tgt, idx, src, axis=0):
    return tgt.at[idx].add(src)

def _segment_sum(src, seg, n):
    return jax.ops.segment_sum(src, seg, n)
kernel_name = 'mk_xattn_ffn_d1_seqx_r8_ae6ff1'

def setup_inputs(seed: int=0):
    np.random.seed(seed)
    _w = jnp.asarray

    def _rec_inputs():
        import jax
        import jax.numpy as jnp
        _rk = jax.random.key(seed)
        x = 7.22e-05 + 1 * jax.random.normal(jax.random.fold_in(_rk, 1), (32, 128, 128), jnp.float32)
        _lenS = 128 - jax.random.randint(jax.random.fold_in(_rk, 7), (32,), 0, max(1, 128 // 4) + 1, jnp.int32)
        _lenS2 = 128 - jax.random.randint(jax.random.fold_in(_rk, 8), (32,), 0, max(1, 128 // 4) + 1, jnp.int32)
        _ctx_768P = jax.random.normal(jax.random.fold_in(_rk, 11), (32, 16, 96), jnp.float32)
        _ctx_768c = jax.random.dirichlet(jax.random.fold_in(_rk, 511), 0.3 * jnp.ones((16,), jnp.float32), (32, 128))
        _ctx_768t = jnp.einsum('bsk,bkd->bsd', _ctx_768c, _ctx_768P)
        _ctx_768t = _ctx_768t * jax.lax.rsqrt(jnp.mean(jnp.square(_ctx_768t)) + 1e-12) * 0.953939
        ctx_768 = -0.000191848 + 0.999787 * (_ctx_768t + 0.3 * jax.random.normal(jax.random.fold_in(_rk, 611), (32, 128, 96), jnp.float32))
        return (x, ctx_768)
    x, ctx_768 = _rec_inputs()

    def _L0_xattn_setup():
        import jax, jax.numpy as jnp
        import numpy as np
        NUM_HEADS = 16
        CLAMP = 10000.0
        key = jax.random.key(seed)
        ks = jax.random.split(key, 8)
        B, Nq, Nkv, Cq, Ckv = (4, 256, 256, 128, 96)
        s_q = 1.0 / np.sqrt(Cq)
        s_kv = 1.0 / np.sqrt(Ckv)
        return {'query': jax.random.normal(ks[0], (B, Nq, Cq), jnp.float32), 'key_value': jax.random.normal(ks[1], (B, Nkv, Ckv), jnp.float32), 'Wq': jax.random.normal(ks[2], (Cq, Cq), jnp.float32) * s_q, 'bq': jnp.zeros((Cq,), jnp.float32), 'Wk': jax.random.normal(ks[3], (Ckv, Cq), jnp.float32) * s_kv, 'bk': jnp.zeros((Cq,), jnp.float32), 'Wv': jax.random.normal(ks[4], (Ckv, Cq), jnp.float32) * s_kv, 'bv': jnp.zeros((Cq,), jnp.float32), 'Wo': jax.random.normal(ks[5], (Cq, Cq), jnp.float32) * s_q, 'bo': jnp.zeros((Cq,), jnp.float32)}
    _L0_xattn_all = _L0_xattn_setup()
    _L0_xattn_in = {k: v for k, v in _L0_xattn_all.items() if k in ('Wq', 'bq', 'Wk', 'bk', 'Wv', 'bv', 'Wo', 'bo')}
    del _L0_xattn_all

    def _L0_ffn_setup():
        import jax, jax.numpy as jnp
        import numpy as np
        B, S, D, FF, E, TOP_K = (4, 256, 128, 512, 8, 2)

        def _hybrid_moe(x, Wr, br, Wg, bg, W1, b1, W2, b2, D1, d1b, D2, d2b):
            b, s, d = x.shape
            t = x.reshape(-1, d)
            T = t.shape[0]
            rp = jax.nn.softmax(x @ Wr + br, axis=-1)
            gp = jax.nn.softmax(t @ Wg + bg, axis=-1)
            vals, idx = jax.lax.top_k(gp, TOP_K)
            vals = vals / jnp.sum(vals, axis=-1, keepdims=True)
            cw = jnp.zeros((T, E), t.dtype).at[jnp.arange(T)[:, None], idx].add(vals)
            h = jax.nn.relu(jnp.einsum('td,edf->tef', t, W1) + b1)
            eo = jnp.einsum('tef,efd->ted', h, W2) + b2
            moe = jnp.einsum('te,ted->td', cw, eo).reshape(b, s, d)
            dense = jax.nn.relu(x @ D1 + d1b) @ D2 + d2b
            return rp[..., 0:1] * moe + rp[..., 1:2] * dense
        key = jax.random.key(seed)
        ks = jax.random.split(key, 13)
        sd = 1.0 / np.sqrt(D)
        sf = 1.0 / np.sqrt(FF)
        return {'x': jax.random.normal(ks[0], (B, S, D), jnp.float32), 'Wr': jax.random.normal(ks[1], (D, 2), jnp.float32) * sd, 'br': jnp.zeros((2,), jnp.float32), 'Wg': jax.random.normal(ks[2], (D, E), jnp.float32) * sd, 'bg': jnp.zeros((E,), jnp.float32), 'W1': jax.random.normal(ks[3], (E, D, FF), jnp.float32) * sd, 'b1': jnp.zeros((E, FF), jnp.float32), 'W2': jax.random.normal(ks[4], (E, FF, D), jnp.float32) * sf, 'b2': jnp.zeros((E, D), jnp.float32), 'D1': jax.random.normal(ks[5], (D, FF), jnp.float32) * sd, 'd1b': jnp.zeros((FF,), jnp.float32), 'D2': jax.random.normal(ks[6], (FF, D), jnp.float32) * sf, 'd2b': jnp.zeros((D,), jnp.float32)}
    _L0_ffn_all = _L0_ffn_setup()
    _L0_ffn_in = {k: v for k, v in _L0_ffn_all.items() if k in ('Wr', 'br', 'Wg', 'bg', 'W1', 'b1', 'W2', 'b2', 'D1', 'd1b', 'D2', 'd2b')}
    del _L0_ffn_all
    return {'x': x, 'ctx_768': ctx_768, 'L0_xattn_Wq': _L0_xattn_in['Wq'], 'L0_xattn_bq': _L0_xattn_in['bq'], 'L0_xattn_Wk': _L0_xattn_in['Wk'], 'L0_xattn_bk': _L0_xattn_in['bk'], 'L0_xattn_Wv': _L0_xattn_in['Wv'], 'L0_xattn_bv': _L0_xattn_in['bv'], 'L0_xattn_Wo': _L0_xattn_in['Wo'], 'L0_xattn_bo': _L0_xattn_in['bo'], 'L0_ffn_Wr': _L0_ffn_in['Wr'], 'L0_ffn_br': _L0_ffn_in['br'], 'L0_ffn_Wg': _L0_ffn_in['Wg'], 'L0_ffn_bg': _L0_ffn_in['bg'], 'L0_ffn_W1': _L0_ffn_in['W1'], 'L0_ffn_b1': _L0_ffn_in['b1'], 'L0_ffn_W2': _L0_ffn_in['W2'], 'L0_ffn_b2': _L0_ffn_in['b2'], 'L0_ffn_D1': _L0_ffn_in['D1'], 'L0_ffn_d1b': _L0_ffn_in['d1b'], 'L0_ffn_D2': _L0_ffn_in['D2'], 'L0_ffn_d2b': _L0_ffn_in['d2b']}

def reference(x, ctx_768, L0_xattn_Wq, L0_xattn_bq, L0_xattn_Wk, L0_xattn_bk, L0_xattn_Wv, L0_xattn_bv, L0_xattn_Wo, L0_xattn_bo, L0_ffn_Wr, L0_ffn_br, L0_ffn_Wg, L0_ffn_bg, L0_ffn_W1, L0_ffn_b1, L0_ffn_W2, L0_ffn_b2, L0_ffn_D1, L0_ffn_d1b, L0_ffn_D2, L0_ffn_d2b):
    import jax
    import jax.numpy as jnp

    def _L0_xattn_ref(query, key_value, Wq, bq, Wk, bk, Wv, bv, Wo, bo):
        import jax, jax.numpy as jnp
        import numpy as np
        NUM_HEADS = 16
        CLAMP = 10000.0
        B, Nq, Cq = query.shape
        Nkv = key_value.shape[1]
        H = NUM_HEADS
        D = Cq // H
        scale = D ** (-0.5)
        q = (query @ Wq + bq).reshape(B, Nq, H, D).transpose(0, 2, 1, 3)
        k = (key_value @ Wk + bk).reshape(B, Nkv, H, D).transpose(0, 2, 1, 3)
        v = (key_value @ Wv + bv).reshape(B, Nkv, H, D).transpose(0, 2, 1, 3)
        attn = jnp.einsum('bhqd,bhkd->bhqk', q, k) * scale
        attn = jnp.clip(attn, -CLAMP, CLAMP)
        attn = jax.nn.softmax(attn, axis=-1)
        attn = jnp.where(jnp.any(jnp.isnan(attn)), jnp.asarray(1.0 / Nkv, attn.dtype), attn)
        x = jnp.einsum('bhqk,bhkd->bqhd', attn, v).reshape(B, Nq, Cq)
        return x @ Wo + bo

    def _L0_ffn_ref(x, Wr, br, Wg, bg, W1, b1, W2, b2, D1, d1b, D2, d2b):
        import jax, jax.numpy as jnp
        import numpy as np
        B, S, D, FF, E, TOP_K = (4, 256, 128, 512, 8, 2)

        def _hybrid_moe(x, Wr, br, Wg, bg, W1, b1, W2, b2, D1, d1b, D2, d2b):
            b, s, d = x.shape
            t = x.reshape(-1, d)
            T = t.shape[0]
            rp = jax.nn.softmax(x @ Wr + br, axis=-1)
            gp = jax.nn.softmax(t @ Wg + bg, axis=-1)
            vals, idx = jax.lax.top_k(gp, TOP_K)
            vals = vals / jnp.sum(vals, axis=-1, keepdims=True)
            cw = jnp.zeros((T, E), t.dtype).at[jnp.arange(T)[:, None], idx].add(vals)
            h = jax.nn.relu(jnp.einsum('td,edf->tef', t, W1) + b1)
            eo = jnp.einsum('tef,efd->ted', h, W2) + b2
            moe = jnp.einsum('te,ted->td', cw, eo).reshape(b, s, d)
            dense = jax.nn.relu(x @ D1 + d1b) @ D2 + d2b
            return rp[..., 0:1] * moe + rp[..., 1:2] * dense
        return _hybrid_moe(x, Wr, br, Wg, bg, W1, b1, W2, b2, D1, d1b, D2, d2b)
    x = x + _L0_xattn_ref(_layernorm(x, axis=-1), ctx_768, L0_xattn_Wq, L0_xattn_bq, L0_xattn_Wk, L0_xattn_bk, L0_xattn_Wv, L0_xattn_bv, L0_xattn_Wo, L0_xattn_bo)
    x = x + _L0_ffn_ref(_layernorm(x, axis=-1), L0_ffn_Wr, L0_ffn_br, L0_ffn_Wg, L0_ffn_bg, L0_ffn_W1, L0_ffn_b1, L0_ffn_W2, L0_ffn_b2, L0_ffn_D1, L0_ffn_d1b, L0_ffn_D2, L0_ffn_d2b)
    return x

_drawn_inputs = setup_inputs


def setup_inputs(seed=0):
    import zlib

    import numpy as np

    out = dict(_drawn_inputs(seed))
    spreads = {'L0_xattn_bq': (0.0, 0.1),
     'L0_xattn_bk': (0.0, 0.8),
     'L0_xattn_bv': (0.0, 0.1),
     'L0_xattn_bo': (0.0, 0.1),
     'L0_ffn_br': (0.0, 0.382),
     'L0_ffn_bg': (0.0, 0.1),
     'L0_ffn_b1': (0.0, 0.34),
     'L0_ffn_b2': (0.0, 0.1),
     'L0_ffn_d1b': (0.0, 0.277),
     'L0_ffn_d2b': (0.0, 0.1)}
    factors = {}
    for name, (base, spread) in spreads.items():
        noise = np.random.default_rng([zlib.crc32(name.encode()), seed]).standard_normal(out[name].shape)
        drawn = base * np.exp(spread * noise) if base else spread * noise
        out[name] = jnp.asarray(drawn.astype(out[name].dtype))
    for name, factor in factors.items():
        out[name] = (out[name] * factor).astype(out[name].dtype)
    return out
```

```python
from contextlib import ExitStack

import concourse.bass as bass
from concourse import mybir

ALU = mybir.AluOpType
ACT = mybir.ActivationFunctionType
AX = mybir.AxisListType
F32 = mybir.dt.float32
F32R = mybir.dt.float32r
F16 = mybir.dt.float16
I32 = mybir.dt.int32
U32 = mybir.dt.uint32

P = 128
CLAMP = 10000.0
EPS = 1e-5
TINY_EXPONENT = 87.0
TINY = 1.6458115e-38
WSCALE = 16.0


def cross_attention_moe(nc, x, ctx_in, wq, bq, wk, bk, wv, bv, wo, bo, wr, br, wg, bg,
                        w1, b1, w2, b2, d1, d1b, d2, d2b, out):
    NB, _, C = x.shape
    CK = ctx_in.shape[2]
    H = 16
    D = C // H
    E = wg.shape[1]
    FF = w1.shape[2]
    FC = FF // P
    TOP = 2
    T = NB * P
    G = 4
    NG = NB // G
    GT = G * P
    HG = H // 4
    RD = E + 2
    ROW = C + 2 * E
    CAP = T + P
    NT = TOP * T // P + E
    assert NT % 4 == 0 and NG == 8 and C == P and H * D == C
    q_scale = float(D) ** -0.5
    floor_max = -CLAMP + TINY_EXPONENT

    rows = nc.dram_tensor("routed_rows", (E * CAP + P, ROW), F32, kind="Internal").ap()
    expert_out = nc.dram_tensor("expert_out", (TOP * T, C), F32, kind="Internal").ap()
    x_v = x.rearrange("b s c -> s b c")
    out_v = out.rearrange("b s c -> s b c")
    ctx_v = ctx_in.rearrange("b s c -> s b c")
    w1_v = w1.rearrange("e d f -> d e f")
    w2_v = w2.rearrange("e (c p) d -> p e c d", p=P)
    d2_v = d2.rearrange("(c p) d -> p c d", p=P)
    b1_v = b1.rearrange("e (c p) -> p e c", p=P)
    d1b_v = d1b.rearrange("(c p) -> p c", p=P)

    with ExitStack() as stack:
        def sb(name, shape, dt=F32):
            return stack.enter_context(nc.sbuf_tensor(name, shape, dt))

        def sem(name):
            return stack.enter_context(nc.semaphore(name))

        wq_sb = sb("wq_sb", [P, C])
        wk_sb = sb("wk_sb", [CK, C])
        wv_sb = sb("wv_sb", [CK, C])
        wo_sb = sb("wo_sb", [P, C])
        qb_col = sb("qb_col", [P, 1])
        kb_col = sb("kb_col", [P, 1])
        vb_row = sb("vb_row", [P, C])
        ob_row = sb("ob_row", [P, C])
        wr_sb = sb("wr_sb", [P, RD])
        wr_part = sb("wr_part", [P, 2, RD], F16)
        rb_row = sb("rb_row", [P, RD])
        w1_raw = sb("w1_raw", [P, 2, FF])
        w1_part = sb("w1_part", [P, 2, (E + 1) * FF], F16)
        w2_sb = sb("w2_sb", [P, (E + 1) * FC * C])
        b1_sb = sb("b1_sb", [P, (E + 1) * FC])
        b2_sb = sb("b2_sb", [E + 1, C])
        ident = sb("ident", [P, P])
        ident16 = sb("ident16", [P, P], F16)
        sel_raw = sb("sel_raw", [P, 3, 4 * P])
        sel = sb("sel", [P, 4, 4 * P], F32R)
        pick_raw = sb("pick_raw", [P, HG, P])
        pick = sb("pick", [P, HG, P], F32R)
        before = sb("before", [P, P], F16)
        ones16 = sb("ones16", [P, P], F16)
        expert_no = sb("expert_no", [P, E])
        half = sb("half", [P, G])
        target0 = sb("target0", [P, G])
        pad_rows = sb("pad_rows", [P, ROW])
        xs = sb("xs", [P, NB, C])
        tokT = sb("tokT", [P, 2, T], F16)
        dense_w = sb("dense_w", [P, NB])
        ctx_sb = sb("ctx_sb", [P, 2, G, CK])
        ln_raw = sb("ln_raw", [P, 2, G, 6])
        ln_mv = sb("ln_mv", [P, 2, G, 2])
        ln_eps = sb("ln_eps", [P, 2, G])
        ln_rstd = sb("ln_rstd", [P, 2, G])
        xn = sb("xn", [P, G, C])
        xnT = sb("xnT", [P, GT])
        ctxT = sb("ctxT", [CK, GT])
        q_part = sb("q_part", [P, 2, GT], F32R)
        k_part = sb("k_part", [P, 2, GT], F32R)
        q_rows = sb("q_rows", [P, 2, HG, GT], F32R)
        k_rows = sb("k_rows", [P, 2, HG, GT], F32R)
        v_sb = sb("v_sb", [P, 2, G, H, 32])
        score_max = sb("score_max", [P, 2, 4, HG])
        shift = sb("shift", [P, 2, 4, HG])
        shift_part = sb("shift_part", [P, 2, 4, 32], F32R)
        shiftT = sb("shiftT", [P, 2, P], F32R)
        probs = sb("probs", [P, 2, 2 * HG, P])
        oT = sb("oT", [P, HG * P])
        sums_inv = sb("sums_inv", [P, H])
        att = sb("att", [P, 2, G, C])
        attT = sb("attT", [P, GT])
        tok = sb("tok", [P, G, C])
        pay = sb("pay", [P, 2, G, ROW])
        lg = sb("lg", [P, G, 24])
        top_at = sb("top_at", [P, G, 8], U32)
        mask = sb("mask", [P, G, TOP, E])
        chosen = sb("chosen", [P, G, E], F16)
        count = sb("count", [P, E])
        pos = sb("pos", [P, G, E])
        mpos = sb("mpos", [P, G, TOP, E])
        slot_at = sb("slot_at", [P, 2, G, TOP], I32)
        dif = sb("dif", [P, G, 2, 2])
        dif_exp = sb("dif_exp", [P, G, 2, 2])
        dif_sum = sb("dif_sum", [P, G, 2, 2])
        share = sb("share", [P, G, 2, 2])
        wsh = sb("wsh", [P, G, TOP])
        wmask = sb("wmask", [P, G, TOP, E])
        mixw = sb("mixw", [P, G, E + 1])
        mixT = sb("mixT", [E + 1, GT])
        cum_mask = sb("cum_mask", [1, E, E])
        tile_no = sb("tile_no", [1, NT + 4])
        n_tok = sb("n_tok", [1, E])
        n_i = sb("n_i", [1, E], I32)
        n_tiles_i = sb("n_tiles_i", [1, E], I32)
        n_tiles = sb("n_tiles", [1, E])
        cum_w = sb("cum_w", [1, E, E])
        cum = sb("cum", [1, E])
        past = sb("past", [1, NT + 4, E])
        past_w = sb("past_w", [1, NT + 4, E])
        tile_e = sb("tile_e", [1, NT + 4])
        tile_s = sb("tile_s", [1, NT + 4])
        tile_r = sb("tile_r", [1, NT + 4])
        tab_e = sb("tab_e", [1, NT + 4], I32)
        tab_row = sb("tab_row", [1, NT + 4], I32)
        tab_pad = sb("tab_pad", [1, E], I32)
        row_sb = sb("row_sb", [P, 4, ROW])
        tileT = sb("tileT", [P, 2, 2 * P], F16)
        hid = sb("hid", [P, 2, FC, P])
        y_sb = sb("y_sb", [P, 4, C])
        y_at = sb("y_at", [P, 4], I32)
        y_back = v_sb[:, 0, :, :, :].rearrange("p s h d -> p (s h d)").rearrange("p (a s c) -> p a s c", a=2, s=G)

        ps_score = stack.enter_context(nc.psum_tensor("ps_score", [P, 2, 512], F32))
        ps_st = stack.enter_context(nc.psum_tensor("ps_st", [P, 2, 2, 512], F32))
        ps_stage = stack.enter_context(nc.psum_tensor("ps_stage", [P, 512], F32))
        ps_att = stack.enter_context(nc.psum_tensor("ps_att", [P, 512], F32))

        y_bank = (ps_stage, ps_att)

        def hid_bank(j, c):
            half_c, at = c // (FC // 2), c % (FC // 2)
            return ps_st[:, half_c, j % 2, at * P:(at + 1) * P]

        small_loaded = sem("small_loaded")
        x0_loaded = sem("x0_loaded")
        x_loaded = sem("x_loaded")
        ctx_loaded = [sem(f"ctx_loaded{i}") for i in range(2)]
        w1_loaded = [sem(f"w1_loaded{i}") for i in range(2)]
        ffn_loaded = sem("ffn_loaded")
        consts = sem("consts")
        consts_s = sem("consts_s")
        consts_v = sem("consts_v")
        ln_stats = [sem("ln1_stats"), sem("ln2_stats")]
        ln_aggr = [sem("ln1_aggr"), sem("ln2_aggr")]
        ln_inv = [sem("ln1_inv"), sem("ln2_inv")]
        xn_ready = sem("xn_ready")
        xbo_ready = sem("xbo_ready")
        stage_filled = sem("stage_filled")
        stage_copied = sem("stage_copied")
        q_high = sem("q_high")
        k_high = sem("k_high")
        score_filled = sem("score_filled")
        max_done = sem("max_done")
        shift_steps = sem("shift_steps")
        shift_turned = sem("shift_turned")
        shift_copied = sem("shift_copied")
        st_filled = sem("st_filled")
        exp_done = sem("exp_done")
        clamp_done = sem("clamp_done")
        pv_done = sem("pv_done")
        o_copied = sem("o_copied")
        o_turned = sem("o_turned")
        sums_ready = sem("sums_ready")
        att_ready = sem("att_ready")
        tok_ready = sem("tok_ready")
        tok_high = sem("tok_high")
        tok_low = sem("tok_low")
        route = sem("route")
        dif_exped = sem("dif_exped")
        scattered = [sem(f"scattered{i}") for i in range(2)]
        w1_split = sem("w1_split")
        tab_steps = sem("tab_steps")
        table = sem("table")
        pads_written = sem("pads_written")
        hid_filled = sem("hid_filled")
        relu_s = sem("relu_s")
        relu_v = sem("relu_v")
        y_filled = sem("y_filled")
        y_target = sem("y_target")
        y_ready = sem("y_ready")
        tile_filled = sem("tile_filled")
        tile_copied = sem("tile_copied")
        row_loaded = [sem(f"row_loaded{i}") for i in range(4)]
        y_sent = [sem(f"y_sent{i}") for i in range(4)]
        back_loaded = [sem(f"back_loaded{i}") for i in range(2)]
        sum1 = sem("sum1")
        sum2 = sem("sum2")
        stored = sem("stored")

        PRE = ["ctxT", "xT", "q", "k", "v", "qr0", "qr1", "qr2", "qr3", "kr0", "kr1", "kr2", "kr3"]
        POST = ["attT", "wo", "tokT", "logits", "rank", "mixT", "bias"]
        GAPS = [
            {"a": ["ctxT"], "b": ["attT"], "d": ["wo"]},
            {"a": ["xT"], "b": ["q"], "c": ["k"], "d": ["v"], "e": ["tokT"]},
            {"a": ["qr0"], "b": ["qr1"], "c": ["qr2"], "d": ["qr3"], "e": ["kr0"], "f": ["logits"]},
            {"a": ["kr1"], "b": ["kr2", "kr3"], "d": ["rank"], "e": ["mixT"], "f": ["bias"]},
        ]
        FULL = [name for slot in GAPS for gap in sorted(slot) for name in slot[gap]]
        NPRE, NPOST, NFULL = len(PRE), len(POST), len(FULL)
        SMALL = 14
        POOL_CONSTS, S_CONSTS, V_CONSTS = 27, 3, 13
        IDENT_AT = 8
        ROUTE, ROUTE_DIF, ROUTE_CHOSEN, ROUTE_MIX = 25, 10, 12, 20
        SENT = 16 * TOP * G
        FREE = 2

        def bodies(eng, prologue, body, tail):
            def no(base, names, turn=0):
                return {name: NFULL * turn + base + i for i, name in enumerate(names)}

            prologue(no(0, PRE))
            body(0, 0, -1, no(NPRE, PRE), True, False)
            with eng.Fori(0, (NG - 2) // 2) as i:
                for u in range(2):
                    body(2 * i + 1 + u, (1 + u) % 2, i, no(2 * NPRE + NFULL * u, FULL, 2 * i), True, True)
            body(NG - 1, 1, (NG - 2) // 2, no(2 * NPRE + NFULL * (NG - 2), POST), False, True)
            tail(NG - 1, 1, (NG - 1) // 2, no(2 * NPRE + NFULL * (NG - 2) + NPOST, POST))

        def in_gap(s, which, no):
            return [name for name in GAPS[s].get(which, []) if name in no]

        def hold(eng, s, value):
            eng.wait_ge(s, value)
            eng.nop(nofuse=True)

        block = stack.enter_context(nc.Block())

        @block.sync
        def _(sp):
            sp.dma_start(xs[:, 0:G, :], x_v[:, 0:G, :]).then_inc(x0_loaded, 16)
            sp.dma_start(ctx_sb[:, 0, :, :], ctx_v[:, 0:G, :]).then_inc(ctx_loaded[0], 16)

            def row(v, n=P):
                return v.rearrange("(a n) -> a n", a=1).to_broadcast([n, v.shape[0]])

            small = [(wq_sb[:, :], wq), (wk_sb[:, :], wk), (wv_sb[:, :], wv), (wo_sb[:, :], wo),
                     (qb_col[:, :], bq.rearrange("(p a) -> p a", a=1)),
                     (kb_col[:, :], bk.rearrange("(p a) -> p a", a=1)),
                     (vb_row[:, :], row(bv)), (ob_row[:, :], row(bo)), (wr_sb[:, 0:2], wr), (wr_sb[:, 2:RD], wg),
                     (rb_row[:, 0:2], row(br)), (rb_row[:, 2:RD], row(bg)),
                     (b2_sb[0:E, :], b2), (b2_sb[E:E + 1, :], row(d2b, 1))]
            assert len(small) == SMALL
            for dst, src in small:
                sp.dma_start(dst, src).then_inc(small_loaded, 16)
            sp.dma_start(ctx_sb[:, 1, :, :], ctx_v[:, G:2 * G, :]).then_inc(ctx_loaded[1], 16)
            sp.dma_start(xs[:, G:NB, :], x_v[:, G:NB, :]).then_inc(x_loaded, 16)
            sp.dma_start(w2_sb[:, 0:E * FC * C].rearrange("p (e c d) -> p e c d", e=E, c=FC), w2_v)\
              .then_inc(ffn_loaded, 16)
            sp.dma_start(w2_sb[:, E * FC * C:].rearrange("p (c d) -> p c d", c=FC), d2_v).then_inc(ffn_loaded, 16)
            with nc.allow_non_contiguous_dma(reason="hidden biases become columns"):
                sp.dma_start(b1_sb[:, 0:E * FC].rearrange("p (e c) -> p e c", e=E), b1_v).then_inc(ffn_loaded, 16)
                sp.dma_start(b1_sb[:, E * FC:], d1b_v).then_inc(ffn_loaded, 16)
            for e in range(E + 1):
                if e >= 2:
                    sp.wait_ge(w1_split, 3 * (e - 1))
                sp.dma_start(w1_raw[:, e % 2, :], w1_v[:, e, :] if e < E else d1).then_inc(w1_loaded[e % 2], 16)

            def load_ctx(g, par, copied):
                sp.wait_ge(stage_copied, copied)
                sp.dma_start(ctx_sb[:, par, :, :], ctx_v[:, bass.ds(G * g, G), :]).then_inc(ctx_loaded[par], 16)

            load_ctx(2, 0, 1)
            load_ctx(3, 1, NPRE + 1)
            with sp.Fori(0, (NG - 4) // 2) as i:
                for u in range(2):
                    load_ctx(2 * i + 4 + u, u, 2 * NFULL * i + 2 * NPRE + NFULL * u + 1)

            sp.wait_ge(table, 1)
            for e in range(E):
                r = sp.value_load(tab_pad[0:1, e:e + 1], min_val=0, max_val=E * CAP - P)
                sp.dma_start(rows[bass.ds(r, P), :], pad_rows[:, :]).then_inc(pads_written, 16)
            sp.wait_ge(pads_written, 16 * E)
            for j in range(4):
                sp.wait_ge(y_sent[j], 16)
            for par in range(2):
                sp.wait_ge(scattered[par], SENT * NG // 2 + 16)
            sp.wait_ge(table, 2)

            def load_rows(k, j, used):
                r = sp.value_load(tab_row[0:1, bass.ds(k, 1)], min_val=0, max_val=E * CAP)
                if used is not None:
                    sp.wait_ge(y_ready, used)
                sp.dma_start(row_sb[:, j, :], rows[bass.ds(r, P), :]).then_inc(row_loaded[j], 16)

            for j in range(4):
                load_rows(j, j, None)
            with sp.Fori(1, NT // 4) as it:
                for j in range(4):
                    load_rows(4 * it + j, j, 4 * it + (j - 3 + NB + FREE))

            for j in range(4):
                sp.wait_ge(y_sent[j], 16 * NT // 4 + 16)
            back_v = expert_out.rearrange("(b p t) c -> p b (t c)", p=P, t=TOP)

            def store(g):
                sp.wait_ge(sum2, g + 1)
                sp.dma_start(out_v[:, G * g:G * g + G, :], xs[:, G * g:G * g + G, :]).then_inc(stored, 16)

            for g in range(NG):
                if g >= 2:
                    sp.wait_ge(sum2, g - 1)
                sp.dma_start(y_back[:, g % 2, :, :], back_v[:, G * g:G * g + G, :]).then_inc(back_loaded[g % 2], 16)
                if g >= 1:
                    store(g - 1)
            store(NG - 1)
            sp.wait_ge(stored, 16 * NG)

        @block.gpsimd
        def _(pool):
            n = 0

            def made(ins):
                nonlocal n
                n += 1
                ins.then_inc(consts, 1)

            made(pool.memset(ident[:, :], 0.0))
            made(pool.memset(half[:, :], -0.5))
            made(pool.memset(sel_raw[:, :, :], 0.0))
            made(pool.memset(pick_raw[:, :, :], 0.0))
            made(pool.memset(pad_rows[:, :], 0.0))
            made(pool.memset(cum_mask[:, :, :], 1.0))
            made(pool.memset(before[:, :], 1.0))
            pool.wait_ge(consts, n)
            made(pool.affine_select(out=ident[:, :], in_=ident[:, :], compare_op=ALU.not_equal, fill=1.0,
                                    base=0, pattern=[[-1, P]], channel_multiplier=1))
            assert n == IDENT_AT

            def rstd(which, g):
                hold(pool, ln_aggr[which], G * g + G)
                pool.tensor_scalar(ln_eps[:, which, :], ln_mv[:, which, :, 1], EPS, None, ALU.add)\
                    .then_inc(ln_inv[which], 1)
                pool.wait_ge(ln_inv[which], 2 * g + 1)
                pool.tensor_tensor(ln_rstd[:, which, :], ln_eps[:, which, :], half[:, :], ALU.pow)\
                    .then_inc(ln_inv[which], 1)

            rstd(0, 0)
            for r in range(3):
                v = sel_raw[:, r, :].rearrange("c (m j r d) -> c m j r d", m=HG, j=4, r=4)[:, :, :, r, :]
                made(pool.affine_select(out=v, in_=v, compare_op=ALU.not_equal, fill=1.0, base=0,
                                        pattern=[[-32, HG], [-8, 4], [-1, D]], channel_multiplier=1))
            for r in range(0, P, 32):
                for low in range(2):
                    pool.wait_ge(consts, n)
                    made(pool.affine_select(out=pick_raw[:, :, :], in_=pick_raw[:, :, :], compare_op=ALU.not_equal,
                                            fill=1.0, base=-(r + HG * low), pattern=[[-1, HG], [0, P]],
                                            channel_multiplier=1))
            made(pool.iota(expert_no[:, :], [[1, E]], base=0, channel_multiplier=0,
                           allow_small_or_imprecise_dtypes=True))
            made(pool.iota(target0[:, :], [[TOP * P, G]], base=0, channel_multiplier=TOP,
                           allow_small_or_imprecise_dtypes=True))
            made(pool.iota(count[:, :], [[CAP, E]], base=0, channel_multiplier=0,
                           allow_small_or_imprecise_dtypes=True))
            made(pool.iota(tile_no[:, :], [[1, NT + 4]], base=0, channel_multiplier=0,
                           allow_small_or_imprecise_dtypes=True))
            made(pool.iota(pad_rows[:, C + E:ROW].bitcast(I32), [[0, E]], base=TOP * T, channel_multiplier=1))
            made(pool.affine_select(out=before[:, :], in_=before[:, :], compare_op=ALU.is_gt, fill=0.0,
                                    base=0, pattern=[[1, P]], channel_multiplier=-1))
            made(pool.affine_select(out=cum_mask[:, :, :], in_=cum_mask[:, :, :], compare_op=ALU.is_ge, fill=0.0,
                                    base=0, pattern=[[1, E], [-1, E]], channel_multiplier=0))
            made(pool.memset(ones16[:, :], 1.0))
            assert n == POOL_CONSTS, n

            def add_bo(g):
                pool.wait_ge(xn_ready, G * g + G)
                pool.tensor_tensor(xs[:, bass.ds(G * g, G), :], xs[:, bass.ds(G * g, G), :],
                                   ob_row[:, :].unsqueeze(1).to_broadcast([P, G, C]), ALU.add).then_inc(xbo_ready, 1)

            def scatter(g, par):
                hold(pool, route, ROUTE * g + ROUTE)
                for s in range(G):
                    for t in range(TOP):
                        pool.indirect_dma_start(
                            rows, bass.IndirectOffsetOnAxis(ap=slot_at[:, par, s, t:t + 1], axis=0),
                            pay[:, par, s, :], None, bounds_check=E * CAP + P - 1, oob_is_err=False)\
                            .then_inc(scattered[par], 16)

            def split_w1():
                for e in range(E + 1):
                    pool.wait_ge(w1_loaded[e % 2], 16 * (e // 2 + 1))
                    raw, high = w1_raw[:, e % 2, :], w1_part[:, 0, e * FF:(e + 1) * FF]
                    pool.tensor_scalar(raw, raw, WSCALE, None, ALU.mult).then_inc(w1_split, 1)
                    pool.wait_ge(w1_split, 3 * e + 1)
                    pool.tensor_copy(high, raw).then_inc(w1_split, 1)
                    pool.wait_ge(w1_split, 3 * e + 2)
                    pool.tensor_tensor(w1_part[:, 1, e * FF:(e + 1) * FF], raw, high, ALU.subtract)\
                        .then_inc(w1_split, 1)

            pool.wait_ge(consts, POOL_CONSTS)
            piece = P // 8
            for i, s in enumerate(scattered + y_sent):
                at = slice(piece * i, piece * (i + 1) if i < 5 else P)
                pool.dma_start(rows[E * CAP + at.start:E * CAP + at.stop, :], pad_rows[at, :]).then_inc(s, 16)

            def prologue(no):
                pool.wait_ge(small_loaded, 16 * SMALL)
                add_bo(0)

            def body(g, par, half_g, no, pre, post):
                if pre:
                    rstd(0, g + 1)
                if post:
                    rstd(1, g - 1)
                if pre:
                    add_bo(g + 1)
                if post:
                    scatter(g - 1, 1 - par)
                else:
                    split_w1()

            def tail(g, par, half_g, no):
                rstd(1, g)
                scatter(g, par)

            bodies(pool, prologue, body, tail)

            with pool.Fori(0, NT // 4) as it:
                for j in range(4):
                    hold(pool, y_ready, 4 * it + (j + 1 + NB + FREE))
                    pool.indirect_dma_start(
                        expert_out, bass.IndirectOffsetOnAxis(ap=y_at[:, j:j + 1], axis=0), y_sb[:, j, :], None,
                        bounds_check=TOP * T - 1, oob_is_err=False).then_inc(y_sent[j], 16)

        def tiles(eng, n, step):
            with eng.Fori(0, n // 4 - 1) as it:
                for j in range(4):
                    step(4 * it + j, j, it, 2)
            for j in range(4):
                step(n - 4 + j, j, n // 4 - 1, 3 - j)

        @block.scalar
        def _(act):
            act.wait_ge(consts, IDENT_AT)
            act.copy(ident16[:, :], ident[:, :]).then_inc(consts_s, 1)
            act.wait_ge(small_loaded, 16 * SMALL)
            act.mul(wq_sb[:, :], wq_sb[:, :], q_scale).then_inc(consts_s, 1)
            act.mul(qb_col[:, :], qb_col[:, :], q_scale).then_inc(consts_s, 1)
            act.wait_ge(consts_s, S_CONSTS)

            def stage(name, g, no, par):
                if name in ("v", "wo", "logits", "rank", "bias"):
                    return
                act.wait_ge(stage_filled, no[name] + 1)
                if name in ("q", "k"):
                    part, col, s = (q_part, qb_col, q_high) if name == "q" else (k_part, kb_col, k_high)
                    act.activation(part[:, 0, :], ps_stage[:, :], ACT.Identity, bias=col[:, :]).then_inc(s, 1)
                    return
                if name == "tokT":
                    dst = tokT[:, :, bass.ds(g * GT, GT)].rearrange("p h (s t) -> p s h t", s=G)
                    src = ps_stage[:, :].bitcast(F16).rearrange("p (s h t) -> p s h t", s=G, h=2)
                else:
                    dst, src = {
                        "ctxT": lambda: (ctxT[:, :], ps_stage[0:CK, :]),
                        "xT": lambda: (xnT[:, :], ps_stage[:, :]),
                        "qr": lambda: (q_rows[:, par, int(name[2]), :], ps_stage[:, :]),
                        "kr": lambda: (k_rows[:, par, int(name[2]), :], ps_stage[:, :]),
                        "attT": lambda: (attT[:, :], ps_stage[:, :]),
                        "mixT": lambda: (mixT[:, :], ps_stage[0:E + 1, :]),
                    }[name.rstrip("0123")]()
                act.copy(dst, src).then_inc(stage_copied, 1)

            def token_high(g, par, sent):
                act.wait_ge(scattered[par], sent + 16)
                act.wait_ge(tok_ready, G * g + G)
                act.copy(pay[:, par, :, 0:C // 2].bitcast(F16), tok[:, :, :]).then_inc(tok_high, 1)

            def router_exp(g):
                act.wait_ge(route, ROUTE * g + ROUTE_DIF)
                act.activation(dif_exp[:, :, :, :], dif[:, :, :, :], ACT.Exp).then_inc(dif_exped, 1)

            def shift_copy(b, p):
                act.wait_ge(shift_turned, b + 1)
                act.copy(shiftT[:, p, :], ps_att[:, 0:P]).then_inc(shift_copied, 1)

            def prologue(no):
                for name in PRE:
                    stage(name, 0, no, 0)
                shift_copy(0, 0)

            def body(g, par, half_g, no, pre, post):
                for s in range(G):
                    b = G * g + s

                    def gap(which):
                        for name in in_gap(s, which, no):
                            stage(name, g + 1 if name in PRE else g - 1, no, 1 - par)

                    def exp(unit):
                        act.wait_ge(st_filled, 2 * b + unit + 1)
                        if post or s > 0:
                            act.wait_ge(pv_done, 2 * b + unit - 1)
                        act.activation(probs[:, unit, :, :].rearrange("p h t -> p (h t)"),
                                       ps_st[:, unit, :, :].rearrange("p j t -> p (j t)"), ACT.Exp)\
                            .then_inc(exp_done, 1)

                    exp(0)
                    gap("a")
                    exp(1)
                    gap("b")
                    gap("c")
                    gap("d")
                    if s == 1 and post:
                        token_high(g - 1, 1 - par, SENT * half_g)
                    if s == 3 and post:
                        router_exp(g - 1)
                    act.wait_ge(pv_done, 2 * b + 2)
                    act.copy(oT[:, :], ps_att[:, :]).then_inc(o_copied, 1)
                    gap("e")
                    gap("f")
                    if pre or s < G - 1:
                        shift_copy(b + 1, (s + 1) % 2)

            def tail(g, par, half_g, no):
                for name in POST:
                    stage(name, g, no, par)
                    if name == "wo":
                        token_high(g, par, SENT * half_g)
                    if name == "logits":
                        router_exp(g)

            bodies(act, prologue, body, tail)

            def relu(k, j, bias):
                act.wait_ge(hid_filled, k + 1)
                act.wait_ge(y_filled, k + 1)
                for c in range(FC // 2):
                    act.activation(hid[:, j % 2, c, :], hid_bank(j, c), ACT.Relu,
                                   bias=bias(c)).then_inc(relu_s, 1)

            def dense(k, j, it, more):
                if more > 0:
                    relu(k + 1, j + 1, dense_bias)

            def dense_bias(c):
                return b1_sb[:, E * FC + c:E * FC + c + 1]

            act.wait_ge(consts_v, V_CONSTS + 1)
            act.sem_inc(relu_s, FREE * FC // 2)
            act.sem_inc(tile_copied, FREE)
            relu(0, 0, dense_bias)
            tiles(act, NB, dense)

            def tile_copy(k, j):
                act.wait_ge(tile_filled, k + 1)
                act.wait_ge(hid_filled, NB + k - 1)
                act.copy(tileT[:, j % 2, :], ps_score[:, j % 2, 0:P].bitcast(F16)).then_inc(tile_copied, 1)

            def expert_relu(k, j):
                e = act.value_load(tab_e[0:1, bass.ds(k, 1)], min_val=0, max_val=E - 1)
                relu(NB + k, j, lambda c: b1_sb[:, bass.ds(e * FC + c, 1)])

            def expert(k, j, it, more):
                if more > 1:
                    tile_copy(k + 2, j)
                if more > 0:
                    expert_relu(k + 1, j + 1)

            act.wait_ge(table, 2)
            tile_copy(0, 0)
            tile_copy(1, 1)
            expert_relu(0, 0)
            tiles(act, NT, expert)

        @block.tensor
        def _(pe):
            pe.wait_ge(consts, POOL_CONSTS)
            pe.wait_ge(consts_s, S_CONSTS)
            pe.wait_ge(consts_v, V_CONSTS)

            def score(b, unit, s, par):
                t = slice(s * P, (s + 1) * P)
                for m in range(HG):
                    for jj in range(2):
                        q4 = slice(64 * unit + 32 * jj, 64 * unit + 32 * jj + 32)
                        mm = pe.matmul(ps_score[:, jj, m * P:(m + 1) * P], q_rows[q4, par, m, t],
                                       k_rows[q4, par, m, t], start=True, stop=True, tile_position=(q4.start, 0))
                mm.then_inc(score_filled, 1)

            def scoreT(b, unit, s, par):
                t = slice(s * P, (s + 1) * P)
                for m in range(HG):
                    for jj in range(2):
                        q4 = slice(64 * unit + 32 * jj, 64 * unit + 32 * jj + 32)
                        to = ps_st[:, unit, jj, m * P:(m + 1) * P]
                        pe.matmul(to, k_rows[q4, par, m, t], q_rows[q4, par, m, t], start=True, stop=False,
                                  tile_position=(q4.start, 0))
                        mm = pe.matmul(to, pick[q4, m, :], shiftT[q4, s % 2, :], start=False, stop=True,
                                       tile_position=(q4.start, 0))
                mm.then_inc(st_filled, 1)

            def values(b, unit, s, par):
                pe.wait_ge(clamp_done, 2 * b + unit + 1)
                for m in range(HG):
                    for jj in range(2):
                        j = 2 * unit + jj
                        mm = pe.matmul(ps_att[32 * j:32 * j + 32, m * P:(m + 1) * P],
                                       v_sb[:, par, s, 4 * m + j, :], probs[:, unit, HG * jj + m, :],
                                       start=True, stop=True, tile_position=(0, 32 * j))
                mm.then_inc(pv_done, 1)

            def shift_turn(b, p):
                pe.wait_ge(shift_steps, 3 * b + 3)
                pe.transpose(ps_att[:, 0:P], shift_part[:, p, :, :].rearrange("p j r -> p (j r)").bitcast(F32),
                             ident[:, :]).then_inc(shift_turned, 1)

            def stage(name, g, no, par, ctx_at):
                if not (isinstance(no[name], int) and no[name] == 0):
                    pe.wait_ge(stage_copied, no[name])
                each = [slice(s * P, (s + 1) * P) for s in range(G)]
                if name == "ctxT":
                    pe.wait_ge(ctx_loaded[par], ctx_at)
                    for s, t in enumerate(each):
                        mm = pe.transpose(ps_stage[0:CK, t], ctx_sb[:, par, s, :], ident[:, :])
                elif name == "xT":
                    pe.wait_ge(xn_ready, G * g + G)
                    for s, t in enumerate(each):
                        mm = pe.transpose(ps_stage[:, t], xn[:, s, :], ident[:, :])
                elif name == "q":
                    mm = pe.matmul(ps_stage[:, :], wq_sb[:, :], xnT[:, :], start=True, stop=True)
                elif name == "k":
                    mm = pe.matmul(ps_stage[:, :], wk_sb[:, :], ctxT[:, :], start=True, stop=True)
                elif name == "v":
                    for t in each:
                        mm = pe.matmul(ps_stage[:, t], ctxT[:, t], wv_sb[:, :], start=True, stop=True)
                elif name[:2] in ("qr", "kr"):
                    m = int(name[2])
                    part, s0 = (q_part, 0) if name[0] == "q" else (k_part, 2)
                    for h in range(2):
                        mm = pe.matmul(ps_stage[:, :], sel[:, s0 + h, m * P:(m + 1) * P], part[:, h, :],
                                       start=(h == 0), stop=(h == 1))
                elif name == "attT":
                    pe.wait_ge(att_ready, G * g + G)
                    for s, t in enumerate(each):
                        mm = pe.transpose(ps_stage[:, t], att[:, par, s, :], ident[:, :])
                elif name == "wo":
                    for t in each:
                        mm = pe.matmul(ps_stage[:, t], attT[:, t], wo_sb[:, :], start=True, stop=True)
                elif name == "tokT":
                    pe.wait_ge(tok_low, g + 1)
                    for s in range(G):
                        for h in range(2):
                            mm = pe.transpose(ps_stage[:, :].bitcast(F16)[:, (2 * s + h) * P:(2 * s + h + 1) * P],
                                              pay[:, par, s, h * C // 2:(h + 1) * C // 2].bitcast(F16),
                                              ident16[:, :])
                elif name == "logits":
                    for s in range(G):
                        for i, (a, w) in enumerate(((0, 0), (0, 1), (1, 0))):
                            mm = pe.matmul(ps_stage[:, 16 * s:16 * s + RD],
                                           tokT[:, a, bass.ds(g * GT + s * P, P)], wr_part[:, w, :],
                                           start=(i == 0), stop=(i == 2))
                elif name == "rank":
                    pe.wait_ge(route, ROUTE * g + ROUTE_CHOSEN)
                    for s in range(G):
                        for r in range(s + 1):
                            pe.matmul(ps_stage[:, E * s:E * s + E], before[:, :] if r == s else ones16[:, :],
                                      chosen[:, r, :], start=(r == 0), stop=(r == s))
                    for s in range(G):
                        mm = pe.matmul(ps_stage[:, E * G:E * G + E], ones16[:, :], chosen[:, s, :],
                                       start=(s == 0), stop=(s == G - 1))
                elif name == "mixT":
                    pe.wait_ge(route, ROUTE * g + ROUTE_MIX)
                    for s, t in enumerate(each):
                        mm = pe.transpose(ps_stage[0:E + 1, t], mixw[:, s, :], ident[:, :])
                elif name == "bias":
                    for t in each:
                        mm = pe.matmul(ps_stage[:, t], mixT[:, t], b2_sb[:, :], start=True, stop=True)
                mm.then_inc(stage_filled, 1)

            def prologue(no):
                for name in PRE:
                    stage(name, 0, no, 0, 16)
                pe.wait_ge(stage_copied, no["kr3"] + 1)
                score(0, 0, 0, 0)
                pe.wait_ge(max_done, 1)
                score(0, 1, 0, 0)
                shift_turn(0, 0)

            def body(g, par, half_g, no, pre, post):
                for s in range(G):
                    b = G * g + s
                    more = pre or s < G - 1
                    s1, par1 = (s + 1, par) if s < G - 1 else (0, 1 - par)

                    def gap(which):
                        for name in in_gap(s, which, no):
                            stage(name, g + 1 if name in PRE else g - 1, no, 1 - par, 16 * (half_g + 2))

                    def unit_free(unit):
                        if post or s > 0:
                            pe.wait_ge(exp_done, 2 * b + unit - 1)

                    pe.wait_ge(shift_copied, b + 1)
                    unit_free(0)
                    scoreT(b, 0, s, par)
                    gap("a")
                    unit_free(1)
                    scoreT(b, 1, s, par)
                    gap("b")
                    if more:
                        if s == G - 1:
                            pe.wait_ge(stage_copied, no["kr3"] + 1)
                        pe.wait_ge(max_done, 2 * b + 2)
                        score(b + 1, 0, s1, par1)
                    gap("c")
                    values(b, 0, s, par)
                    if more:
                        pe.wait_ge(max_done, 2 * b + 3)
                        score(b + 1, 1, s1, par1)
                    gap("d")
                    values(b, 1, s, par)
                    gap("e")
                    pe.wait_ge(o_copied, b + 1)
                    for m in range(HG):
                        mm = pe.transpose(ps_att[:, m * P:(m + 1) * P], oT[:, m * P:(m + 1) * P], ident[:, :])
                    mm.then_inc(o_turned, 1)
                    gap("f")
                    if more:
                        pe.wait_ge(att_ready, b + 1)
                        shift_turn(b + 1, (s + 1) % 2)

            def tail(g, par, half_g, no):
                for name in POST:
                    stage(name, g, no, par, None)

            bodies(pe, prologue, body, tail)

            def layer1(k, j, e, x_high, x_low):
                pe.wait_ge(relu_s, 2 * k + 2)
                pe.wait_ge(relu_v, 2 * k + 2)
                for c in range(FC):
                    for i, (w, xp) in enumerate(((0, x_high), (0, x_low), (1, x_high))):
                        mm = pe.matmul(hid_bank(j, c), w1_part[:, w, bass.ds(e * FF + c * P, P)],
                                       xp, start=(i == 0), stop=(i == 2))
                mm.then_inc(hid_filled, 1)

            def layer2(k, j, e):
                pe.wait_ge(y_ready, k + 1)
                for i, c in enumerate((0, FC // 2, 1, FC // 2 + 1)):
                    pe.wait_ge(relu_s if c < FC // 2 else relu_v, 2 * k + c % (FC // 2) + 1 + FREE * FC // 2)
                    mm = pe.matmul(y_bank[j % 2][:, 0:C], hid[:, j % 2, c, :], w2_sb[:, bass.ds((e * FC + c) * C, C)],
                                   start=(i == 0), stop=(i == FC - 1))
                mm.then_inc(y_filled, 1)

            def dense_layer1(b, j):
                layer1(b, j, E, tokT[:, 0, bass.ds(b * P, P)], tokT[:, 1, bass.ds(b * P, P)])

            def dense(k, j, it, more):
                if more > 0:
                    dense_layer1(k + 1, j + 1)
                layer2(k, j, E)

            pe.wait_ge(w1_split, 3 * (E + 1))
            pe.wait_ge(ffn_loaded, 16 * 4)
            pe.wait_ge(exp_done, 2 * NB)
            pe.sem_inc(y_filled, FREE)
            dense_layer1(0, 0)
            pe.wait_ge(stage_copied, 2 * NPRE + NFULL * (NG - 2) + 2 * NPOST)
            pe.wait_ge(att_ready, NB)
            tiles(pe, NB, dense)

            def turn(k, j, it):
                pe.wait_ge(row_loaded[j % 4], 16 * it + 16)
                pe.wait_ge(tile_copied, k + 1)
                for h in range(2):
                    mm = pe.transpose(ps_score[:, j % 2, 0:P].bitcast(F16)[:, h * P:(h + 1) * P],
                                      row_sb[:, j % 4, h * C // 2:(h + 1) * C // 2].bitcast(F16), ident16[:, :])
                mm.then_inc(tile_filled, 1)

            def expert_layer1(k, j):
                e = pe.value_load(tab_e[0:1, bass.ds(k, 1)], min_val=0, max_val=E - 1)
                pe.wait_ge(tile_copied, k + 1 + FREE)
                layer1(NB + k, j, e, tileT[:, j % 2, 0:P], tileT[:, j % 2, P:2 * P])

            def expert(k, j, it, more):
                if more > 1:
                    turn(k + 2, j + 2, it + (j + 2) // 4)
                if more > 0:
                    expert_layer1(k + 1, j + 1)
                e = pe.value_load(tab_e[0:1, bass.ds(k, 1)], min_val=0, max_val=E - 1)
                layer2(NB + k, j, e)

            pe.wait_ge(table, 2)
            pe.wait_ge(max_done, 2 * NB)
            turn(0, 0, 0)
            turn(1, 1, 0)
            expert_layer1(0, 0)
            tiles(pe, NT, expert)

        @block.vector
        def _(dve):
            def ln(which, g):
                for s in range(G):
                    dve.bn_stats(ln_raw[:, which, s, :], xs[:, bass.ds(G * g + s, 1), :].rearrange("p a c -> p (a c)"))\
                       .then_inc(ln_stats[which], 1)
                hold(dve, ln_stats[which], G * g + G)
                for s in range(G):
                    dve.bn_aggr(ln_mv[:, which, s, :], ln_raw[:, which, s, :]).then_inc(ln_aggr[which], 1)

            def norm(which, g, to, done):
                dve.wait_ge(ln_inv[which], 2 * g + 2)
                for s in range(G):
                    dve.tensor_scalar(to[:, s, :], xs[:, bass.ds(G * g + s, 1), :].rearrange("p a c -> p (a c)"),
                                      ln_mv[:, which, s, 0:1], ln_rstd[:, which, s:s + 1],
                                      ALU.subtract, ALU.mult).then_inc(done, 1)

            dve.wait_ge(x0_loaded, 16)
            ln(0, 0)
            n = 0

            def made(ins):
                nonlocal n
                n += 1
                ins.then_inc(consts_v, 1)

            made(dve.memset(shift_part[:, :, :, :].bitcast(F32), 0.0))
            norm(0, 0, xn, xn_ready)
            v_all = v_sb[:, :, :, :, :].rearrange("p a s h d -> p (a s h) d")
            made(dve.memset(v_all[:, :, D:D + 1], 1.0))
            made(dve.memset(v_all[:, :, D + 1:32], 0.0))
            dve.wait_ge(small_loaded, 16 * SMALL)
            dve.tensor_scalar(wr_sb[:, :], wr_sb[:, :], WSCALE, None, ALU.mult).then_inc(consts_v, 1)
            n += 1
            dve.wait_ge(consts_v, n)
            made(dve.tensor_copy(wr_part[:, 0, :], wr_sb[:, :]))
            dve.wait_ge(consts_v, n)
            made(dve.tensor_tensor(wr_part[:, 1, :], wr_sb[:, :], wr_part[:, 0, :], ALU.subtract))
            made(dve.tensor_scalar(b2_sb[0:E, :], b2_sb[0:E, :], WSCALE, None, ALU.mult))
            dve.wait_ge(consts, POOL_CONSTS)
            made(dve.tensor_tensor(sel[:, 0, :], sel_raw[:, 0, :], sel_raw[:, 1, :], ALU.add))
            made(dve.tensor_copy(sel[:, 1, :], sel_raw[:, 2, :]))
            made(dve.tensor_tensor(sel[:, 2, :], sel_raw[:, 0, :], sel_raw[:, 2, :], ALU.add))
            made(dve.tensor_copy(sel[:, 3, :], sel_raw[:, 1, :]))
            made(dve.tensor_copy(pick[:, :, :], pick_raw[:, :, :]))
            made(dve.memset(mixw[:, :, :], 0.0))
            assert n == V_CONSTS, n

            def take_max(b, unit, p):
                dve.wait_ge(score_filled, 2 * b + unit + 1)
                dve.tensor_reduce(score_max[:, p, 2 * unit:2 * unit + 2, :],
                                  ps_score[:, :, :].rearrange("p j (m t) -> p j m t", m=HG), AX.X, ALU.max)\
                   .then_inc(max_done, 1)

            def shifts(b, p):
                dve.wait_ge(max_done, 2 * b + 2)
                dve.tensor_scalar(shift[:, p, :, :], score_max[:, p, :, :], CLAMP, floor_max, ALU.min, ALU.max)\
                   .then_inc(shift_steps, 1)
                dve.wait_ge(shift_steps, 3 * b + 1)
                dve.tensor_scalar(shift_part[:, p, :, 0:HG], shift[:, p, :, :], -1.0, None, ALU.mult)\
                   .then_inc(shift_steps, 1)
                dve.wait_ge(shift_steps, 3 * b + 2)
                dve.scalar_tensor_tensor(out=shift_part[:, p, :, HG:2 * HG], in0=shift[:, p, :, :], scalar=-1.0,
                                         in1=shift_part[:, p, :, 0:HG].bitcast(F32),
                                         op0=ALU.mult, op1=ALU.subtract).then_inc(shift_steps, 1)

            def clamp(b, unit):
                dve.wait_ge(exp_done, 2 * b + unit + 1)
                dve.tensor_scalar(probs[:, unit, :, :], probs[:, unit, :, :], 1.0, TINY, ALU.min, ALU.max)\
                   .then_inc(clamp_done, 1)

            def normalise(b, par, s):
                dve.wait_ge(o_turned, b + 1)
                turned = ps_att[:, :].rearrange("p (h r) -> p h r", r=32)
                dve.reciprocal(sums_inv[:, :], turned[:, :, D]).then_inc(sums_ready, 1)
                dve.wait_ge(sums_ready, b + 1)
                dve.tensor_tensor(att[:, par, s, :].rearrange("p (h d) -> p h d", d=D), turned[:, :, 0:D],
                                  sums_inv[:, :].unsqueeze(2).to_broadcast([P, H, D]), ALU.mult)\
                   .then_inc(att_ready, 1)

            def low(name, g, no):
                part, col, s = (q_part, qb_col, q_high) if name == "q" else (k_part, kb_col, k_high)
                dve.wait_ge(s, g + 1)
                dve.scalar_tensor_tensor(out=part[:, 1, :], in0=ps_stage[:, :], scalar=col[:, :],
                                         in1=part[:, 0, :].bitcast(F32), op0=ALU.add, op1=ALU.subtract)\
                   .then_inc(stage_copied, 1)

            def v_copy(no, par):
                dve.wait_ge(stage_filled, no["v"] + 1)
                dve.tensor_tensor(v_sb[:, par, :, :, 0:D], ps_stage[:, :].rearrange("p (s h d) -> p s h d", s=G, d=D),
                                  vb_row[:, :].rearrange("p (h d) -> p h d", d=D).unsqueeze(1)
                                  .to_broadcast([P, G, H, D]), ALU.add).then_inc(stage_copied, 1)

            def residual(name, g, no):
                dve.wait_ge(stage_filled, no[name] + 1)
                if name == "wo":
                    dve.wait_ge(xbo_ready, g + 1)
                xg = xs[:, bass.ds(G * g, G), :]
                dve.tensor_tensor(xg, ps_stage[:, :].rearrange("p (s c) -> p s c", s=G), xg, ALU.add)\
                   .then_inc(stage_copied, 1)

            def token_low(g, par):
                dve.wait_ge(tok_high, g + 1)
                dve.tensor_tensor(pay[:, par, :, C // 2:C].bitcast(F16), tok[:, :, :],
                                  pay[:, par, :, 0:C // 2].bitcast(F16), ALU.subtract).then_inc(tok_low, 1)

            class Route:

                def __init__(self, g, at):
                    self.g, self.at = g, at

                def did(self, ins):
                    ins.then_inc(route, 1)
                    self.at += 1

                def wait(self, at):
                    dve.wait_ge(route, ROUTE * self.g + at)

            def each_mask(v):
                return v.unsqueeze(3).to_broadcast([P, G, TOP, E])

            def choose(g, no):
                r = Route(g, 0)
                dve.wait_ge(stage_filled, no["logits"] + 1)
                dve.scalar_tensor_tensor(
                    out=lg[:, :, 8:8 + RD], in0=ps_stage[:, 0:16 * G].rearrange("p (s n) -> p s n", n=16)[:, :, 0:RD],
                    scalar=1.0 / WSCALE, in1=rb_row[:, :].unsqueeze(1).to_broadcast([P, G, RD]),
                    op0=ALU.mult, op1=ALU.add).then_inc(stage_copied, 1)
                hold(dve, stage_copied, no["logits"] + 1)
                for s in range(G):
                    r.did(dve.max(lg[:, s, 0:8], lg[:, s, 10:10 + E]))
                hold(dve, route, ROUTE * g + G)
                for s in range(G):
                    r.did(dve.max_index(top_at[:, s, :], lg[:, s, 0:8], lg[:, s, 10:10 + E]))
                pairs = lg[:, :, 0:16].rearrange("p s (a r) -> p s a r", a=2)
                r.did(dve.tensor_tensor(dif[:, :, :, 0], pairs[:, :, :, 1], pairs[:, :, :, 0], ALU.subtract))
                r.did(dve.tensor_tensor(dif[:, :, :, 1], pairs[:, :, :, 0], pairs[:, :, :, 1], ALU.subtract))
                assert r.at == ROUTE_DIF
                r.wait(8)
                for_e = expert_no[:, :].unsqueeze(1).unsqueeze(1).to_broadcast([P, G, TOP, E])
                r.did(dve.tensor_tensor(mask[:, :, :, :], each_mask(top_at[:, :, 0:TOP]), for_e, ALU.is_equal))
                r.wait(11)
                r.did(dve.tensor_tensor(chosen[:, :, :], mask[:, :, 0, :], mask[:, :, 1, :], ALU.add))
                assert r.at == ROUTE_CHOSEN

            def weigh(g, par):
                r = Route(g, ROUTE_CHOSEN)
                dve.wait_ge(dif_exped, g + 1)
                r.did(dve.tensor_scalar(dif_sum[:, :, :, :], dif_exp[:, :, :, :], 1.0, None, ALU.add))
                r.wait(13)
                r.did(dve.reciprocal(share[:, :, :, :], dif_sum[:, :, :, :]))
                r.wait(14)
                r.did(dve.scalar_tensor_tensor(out=wsh[:, :, :], in0=share[:, :, 0, :], scalar=1.0 / WSCALE,
                                               in1=share[:, :, 1, 0:1].to_broadcast([P, G, TOP]),
                                               op0=ALU.mult, op1=ALU.mult))
                r.did(dve.tensor_scalar(dense_w[:, bass.ds(G * g, G)], share[:, :, 1, 1], 1.0 / WSCALE, None, ALU.mult))
                r.did(dve.tensor_copy(mixw[:, :, E], share[:, :, 1, 1]))
                r.wait(15)
                r.did(dve.tensor_tensor(wmask[:, :, :, :], mask[:, :, :, :], each_mask(wsh[:, :, :]), ALU.mult))
                r.wait(18)
                r.did(dve.tensor_tensor(pay[:, par, :, C:C + E], wmask[:, :, 0, :], wmask[:, :, 1, :], ALU.add))
                r.did(dve.tensor_tensor(mixw[:, :, 0:E], wmask[:, :, 0, :], wmask[:, :, 1, :], ALU.add))
                assert r.at == ROUTE_MIX
                r.did(dve.tensor_tensor(pay[:, par, :, C + E:ROW].bitcast(I32), mask[:, :, 1, :],
                                        target0[:, :].unsqueeze(2).to_broadcast([P, G, E]), ALU.add))

            def place(g, par, no):
                r = Route(g, 21)
                dve.wait_ge(stage_filled, no["rank"] + 1)
                r.did(dve.tensor_tensor(pos[:, :, :], ps_stage[:, 0:E * G].rearrange("p (s e) -> p s e", s=G),
                                        count[:, :].unsqueeze(1).to_broadcast([P, G, E]), ALU.add))
                r.wait(22)
                r.did(dve.tensor_scalar(target0[:, :], target0[:, :], float(TOP * GT), None, ALU.add))
                dve.tensor_tensor(count[:, :], ps_stage[:, E * G:E * G + E], count[:, :], ALU.add)\
                   .then_inc(stage_copied, 1)
                r.did(dve.tensor_tensor(mpos[:, :, :, :], mask[:, :, :, :],
                                        pos[:, :, :].unsqueeze(2).to_broadcast([P, G, TOP, E]), ALU.mult))
                r.wait(24)
                with nc.allow_low_precision(reason="row numbers are exact in float32"):
                    r.did(dve.tensor_reduce(slot_at[:, par, :, :], mpos[:, :, :, :], AX.X, ALU.add))
                assert r.at == ROUTE

            def prologue(no):
                low("q", 0, no)
                low("k", 0, no)
                v_copy(no, 0)
                dve.wait_ge(x_loaded, 16)
                take_max(0, 0, 0)
                take_max(0, 1, 0)
                shifts(0, 0)

            def body(g, par, half_g, no, pre, post):
                for s in range(G):
                    b = G * g + s
                    more = pre or s < G - 1
                    p1 = (s + 1) % 2
                    clamp(b, 0)
                    if s == 0 and pre:
                        ln(0, g + 1)
                    if s == 1 and pre:
                        low("q", g + 1, no)
                    if more:
                        take_max(b + 1, 0, p1)
                    clamp(b, 1)
                    if s == 1 and pre:
                        low("k", g + 1, no)
                    if more:
                        take_max(b + 1, 1, p1)
                        shifts(b + 1, p1)
                    if s == 0 and post:
                        residual("wo", g - 1, no)
                    if s == 1 and pre:
                        v_copy(no, 1 - par)
                    if s == 1 and post:
                        norm(1, g - 1, tok, tok_ready)
                        token_low(g - 1, 1 - par)
                    if s == 3 and post:
                        weigh(g - 1, 1 - par)
                        place(g - 1, 1 - par, no)
                    normalise(b, par, s)
                    if s == 0 and post:
                        ln(1, g - 1)
                    if s == 0 and pre:
                        norm(0, g + 1, xn, xn_ready)
                    if s == 2 and post:
                        choose(g - 1, no)
                    if s == 3 and post:
                        residual("bias", g - 1, no)

            def tail(g, par, half_g, no):
                residual("wo", g, no)
                dve.wait_ge(stage_copied, no["wo"] + 1)
                ln(1, g)
                norm(1, g, tok, tok_ready)
                token_low(g, par)
                choose(g, no)
                weigh(g, par)
                place(g, par, no)
                residual("bias", g, no)

            bodies(dve, prologue, body, tail)

            dve.wait_ge(ffn_loaded, 16 * 4)
            dve.tensor_scalar(b1_sb[:, :], b1_sb[:, :], WSCALE, None, ALU.mult).then_inc(consts_v, 1)
            dve.wait_ge(consts_v, V_CONSTS + 1)
            dve.wait_ge(stage_copied, 2 * NPRE + NFULL * (NG - 2) + 2 * NPOST)
            dve.tensor_copy(tab_pad[:, :], count[0:1, :]).then_inc(table, 1)
            steps = 0

            def did(ins):
                nonlocal steps
                steps += 1
                ins.then_inc(tab_steps, 1)
                dve.wait_ge(tab_steps, steps)

            NE = NT + 4
            did(dve.scalar_tensor_tensor(out=n_tok[:, :], in0=expert_no[0:1, :], scalar=-float(CAP),
                                         in1=count[0:1, :], op0=ALU.mult, op1=ALU.add))
            did(dve.tensor_scalar(n_i[:, :], n_tok[:, :], float(P - 1), None, ALU.add))
            did(dve.tensor_scalar(n_tiles_i[:, :], n_i[:, :], P.bit_length() - 1, None, ALU.logical_shift_right))
            did(dve.tensor_copy(n_tiles[:, :], n_tiles_i[:, :]))
            did(dve.tensor_tensor(cum_w[:, :, :], cum_mask[:, :, :],
                                  n_tiles[:, :].unsqueeze(1).to_broadcast([1, E, E]), ALU.mult))
            did(dve.tensor_reduce(cum[:, :], cum_w[:, :, :], AX.X, ALU.add))
            did(dve.tensor_tensor(past[:, :, :], tile_no[:, :].unsqueeze(2).to_broadcast([1, NE, E]),
                                  cum[:, :].unsqueeze(1).to_broadcast([1, NE, E]), ALU.is_ge))
            did(dve.tensor_reduce(tile_e[:, :], past[:, :, :], AX.X, ALU.add))
            did(dve.tensor_tensor(past_w[:, :, :], past[:, :, :],
                                  n_tiles[:, :].unsqueeze(1).to_broadcast([1, NE, E]), ALU.mult))
            did(dve.tensor_reduce(tile_s[:, :], past_w[:, :, :], AX.X, ALU.add))
            did(dve.tensor_tensor(tile_s[:, :], tile_no[:, :], tile_s[:, :], ALU.subtract))
            did(dve.tensor_scalar(tile_s[:, :], tile_s[:, :], float(P), None, ALU.mult))
            did(dve.scalar_tensor_tensor(out=tile_r[:, :], in0=tile_e[:, :], scalar=float(CAP), in1=tile_s[:, :],
                                         op0=ALU.mult, op1=ALU.add))
            did(dve.tensor_scalar(tab_row[:, :], tile_r[:, :], float(E * CAP), None, ALU.min))
            did(dve.tensor_scalar(tab_e[:, :], tile_e[:, :], float(E - 1), None, ALU.min))
            dve.memset(shift[:, 0, 0, 0:1], 0.0).then_inc(table, 1)

            def relu(k, j, bias):
                dve.wait_ge(hid_filled, k + 1)
                dve.wait_ge(y_filled, k + 1)
                for c in range(FC // 2, FC):
                    dve.tensor_scalar(hid[:, j % 2, c, :], hid_bank(j, c), bias(c), 0.0,
                                      ALU.add, ALU.max).then_inc(relu_v, 1)

            def dense_bias(c):
                return b1_sb[:, E * FC + c:E * FC + c + 1]

            def dense(k, j, it, more):
                if more > 0:
                    relu(k + 1, j + 1, dense_bias)
                dve.wait_ge(y_filled, k + 1 + FREE)
                xb = xs[:, bass.ds(k, 1), :].rearrange("p a c -> p (a c)")
                dve.scalar_tensor_tensor(out=xb, in0=y_bank[j % 2][:, 0:C], scalar=dense_w[:, bass.ds(k, 1)],
                                         in1=xb, op0=ALU.mult, op1=ALU.add).then_inc(y_ready, 1)

            dve.sem_inc(relu_v, FREE * FC // 2)
            dve.sem_inc(y_ready, FREE)
            relu(0, 0, dense_bias)
            tiles(dve, NB, dense)

            def expert(k, j, it, more):
                if more > 0:
                    e1 = dve.value_load(tab_e[0:1, bass.ds(k + 1, 1)], min_val=0, max_val=E - 1)
                    relu(NB + k + 1, j + 1, lambda c: b1_sb[:, bass.ds(e1 * FC + c, 1)])
                e = dve.value_load(tab_e[0:1, bass.ds(k, 1)], min_val=0, max_val=E - 1)
                dve.wait_ge(y_sent[j], 16 * it + 16)
                dve.tensor_copy(y_at[:, j:j + 1], row_sb[:, j, bass.ds(e + (C + E), 1)].bitcast(I32)).then_inc(y_target, 1)
                dve.wait_ge(y_filled, NB + k + 1 + FREE)
                dve.tensor_scalar(y_sb[:, j, :], y_bank[j % 2][:, 0:C], row_sb[:, j, bass.ds(e + C, 1)], None,
                                  ALU.mult).then_inc(y_ready, 1)

            e0 = dve.value_load(tab_e[0:1, 0:1], min_val=0, max_val=E - 1)
            relu(NB, 0, lambda c: b1_sb[:, bass.ds(e0 * FC + c, 1)])
            tiles(dve, NT, expert)

            for g in range(NG):
                dve.wait_ge(back_loaded[g % 2], 16 * (g // 2 + 1))
                xg, back = xs[:, G * g:G * g + G, :], y_back[:, g % 2, :, :]
                dve.tensor_tensor(xg, xg, back[:, :, 0:C], ALU.add).then_inc(sum1, 1)
                dve.wait_ge(sum1, g + 1)
                dve.tensor_tensor(xg, xg, back[:, :, C:2 * C], ALU.add).then_inc(sum2, 1)


_INS = ['x', 'ctx_768', 'L0_xattn_Wq', 'L0_xattn_bq', 'L0_xattn_Wk', 'L0_xattn_bk', 'L0_xattn_Wv', 'L0_xattn_bv',
        'L0_xattn_Wo', 'L0_xattn_bo', 'L0_ffn_Wr', 'L0_ffn_br', 'L0_ffn_Wg', 'L0_ffn_bg', 'L0_ffn_W1', 'L0_ffn_b1',
        'L0_ffn_W2', 'L0_ffn_b2', 'L0_ffn_D1', 'L0_ffn_d1b', 'L0_ffn_D2', 'L0_ffn_d2b']
_OUTS = [((32, 128, 128), 'float32')]


def kernel(**inputs):
    import numpy as _np
    import concourse.bacc as _bacc
    from concourse import mybir as _mybir
    from concourse.bass_utils import run_bass_kernel_spmd as _run

    nc = _bacc.Bacc("TRN2", target_bir_lowering=False, num_devices=1)
    arrays, args = {}, []
    for name in _INS:
        a = _np.ascontiguousarray(inputs[name])
        arrays[f"in_{name}_dram"] = a
        args.append(nc.dram_tensor(f"in_{name}_dram", a.shape, _mybir.dt.from_np(a.dtype), kind="ExternalInput").ap())
    for i, (shape, dtype) in enumerate(_OUTS):
        dt = _mybir.dt.from_np(_np.dtype(dtype))
        args.append(nc.dram_tensor(f"out_{i}_dram", shape, dt, kind="ExternalOutput").ap())
    cross_attention_moe(nc, *args)
    r = _run(nc, [arrays], core_ids=[0])
    got = tuple(r.results[0][f"out_{i}_dram"] for i in range(len(_OUTS)))
    return got[0]
```

```python
from contextlib import ExitStack

import concourse.bass as bass
from concourse import mybir

ALU = mybir.AluOpType
ACT = mybir.ActivationFunctionType
AX = mybir.AxisListType
F32 = mybir.dt.float32
F32R = mybir.dt.float32r
F16 = mybir.dt.float16
I32 = mybir.dt.int32
U32 = mybir.dt.uint32

P = 128
CLAMP = 10000.0
EPS = 1e-5
TINY_EXPONENT = 87.0
TINY = 1.6458115e-38
WSCALE = 16.0


def cross_attention_moe(nc, x, ctx_in, wq, bq, wk, bk, wv, bv, wo, bo, wr, br, wg, bg,
                        w1, b1, w2, b2, d1, d1b, d2, d2b, out):
    NB, _, C = x.shape
    CK = ctx_in.shape[2]
    H = 16
    D = C // H
    E = wg.shape[1]
    FF = w1.shape[2]
    FC = FF // P
    TOP = 2
    T = NB * P
    G = 4
    NG = NB // G
    GT = G * P
    HG = H // 4
    RD = E + 2
    ROW = C + 2 * E
    CAP = T + P
    NT = TOP * T // P + E
    assert NT % 4 == 0 and NG == 8 and C == P and H * D == C
    q_scale = float(D) ** -0.5
    floor_max = -CLAMP + TINY_EXPONENT

    rows = nc.dram_tensor("routed_rows", (E * CAP + P, ROW), F32, kind="Internal").ap()
    expert_out = nc.dram_tensor("expert_out", (TOP * T, C), F32, kind="Internal").ap()
    x_v = x.rearrange("b s c -> s b c")
    out_v = out.rearrange("b s c -> s b c")
    ctx_v = ctx_in.rearrange("b s c -> s b c")
    w1_v = w1.rearrange("e d f -> d e f")
    w2_v = w2.rearrange("e (c p) d -> p e c d", p=P)
    d2_v = d2.rearrange("(c p) d -> p c d", p=P)
    b1_v = b1.rearrange("e (c p) -> p e c", p=P)
    d1b_v = d1b.rearrange("(c p) -> p c", p=P)

    with ExitStack() as stack:
        def sb(name, shape, dt=F32):
            return stack.enter_context(nc.sbuf_tensor(name, shape, dt))

        def sem(name):
            return stack.enter_context(nc.semaphore(name))

        wq_sb = sb("wq_sb", [P, C])
        wk_sb = sb("wk_sb", [CK, C])
        wv_sb = sb("wv_sb", [CK, C])
        wo_sb = sb("wo_sb", [P, C])
        qb_col = sb("qb_col", [P, 1])
        kb_col = sb("kb_col", [P, 1])
        vb_row = sb("vb_row", [P, C])
        ob_row = sb("ob_row", [P, C])
        wr_sb = sb("wr_sb", [P, RD])
        wr_part = sb("wr_part", [P, 2, RD], F16)
        rb_row = sb("rb_row", [P, RD])
        w1_raw = sb("w1_raw", [P, 2, FF])
        w1_part = sb("w1_part", [P, 2, (E + 1) * FF], F16)
        w2_sb = sb("w2_sb", [P, (E + 1) * FC * C])
        b1_sb = sb("b1_sb", [P, (E + 1) * FC])
        b2_sb = sb("b2_sb", [E + 1, C])
        ident = sb("ident", [P, P])
        ident16 = sb("ident16", [P, P], F16)
        sel_raw = sb("sel_raw", [P, 3, 4 * P])
        sel = sb("sel", [P, 4, 4 * P], F32R)
        pick_raw = sb("pick_raw", [P, HG, P])
        pick = sb("pick", [P, HG, P], F32R)
        before = sb("before", [P, P], F16)
        ones16 = sb("ones16", [P, P], F16)
        expert_no = sb("expert_no", [P, E])
        half = sb("half", [P, G])
        target0 = sb("target0", [P, G])
        pad_rows = sb("pad_rows", [P, ROW])
        xs = sb("xs", [P, NB, C])
        tokT = sb("tokT", [P, 2, T], F16)
        dense_w = sb("dense_w", [P, NB])
        ctx_sb = sb("ctx_sb", [P, 2, G, CK])
        ln_raw = sb("ln_raw", [P, 2, G, 6])
        ln_mv = sb("ln_mv", [P, 2, G, 2])
        ln_eps = sb("ln_eps", [P, 2, G])
        ln_rstd = sb("ln_rstd", [P, 2, G])
        xn = sb("xn", [P, G, C])
        xnT = sb("xnT", [P, GT])
        ctxT = sb("ctxT", [CK, GT])
        q_part = sb("q_part", [P, 2, 2, GT], F32R)
        k_part = sb("k_part", [P, 2, GT], F32R)
        k_rows = sb("k_rows", [P, 2, HG, GT], F32R)
        v_sb = sb("v_sb", [P, 2, G, H, 32])
        score_max = sb("score_max", [P, 2, HG, 4])
        shift = sb("shift", [P, 2, HG, 4])
        shift_part = sb("shift_part", [P, 2, 4, 32], F32R)
        q_diag = sb("q_diag", [P, 2, HG, 4, P], F32R)
        shift_diag = sb("shift_diag", [P, 2, 4, P], F32R)
        probs = sb("probs", [P, HG, 4, P])
        oT = sb("oT", [P, HG * P])
        sums_inv = sb("sums_inv", [P, H])
        att = sb("att", [P, 2, G, C])
        attT = sb("attT", [P, GT])
        tok = sb("tok", [P, G, C])
        pay = sb("pay", [P, 2, G, ROW])
        lg = sb("lg", [P, G, 24])
        top_at = sb("top_at", [P, G, 8], U32)
        mask = sb("mask", [P, G, TOP, E])
        chosen = sb("chosen", [P, G, E], F16)
        count = sb("count", [P, E])
        pos = sb("pos", [P, G, E])
        mpos = sb("mpos", [P, G, TOP, E])
        slot_at = sb("slot_at", [P, 2, G, TOP], I32)
        dif = sb("dif", [P, G, 2, 2])
        dif_exp = sb("dif_exp", [P, G, 2, 2])
        dif_sum = sb("dif_sum", [P, G, 2, 2])
        share = sb("share", [P, G, 2, 2])
        wsh = sb("wsh", [P, G, TOP])
        wmask = sb("wmask", [P, G, TOP, E])
        mixw = sb("mixw", [P, G, E + 1])
        mixT = sb("mixT", [E + 1, GT])
        cum_mask = sb("cum_mask", [1, E, E])
        tile_no = sb("tile_no", [1, NT + 4])
        n_tok = sb("n_tok", [1, E])
        n_i = sb("n_i", [1, E], I32)
        n_tiles_i = sb("n_tiles_i", [1, E], I32)
        n_tiles = sb("n_tiles", [1, E])
        cum_w = sb("cum_w", [1, E, E])
        cum = sb("cum", [1, E])
        past = sb("past", [1, NT + 4, E])
        past_w = sb("past_w", [1, NT + 4, E])
        tile_e = sb("tile_e", [1, NT + 4])
        tile_s = sb("tile_s", [1, NT + 4])
        tile_r = sb("tile_r", [1, NT + 4])
        tab_e = sb("tab_e", [1, NT + 4], I32)
        tab_row = sb("tab_row", [1, NT + 4], I32)
        tab_pad = sb("tab_pad", [1, E], I32)
        row_sb = sb("row_sb", [P, 4, ROW])
        tileT = sb("tileT", [P, 2, 2 * P], F16)
        late = v_sb[:, 1, :, :, :].rearrange("p s h d -> p (s h d)")
        hid = late[:, 0:2 * FC * P].rearrange("p (a c t) -> p a c t", a=2, c=FC)
        y_sb = late[:, 2 * FC * P:2 * FC * P + 4 * C].rearrange("p (a c) -> p a c", a=4)
        y_at = sb("y_at", [P, 4], I32)
        y_back = v_sb[:, 0, :, :, :].rearrange("p s h d -> p (s h d)").rearrange("p (a s c) -> p a s c", a=2, s=G)

        bank = stack.enter_context(nc.psum_tensor("bank", [P, 8, 512], F32))
        score_bank, stage_bank, att_bank = bank[:, 0:2, :], (bank[:, 5, :], bank[:, 6, :]), bank[:, 7, :]
        st_bank = (bank[:, 2, :], bank[:, 3, :], bank[:, 4, :], bank[:, 2, :])
        y_bank, turn_bank = stage_bank, (bank[:, 0, :], bank[:, 1, :])

        def hid_bank(j, c):
            b, at = (2, 4)[c // (FC // 2)] + j % 2 * (1, 3)[c // (FC // 2)], c % (FC // 2)
            return bank[:, b, at * P:(at + 1) * P]

        small_loaded = sem("small_loaded")
        x0_loaded = sem("x0_loaded")
        x_loaded = sem("x_loaded")
        ctx_loaded = [sem(f"ctx_loaded{i}") for i in range(2)]
        w1_loaded = [sem(f"w1_loaded{i}") for i in range(2)]
        ffn_loaded = sem("ffn_loaded")
        consts = sem("consts")
        consts_s = sem("consts_s")
        consts_v = sem("consts_v")
        ln_stats = [sem("ln1_stats"), sem("ln2_stats")]
        ln_aggr = [sem("ln1_aggr"), sem("ln2_aggr")]
        ln_inv = [sem("ln1_inv"), sem("ln2_inv")]
        xn_ready = sem("xn_ready")
        xbo_ready = sem("xbo_ready")
        stage_filled = sem("stage_filled")
        stage_copied = [sem(f"stage{i}_copied") for i in range(2)]
        diag_copied = sem("diag_copied")
        q_high = sem("q_high")
        k_high = sem("k_high")
        score_filled = sem("score_filled")
        max_done = sem("max_done")
        shift_steps = sem("shift_steps")
        st_filled = sem("st_filled")
        exp_done = sem("exp_done")
        clamp_done = sem("clamp_done")
        pv_done = sem("pv_done")
        o_copied = sem("o_copied")
        o_turned = sem("o_turned")
        sums_ready = sem("sums_ready")
        att_ready = sem("att_ready")
        tok_ready = sem("tok_ready")
        tok_high = sem("tok_high")
        tok_low = sem("tok_low")
        route = sem("route")
        dif_exped = sem("dif_exped")
        scattered = [sem(f"scattered{i}") for i in range(2)]
        w1_split = sem("w1_split")
        tab_steps = sem("tab_steps")
        table = sem("table")
        pads_written = sem("pads_written")
        hid_filled = sem("hid_filled")
        relu_s = sem("relu_s")
        relu_v = sem("relu_v")
        y_filled = sem("y_filled")
        y_target = sem("y_target")
        y_ready = sem("y_ready")
        tile_filled = sem("tile_filled")
        tile_copied = sem("tile_copied")
        row_loaded = [sem(f"row_loaded{i}") for i in range(4)]
        y_sent = [sem(f"y_sent{i}") for i in range(4)]
        back_loaded = [sem(f"back_loaded{i}") for i in range(2)]
        sum1 = sem("sum1")
        sum2 = sem("sum2")
        stored = sem("stored")

        PRE = ["ctxT", "xT", "q", "k", "v", "kr0", "kr1", "kr2", "kr3", "rows2", "rows3", "turn3"]
        POST = ["attT", "wo", "tokT", "logits", "rank", "mixT", "bias"]
        GAPS = [
            {"a": ["ctxT"], "b": ["rows0"], "c": ["attT"], "d": ["wo"], "e": ["turn0", "k"]},
            {"a": ["kr0"], "b": ["rows1", "xT"], "c": ["q"], "d": ["kr1"], "e": ["turn1", "v"]},
            {"a": ["kr2"], "b": ["rows2"], "c": ["kr3"], "d": ["tokT"], "e": ["turn2"], "f": ["logits"]},
            {"b": ["rows3"], "c": ["rank"], "e": ["turn3", "mixT"], "f": ["bias"]},
        ]
        NEEDS = {"q": "xT", "k": "ctxT", "v": "ctxT", "kr0": "k", "kr1": "k", "kr2": "k", "kr3": "k", "rows2": "q",
                 "wo": "attT", "logits": "tokT", "bias": "mixT"}
        FULL = [name for slot in GAPS for gap in sorted(slot) for name in slot[gap]]
        FIRST = [name for name in FULL if name not in POST]
        LAST = [name for name in FULL if name in POST or name in ("rows0", "rows1", "turn0", "turn1", "turn2")]
        AT_FIRST = len(PRE)
        AT_LOOP = AT_FIRST + len(FIRST)
        AT_LAST = AT_LOOP + len(FULL) * (NG - 2)
        AT_TAIL = AT_LAST + len(LAST)
        STAGED = AT_TAIL + len(POST)
        assert len(FULL) % 2 == 0
        SMALL = 14
        POOL_CONSTS, S_CONSTS, V_CONSTS = 27, 3, 15
        IDENT_AT = 8
        ROUTE, ROUTE_DIF, ROUTE_CHOSEN, ROUTE_PLACED = 25, 10, 12, 17
        SENT = 16 * TOP * G
        FREE = 2

        class Product:

            def __init__(self, base, loops):
                self.bank = base % 2
                self.n = len(FULL) * loops + base
                self.at = len(FULL) // 2 * loops + base // 2

        def products(base, names, loops=0):
            return {name: Product(base + i, loops) for i, name in enumerate(names)}

        def bodies(eng, prologue, body, tail):
            prologue(products(0, PRE))
            body(0, 0, -1, products(AT_FIRST, FIRST), True, False)
            with eng.Fori(0, (NG - 2) // 2) as i:
                for u in range(2):
                    body(2 * i + 1 + u, (1 + u) % 2, i, products(AT_LOOP + len(FULL) * u, FULL, 2 * i), True, True)
            body(NG - 1, 1, (NG - 2) // 2, products(AT_LAST, LAST), False, True)
            tail(NG - 1, 1, (NG - 1) // 2, products(AT_TAIL, POST))

        def in_gap(s, which, no):
            return [name for name in GAPS[s].get(which, []) if name in no]

        def hold(eng, s, value):
            eng.wait_ge(s, value)
            eng.nop(nofuse=True)

        block = stack.enter_context(nc.Block())

        @block.sync
        def _(sp):
            sp.dma_start(xs[:, 0:G, :], x_v[:, 0:G, :]).then_inc(x0_loaded, 16)
            sp.dma_start(ctx_sb[:, 0, :, :], ctx_v[:, 0:G, :]).then_inc(ctx_loaded[0], 16)

            def row(v, n=P):
                return v.rearrange("(a n) -> a n", a=1).to_broadcast([n, v.shape[0]])

            small = [(wq_sb[:, :], wq), (wk_sb[:, :], wk), (wv_sb[:, :], wv), (wo_sb[:, :], wo),
                     (qb_col[:, :], bq.rearrange("(p a) -> p a", a=1)),
                     (kb_col[:, :], bk.rearrange("(p a) -> p a", a=1)),
                     (vb_row[:, :], row(bv)), (ob_row[:, :], row(bo)), (wr_sb[:, 0:2], wr), (wr_sb[:, 2:RD], wg),
                     (rb_row[:, 0:2], row(br)), (rb_row[:, 2:RD], row(bg)),
                     (b2_sb[0:E, :], b2), (b2_sb[E:E + 1, :], row(d2b, 1))]
            assert len(small) == SMALL
            for dst, src in small:
                sp.dma_start(dst, src).then_inc(small_loaded, 16)
            sp.dma_start(ctx_sb[:, 1, :, :], ctx_v[:, G:2 * G, :]).then_inc(ctx_loaded[1], 16)
            sp.dma_start(xs[:, G:NB, :], x_v[:, G:NB, :]).then_inc(x_loaded, 16)
            sp.dma_start(w2_sb[:, 0:E * FC * C].rearrange("p (e c d) -> p e c d", e=E, c=FC), w2_v)\
              .then_inc(ffn_loaded, 16)
            sp.dma_start(w2_sb[:, E * FC * C:].rearrange("p (c d) -> p c d", c=FC), d2_v).then_inc(ffn_loaded, 16)
            with nc.allow_non_contiguous_dma(reason="hidden biases become columns"):
                sp.dma_start(b1_sb[:, 0:E * FC].rearrange("p (e c) -> p e c", e=E), b1_v).then_inc(ffn_loaded, 16)
                sp.dma_start(b1_sb[:, E * FC:], d1b_v).then_inc(ffn_loaded, 16)
            for e in range(E + 1):
                if e >= 2:
                    sp.wait_ge(w1_split, 3 * (e - 1))
                sp.dma_start(w1_raw[:, e % 2, :], w1_v[:, e, :] if e < E else d1).then_inc(w1_loaded[e % 2], 16)

            def load_ctx(g, par, former):
                sp.wait_ge(stage_copied[former.bank], former.at + 1)
                sp.dma_start(ctx_sb[:, par, :, :], ctx_v[:, bass.ds(G * g, G), :]).then_inc(ctx_loaded[par], 16)

            load_ctx(2, 0, products(0, PRE)["ctxT"])
            load_ctx(3, 1, products(AT_FIRST, FIRST)["ctxT"])
            with sp.Fori(0, (NG - 4) // 2) as i:
                for u in range(2):
                    load_ctx(2 * i + 4 + u, u, products(AT_LOOP + len(FULL) * u, FULL, 2 * i)["ctxT"])

            sp.wait_ge(table, 1)
            for e in range(E):
                r = sp.value_load(tab_pad[0:1, e:e + 1], min_val=0, max_val=E * CAP - P)
                sp.dma_start(rows[bass.ds(r, P), :], pad_rows[:, :]).then_inc(pads_written, 16)
            sp.wait_ge(pads_written, 16 * E)
            for j in range(4):
                sp.wait_ge(y_sent[j], 16)
            for par in range(2):
                sp.wait_ge(scattered[par], SENT * NG // 2 + 16)
            sp.wait_ge(table, 2)

            def load_rows(k, j, used):
                r = sp.value_load(tab_row[0:1, bass.ds(k, 1)], min_val=0, max_val=E * CAP)
                if used is not None:
                    sp.wait_ge(y_ready, used)
                sp.dma_start(row_sb[:, j, :], rows[bass.ds(r, P), :]).then_inc(row_loaded[j], 16)

            for j in range(4):
                load_rows(j, j, None)
            with sp.Fori(1, NT // 4) as it:
                for j in range(4):
                    load_rows(4 * it + j, j, 4 * it + (j - 3 + NB + FREE))

            for j in range(4):
                sp.wait_ge(y_sent[j], 16 * NT // 4 + 16)
            back_v = expert_out.rearrange("(b p t) c -> p b (t c)", p=P, t=TOP)

            def store(g):
                sp.wait_ge(sum2, g + 1)
                sp.dma_start(out_v[:, G * g:G * g + G, :], xs[:, G * g:G * g + G, :]).then_inc(stored, 16)

            for g in range(NG):
                if g >= 2:
                    sp.wait_ge(sum2, g - 1)
                sp.dma_start(y_back[:, g % 2, :, :], back_v[:, G * g:G * g + G, :]).then_inc(back_loaded[g % 2], 16)
                if g >= 1:
                    store(g - 1)
            store(NG - 1)
            sp.wait_ge(stored, 16 * NG)

        @block.gpsimd
        def _(pool):
            n = 0

            def made(ins):
                nonlocal n
                n += 1
                ins.then_inc(consts, 1)

            made(pool.memset(ident[:, :], 0.0))
            made(pool.memset(half[:, :], -0.5))
            made(pool.memset(sel_raw[:, :, :], 0.0))
            made(pool.memset(pick_raw[:, :, :], 0.0))
            made(pool.memset(pad_rows[:, :], 0.0))
            made(pool.memset(cum_mask[:, :, :], 1.0))
            made(pool.memset(before[:, :], 1.0))
            pool.wait_ge(consts, n)
            made(pool.affine_select(out=ident[:, :], in_=ident[:, :], compare_op=ALU.not_equal, fill=1.0,
                                    base=0, pattern=[[-1, P]], channel_multiplier=1))
            assert n == IDENT_AT

            def rstd(which, g):
                hold(pool, ln_aggr[which], G * g + G)
                pool.tensor_scalar(ln_eps[:, which, :], ln_mv[:, which, :, 1], EPS, None, ALU.add)\
                    .then_inc(ln_inv[which], 1)
                pool.wait_ge(ln_inv[which], 2 * g + 1)
                pool.tensor_tensor(ln_rstd[:, which, :], ln_eps[:, which, :], half[:, :], ALU.pow)\
                    .then_inc(ln_inv[which], 1)

            rstd(0, 0)
            for r in range(3):
                v = sel_raw[:, r, :].rearrange("c (m j r d) -> c m j r d", m=HG, j=4, r=4)[:, :, :, r, :]
                made(pool.affine_select(out=v, in_=v, compare_op=ALU.not_equal, fill=1.0, base=0,
                                        pattern=[[-32, HG], [-8, 4], [-1, D]], channel_multiplier=1))
            for r in range(0, P, 32):
                for low in range(2):
                    pool.wait_ge(consts, n)
                    made(pool.affine_select(out=pick_raw[:, :, :], in_=pick_raw[:, :, :], compare_op=ALU.not_equal,
                                            fill=1.0, base=-(r + HG * low), pattern=[[-1, HG], [0, P]],
                                            channel_multiplier=1))
            made(pool.iota(expert_no[:, :], [[1, E]], base=0, channel_multiplier=0,
                           allow_small_or_imprecise_dtypes=True))
            made(pool.iota(target0[:, :], [[TOP * P, G]], base=0, channel_multiplier=TOP,
                           allow_small_or_imprecise_dtypes=True))
            made(pool.iota(count[:, :], [[CAP, E]], base=0, channel_multiplier=0,
                           allow_small_or_imprecise_dtypes=True))
            made(pool.iota(tile_no[:, :], [[1, NT + 4]], base=0, channel_multiplier=0,
                           allow_small_or_imprecise_dtypes=True))
            made(pool.iota(pad_rows[:, C + E:ROW].bitcast(I32), [[0, E]], base=TOP * T, channel_multiplier=1))
            made(pool.affine_select(out=before[:, :], in_=before[:, :], compare_op=ALU.is_gt, fill=0.0,
                                    base=0, pattern=[[1, P]], channel_multiplier=-1))
            made(pool.affine_select(out=cum_mask[:, :, :], in_=cum_mask[:, :, :], compare_op=ALU.is_ge, fill=0.0,
                                    base=0, pattern=[[1, E], [-1, E]], channel_multiplier=0))
            made(pool.memset(ones16[:, :], 1.0))
            assert n == POOL_CONSTS, n

            def add_bo(g):
                pool.wait_ge(xn_ready, G * g + G)
                pool.tensor_tensor(xs[:, bass.ds(G * g, G), :], xs[:, bass.ds(G * g, G), :],
                                   ob_row[:, :].unsqueeze(1).to_broadcast([P, G, C]), ALU.add).then_inc(xbo_ready, 1)

            def scatter(g, par):
                hold(pool, route, ROUTE * g + ROUTE)
                for s in range(G):
                    for t in range(TOP):
                        pool.indirect_dma_start(
                            rows, bass.IndirectOffsetOnAxis(ap=slot_at[:, par, s, t:t + 1], axis=0),
                            pay[:, par, s, :], None, bounds_check=E * CAP + P - 1, oob_is_err=False)\
                            .then_inc(scattered[par], 16)

            def split_w1():
                for e in range(E + 1):
                    pool.wait_ge(w1_loaded[e % 2], 16 * (e // 2 + 1))
                    raw, high = w1_raw[:, e % 2, :], w1_part[:, 0, e * FF:(e + 1) * FF]
                    pool.tensor_scalar(raw, raw, WSCALE, None, ALU.mult).then_inc(w1_split, 1)
                    pool.wait_ge(w1_split, 3 * e + 1)
                    pool.tensor_copy(high, raw).then_inc(w1_split, 1)
                    pool.wait_ge(w1_split, 3 * e + 2)
                    pool.tensor_tensor(w1_part[:, 1, e * FF:(e + 1) * FF], raw, high, ALU.subtract)\
                        .then_inc(w1_split, 1)

            pool.wait_ge(consts, POOL_CONSTS)
            piece = P // 8
            for i, s in enumerate(scattered + y_sent):
                at = slice(piece * i, piece * (i + 1) if i < 5 else P)
                pool.dma_start(rows[E * CAP + at.start:E * CAP + at.stop, :], pad_rows[at, :]).then_inc(s, 16)

            def prologue(no):
                pool.wait_ge(small_loaded, 16 * SMALL)
                add_bo(0)

            def body(g, par, half_g, no, pre, post):
                if pre:
                    rstd(0, g + 1)
                if post:
                    rstd(1, g - 1)
                if pre:
                    add_bo(g + 1)
                if post:
                    scatter(g - 1, 1 - par)
                else:
                    split_w1()

            def tail(g, par, half_g, no):
                rstd(1, g)
                scatter(g, par)

            bodies(pool, prologue, body, tail)

            with pool.Fori(0, NT // 4) as it:
                for j in range(4):
                    hold(pool, y_ready, 4 * it + (j + 1 + NB + FREE))
                    pool.indirect_dma_start(
                        expert_out, bass.IndirectOffsetOnAxis(ap=y_at[:, j:j + 1], axis=0), y_sb[:, j, :], None,
                        bounds_check=TOP * T - 1, oob_is_err=False).then_inc(y_sent[j], 16)

        def tiles(eng, n, step):
            with eng.Fori(0, n // 4 - 1) as it:
                for j in range(4):
                    step(4 * it + j, j, it, 2)
            for j in range(4):
                step(n - 4 + j, j, n // 4 - 1, 3 - j)

        @block.scalar
        def _(act):
            act.wait_ge(consts, IDENT_AT)
            act.copy(ident16[:, :], ident[:, :]).then_inc(consts_s, 1)
            act.wait_ge(small_loaded, 16 * SMALL)
            act.mul(wq_sb[:, :], wq_sb[:, :], q_scale).then_inc(consts_s, 1)
            act.mul(qb_col[:, :], qb_col[:, :], q_scale).then_inc(consts_s, 1)
            act.wait_ge(consts_s, S_CONSTS)

            def stage(name, g, no, par):
                if name in ("v", "wo", "logits", "rank", "bias"):
                    return
                act.wait_ge(stage_filled, no[name].n + 1)
                ps, copied = stage_bank[no[name].bank], stage_copied[no[name].bank]
                if name in ("q", "k"):
                    high, col, s = (q_part[:, par, 0, :], qb_col, q_high) if name == "q" \
                        else (k_part[:, 0, :], kb_col, k_high)
                    act.activation(high, ps, ACT.Identity, bias=col[:, :]).then_inc(s, 1)
                elif name[:4] in ("rows", "turn"):
                    p = (int(name[4]) + (name[:4] == "turn")) % 2
                    for j in range(4):
                        rows_j = slice(32 * j, 32 * j + 32)
                        if name[:4] == "rows":
                            dst, src = q_diag[rows_j, p, :, j, :], ps[rows_j, :].rearrange("p (m t) -> p m t", m=HG)
                        else:
                            dst, src = shift_diag[rows_j, p, j, :], ps[rows_j, 0:P]
                        act.copy(dst, src).then_inc(copied if j == 3 else diag_copied, 1)
                else:
                    if name == "tokT":
                        dst = tokT[:, :, bass.ds(g * GT, GT)].rearrange("p h (s t) -> p s h t", s=G)
                        src = ps.bitcast(F16).rearrange("p (s h t) -> p s h t", s=G, h=2)
                    else:
                        dst, src = {
                            "ctxT": lambda: (ctxT[:, :], ps[0:CK, :]),
                            "xT": lambda: (xnT[:, :], ps),
                            "kr": lambda: (k_rows[:, par, int(name[2]), :], ps),
                            "attT": lambda: (attT[:, :], ps),
                            "mixT": lambda: (mixT[:, :], ps[0:E + 1, :]),
                        }[name.rstrip("0123")]()
                    act.copy(dst, src).then_inc(copied, 1)

            def token_high(g, par, sent):
                act.wait_ge(scattered[par], sent + 16)
                act.wait_ge(tok_ready, G * g + G)
                act.copy(pay[:, par, :, 0:C // 2].bitcast(F16), tok[:, :, :]).then_inc(tok_high, 1)

            def router_exp(g):
                act.wait_ge(route, ROUTE * g + ROUTE_DIF)
                act.activation(dif_exp[:, :, :, :], dif[:, :, :, :], ACT.Exp).then_inc(dif_exped, 1)

            def prologue(no):
                act.wait_ge(consts_v, V_CONSTS)
                for name in PRE:
                    stage(name, 0, no, 0)

            def body(g, par, half_g, no, pre, post):
                for s in range(G):
                    b = G * g + s

                    def gap(which):
                        for name in in_gap(s, which, no):
                            stage(name, g + 1 if name in PRE else g - 1, no, 1 - par)

                    def exp(m):
                        act.wait_ge(st_filled, HG * b + m + 1)
                        if post or s > 0:
                            act.wait_ge(pv_done, 2 * b + m // 2 - 1)
                        act.activation(probs[:, m, :, :].rearrange("p j t -> p (j t)"), st_bank[m], ACT.Exp)\
                            .then_inc(exp_done, 1)

                    exp(0)
                    exp(1)
                    gap("a")
                    exp(2)
                    exp(3)
                    gap("b")
                    gap("c")
                    gap("d")
                    if s == 3 and post:
                        router_exp(g - 1)
                    act.wait_ge(pv_done, 2 * b + 2)
                    act.copy(oT[:, :], att_bank).then_inc(o_copied, 1)
                    gap("e")
                    gap("f")
                    if s == 1 and post:
                        token_high(g - 1, 1 - par, SENT * half_g)

            def tail(g, par, half_g, no):
                for name in POST:
                    stage(name, g, no, par)
                    if name == "wo":
                        token_high(g, par, SENT * half_g)
                    if name == "logits":
                        router_exp(g)

            bodies(act, prologue, body, tail)

            def relu(k, j, bias):
                act.wait_ge(hid_filled, k + 1)
                act.wait_ge(y_filled, k + 1)
                for c in range(FC // 2):
                    act.activation(hid[:, j % 2, c, :], hid_bank(j, c), ACT.Relu,
                                   bias=bias(c)).then_inc(relu_s, 1)

            def dense(k, j, it, more):
                if more > 0:
                    relu(k + 1, j + 1, dense_bias)

            def dense_bias(c):
                return b1_sb[:, E * FC + c:E * FC + c + 1]

            act.wait_ge(consts_v, V_CONSTS + 1)
            act.sem_inc(relu_s, FREE * FC // 2)
            act.sem_inc(tile_copied, FREE)
            relu(0, 0, dense_bias)
            tiles(act, NB, dense)

            def tile_copy(k, j):
                act.wait_ge(tile_filled, k + 1)
                act.wait_ge(hid_filled, NB + k - 1)
                act.copy(tileT[:, j % 2, :], turn_bank[j % 2][:, 0:P].bitcast(F16)).then_inc(tile_copied, 1)

            def expert_relu(k, j):
                e = act.value_load(tab_e[0:1, bass.ds(k, 1)], min_val=0, max_val=E - 1)
                relu(NB + k, j, lambda c: b1_sb[:, bass.ds(e * FC + c, 1)])

            def expert(k, j, it, more):
                if more > 1:
                    tile_copy(k + 2, j)
                if more > 0:
                    expert_relu(k + 1, j + 1)

            act.wait_ge(table, 2)
            tile_copy(0, 0)
            tile_copy(1, 1)
            expert_relu(0, 0)
            tiles(act, NT, expert)

        @block.tensor
        def _(pe):
            pe.wait_ge(consts, POOL_CONSTS)
            pe.wait_ge(consts_s, S_CONSTS)
            pe.wait_ge(consts_v, V_CONSTS)

            def score(b, unit, s, par):
                t = slice(s * P, (s + 1) * P)
                for m in (2 * unit, 2 * unit + 1):
                    for j in range(4):
                        mm = pe.matmul(score_bank[:, m % 2, j * P:(j + 1) * P], q_diag[:, s % 2, m, j, :],
                                       k_rows[:, par, m, t], start=True, stop=True)
                mm.then_inc(score_filled, 1)

            def scoreT(b, m, s, par, waits):
                t = slice(s * P, (s + 1) * P)
                if waits:
                    pe.wait_ge(exp_done, HG * b + {0: 0, 1: -2, 2: -1, 3: 1}[m])
                pe.matmul(st_bank[m], k_rows[:, par, m, t], q_diag[:, s % 2, m, :, :].rearrange("p j t -> p (j t)"),
                          start=True, stop=False)
                pe.matmul(st_bank[m], pick[:, m, :], shift_diag[:, s % 2, :, :].rearrange("p j t -> p (j t)"),
                          start=False, stop=True).then_inc(st_filled, 1)

            def values(b, unit, s, par, waits):
                pe.wait_ge(clamp_done, 2 * b + unit + 1)
                if unit == 0 and waits:
                    pe.wait_ge(att_ready, b)
                for m in (2 * unit, 2 * unit + 1):
                    for j in range(4):
                        mm = pe.matmul(att_bank[32 * j:32 * j + 32, m * P:(m + 1) * P],
                                       v_sb[:, par, s, 4 * m + j, :], probs[:, m, j, :],
                                       start=True, stop=True, tile_position=(0, 32 * j))
                mm.then_inc(pv_done, 1)

            def stage(name, g, no, par, ctx_at=None, turn_b=None):
                ps = stage_bank[no[name].bank]
                if not (isinstance(no[name].at, int) and no[name].at == 0):
                    pe.wait_ge(stage_copied[no[name].bank], no[name].at)
                if name in NEEDS:
                    need = no[NEEDS[name]]
                    pe.wait_ge(stage_copied[need.bank], need.at + 1)
                each = [slice(s * P, (s + 1) * P) for s in range(G)]
                if name == "ctxT":
                    pe.wait_ge(ctx_loaded[par], ctx_at)
                    for s, t in enumerate(each):
                        mm = pe.transpose(ps[0:CK, t], ctx_sb[:, par, s, :], ident[:, :])
                elif name == "xT":
                    pe.wait_ge(xn_ready, G * g + G)
                    for s, t in enumerate(each):
                        mm = pe.transpose(ps[:, t], xn[:, s, :], ident[:, :])
                elif name == "q":
                    mm = pe.matmul(ps, wq_sb[:, :], xnT[:, :], start=True, stop=True)
                elif name == "k":
                    mm = pe.matmul(ps, wk_sb[:, :], ctxT[:, :], start=True, stop=True)
                elif name == "v":
                    for t in each:
                        mm = pe.matmul(ps[:, t], ctxT[:, t], wv_sb[:, :], start=True, stop=True)
                elif name[:2] == "kr":
                    m = int(name[2])
                    for h in range(2):
                        mm = pe.matmul(ps, sel[:, 2 + h, m * P:(m + 1) * P], k_part[:, h, :],
                                       start=(h == 0), stop=(h == 1))
                elif name[:4] == "rows":
                    s1 = (int(name[4]) + 2) % G
                    par1 = par if s1 < 2 else 1 - par
                    for m in range(HG):
                        for h in range(2):
                            mm = pe.matmul(ps[:, m * P:(m + 1) * P], sel[:, h, m * P:(m + 1) * P],
                                           q_part[:, par1, h, s1 * P:(s1 + 1) * P], start=(h == 0), stop=(h == 1))
                elif name[:4] == "turn":
                    s1 = (int(name[4]) + 1) % G
                    pe.wait_ge(shift_steps, 3 * (turn_b + 1))
                    mm = pe.transpose(ps[:, 0:P], shift_part[:, s1 % 2, :, :].rearrange("p j r -> p (j r)").bitcast(F32),
                                      ident[:, :])
                elif name == "attT":
                    pe.wait_ge(att_ready, G * g + G)
                    for s, t in enumerate(each):
                        mm = pe.transpose(ps[:, t], att[:, par, s, :], ident[:, :])
                elif name == "wo":
                    for t in each:
                        mm = pe.matmul(ps[:, t], attT[:, t], wo_sb[:, :], start=True, stop=True)
                elif name == "tokT":
                    pe.wait_ge(tok_low, g + 1)
                    for s in range(G):
                        for h in range(2):
                            mm = pe.transpose(ps.bitcast(F16)[:, (2 * s + h) * P:(2 * s + h + 1) * P],
                                              pay[:, par, s, h * C // 2:(h + 1) * C // 2].bitcast(F16),
                                              ident16[:, :])
                elif name == "logits":
                    for s in range(G):
                        for i, (a, w) in enumerate(((0, 0), (0, 1), (1, 0))):
                            mm = pe.matmul(ps[:, 16 * s:16 * s + RD],
                                           tokT[:, a, bass.ds(g * GT + s * P, P)], wr_part[:, w, :],
                                           start=(i == 0), stop=(i == 2))
                elif name == "rank":
                    pe.wait_ge(route, ROUTE * g + ROUTE_CHOSEN)
                    for s in range(G):
                        for r in range(s + 1):
                            pe.matmul(ps[:, E * s:E * s + E], before[:, :] if r == s else ones16[:, :],
                                      chosen[:, r, :], start=(r == 0), stop=(r == s))
                    for s in range(G):
                        mm = pe.matmul(ps[:, E * G:E * G + E], ones16[:, :], chosen[:, s, :],
                                       start=(s == 0), stop=(s == G - 1))
                elif name == "mixT":
                    pe.wait_ge(route, ROUTE * g + ROUTE)
                    for s, t in enumerate(each):
                        mm = pe.transpose(ps[0:E + 1, t], mixw[:, s, :], ident[:, :])
                elif name == "bias":
                    for t in each:
                        mm = pe.matmul(ps[:, t], mixT[:, t], b2_sb[:, :], start=True, stop=True)
                mm.then_inc(stage_filled, 1)

            def prologue(no):
                for name in PRE[:-1]:
                    stage(name, 0, no, 0, 16)
                for name in ("kr2", "kr3", "rows2", "rows3"):
                    pe.wait_ge(stage_copied[no[name].bank], no[name].at + 1)
                score(0, 0, 0, 0)
                pe.wait_ge(max_done, 1)
                score(0, 1, 0, 0)
                stage("turn3", 0, no, 0, turn_b=0)
                pe.wait_ge(stage_copied[no["turn3"].bank], no["turn3"].at + 1)

            def body(g, par, half_g, no, pre, post):
                for s in range(G):
                    b = G * g + s
                    more = pre or s < G - 1
                    waits = post or s > 0
                    s1, par1 = (s + 1, par) if s < G - 1 else (0, 1 - par)

                    def gap(which):
                        for name in in_gap(s, which, no):
                            stage(name, g + 1 if name in PRE else g - 1, no, 1 - par, 16 * (half_g + 2), b + 1)

                    if more:
                        if s == G - 1:
                            for name in ("kr2", "kr3", "rows2"):
                                pe.wait_ge(stage_copied[no[name].bank], no[name].at + 1)
                        pe.wait_ge(max_done, 2 * b + 2)
                        score(b + 1, 0, s1, par1)
                    for m in range(2):
                        scoreT(b, m, s, par, waits)
                    gap("a")
                    for m in range(2, 4):
                        scoreT(b, m, s, par, waits or m == 3)
                    gap("b")
                    if more:
                        pe.wait_ge(max_done, 2 * b + 3)
                        score(b + 1, 1, s1, par1)
                    gap("c")
                    values(b, 0, s, par, waits)
                    gap("d")
                    values(b, 1, s, par, waits)
                    gap("e")
                    pe.wait_ge(o_copied, b + 1)
                    for m in range(HG):
                        mm = pe.transpose(att_bank[:, m * P:(m + 1) * P], oT[:, m * P:(m + 1) * P], ident[:, :])
                    mm.then_inc(o_turned, 1)
                    gap("f")
                    if more:
                        turn_at = no[f"turn{s}"]
                        pe.wait_ge(stage_copied[turn_at.bank], turn_at.at + 1)

            def tail(g, par, half_g, no):
                for name in POST:
                    stage(name, g, no, par)

            bodies(pe, prologue, body, tail)

            def layer1(k, j, e, x_high, x_low):
                pe.wait_ge(relu_s, 2 * k + 2)
                pe.wait_ge(relu_v, 2 * k + 2)
                for c in range(FC):
                    for i, (w, xp) in enumerate(((0, x_high), (0, x_low), (1, x_high))):
                        mm = pe.matmul(hid_bank(j, c), w1_part[:, w, bass.ds(e * FF + c * P, P)],
                                       xp, start=(i == 0), stop=(i == 2))
                mm.then_inc(hid_filled, 1)

            def layer2(k, j, e):
                pe.wait_ge(y_ready, k + 1)
                for i, c in enumerate((0, FC // 2, 1, FC // 2 + 1)):
                    pe.wait_ge(relu_s if c < FC // 2 else relu_v, 2 * k + c % (FC // 2) + 1 + FREE * FC // 2)
                    mm = pe.matmul(y_bank[j % 2][:, 0:C], hid[:, j % 2, c, :], w2_sb[:, bass.ds((e * FC + c) * C, C)],
                                   start=(i == 0), stop=(i == FC - 1))
                mm.then_inc(y_filled, 1)

            def dense_layer1(b, j):
                layer1(b, j, E, tokT[:, 0, bass.ds(b * P, P)], tokT[:, 1, bass.ds(b * P, P)])

            def dense(k, j, it, more):
                if more > 0:
                    dense_layer1(k + 1, j + 1)
                layer2(k, j, E)

            pe.wait_ge(w1_split, 3 * (E + 1))
            pe.wait_ge(ffn_loaded, 16 * 4)
            pe.wait_ge(exp_done, HG * NB)
            pe.sem_inc(y_filled, FREE)
            dense_layer1(0, 0)
            for i in range(2):
                pe.wait_ge(stage_copied[i], (STAGED + 1 - i) // 2)
            pe.wait_ge(att_ready, NB)
            tiles(pe, NB, dense)

            def turn(k, j, it):
                pe.wait_ge(row_loaded[j % 4], 16 * it + 16)
                pe.wait_ge(tile_copied, k + 1)
                for h in range(2):
                    mm = pe.transpose(turn_bank[j % 2][:, 0:P].bitcast(F16)[:, h * P:(h + 1) * P],
                                      row_sb[:, j % 4, h * C // 2:(h + 1) * C // 2].bitcast(F16), ident16[:, :])
                mm.then_inc(tile_filled, 1)

            def expert_layer1(k, j):
                e = pe.value_load(tab_e[0:1, bass.ds(k, 1)], min_val=0, max_val=E - 1)
                pe.wait_ge(tile_copied, k + 1 + FREE)
                layer1(NB + k, j, e, tileT[:, j % 2, 0:P], tileT[:, j % 2, P:2 * P])

            def expert(k, j, it, more):
                if more > 1:
                    turn(k + 2, j + 2, it + (j + 2) // 4)
                if more > 0:
                    expert_layer1(k + 1, j + 1)
                e = pe.value_load(tab_e[0:1, bass.ds(k, 1)], min_val=0, max_val=E - 1)
                layer2(NB + k, j, e)

            pe.wait_ge(table, 2)
            pe.wait_ge(max_done, 2 * NB)
            turn(0, 0, 0)
            turn(1, 1, 0)
            expert_layer1(0, 0)
            tiles(pe, NT, expert)

        @block.vector
        def _(dve):
            def ln(which, g):
                for s in range(G):
                    dve.bn_stats(ln_raw[:, which, s, :], xs[:, bass.ds(G * g + s, 1), :].rearrange("p a c -> p (a c)"))\
                       .then_inc(ln_stats[which], 1)
                hold(dve, ln_stats[which], G * g + G)
                for s in range(G):
                    dve.bn_aggr(ln_mv[:, which, s, :], ln_raw[:, which, s, :]).then_inc(ln_aggr[which], 1)

            def norm(which, g, to, done):
                dve.wait_ge(ln_inv[which], 2 * g + 2)
                for s in range(G):
                    dve.tensor_scalar(to[:, s, :], xs[:, bass.ds(G * g + s, 1), :].rearrange("p a c -> p (a c)"),
                                      ln_mv[:, which, s, 0:1], ln_rstd[:, which, s:s + 1],
                                      ALU.subtract, ALU.mult).then_inc(done, 1)

            dve.wait_ge(x0_loaded, 16)
            ln(0, 0)
            n = 0

            def made(ins):
                nonlocal n
                n += 1
                ins.then_inc(consts_v, 1)

            made(dve.memset(shift_part[:, :, :, :].bitcast(F32), 0.0))
            made(dve.memset(shift_diag[:, :, :, :].bitcast(F32), 0.0))
            made(dve.memset(q_diag[:, :, :, :, :].bitcast(F32), 0.0))
            norm(0, 0, xn, xn_ready)
            v_all = v_sb[:, :, :, :, :].rearrange("p a s h d -> p (a s h) d")
            made(dve.memset(v_all[:, :, D:D + 1], 1.0))
            made(dve.memset(v_all[:, :, D + 1:32], 0.0))
            dve.wait_ge(small_loaded, 16 * SMALL)
            dve.tensor_scalar(wr_sb[:, :], wr_sb[:, :], WSCALE, None, ALU.mult).then_inc(consts_v, 1)
            n += 1
            dve.wait_ge(consts_v, n)
            made(dve.tensor_copy(wr_part[:, 0, :], wr_sb[:, :]))
            dve.wait_ge(consts_v, n)
            made(dve.tensor_tensor(wr_part[:, 1, :], wr_sb[:, :], wr_part[:, 0, :], ALU.subtract))
            made(dve.tensor_scalar(b2_sb[0:E, :], b2_sb[0:E, :], WSCALE, None, ALU.mult))
            dve.wait_ge(consts, POOL_CONSTS)
            made(dve.tensor_tensor(sel[:, 0, :], sel_raw[:, 0, :], sel_raw[:, 1, :], ALU.add))
            made(dve.tensor_copy(sel[:, 1, :], sel_raw[:, 2, :]))
            made(dve.tensor_tensor(sel[:, 2, :], sel_raw[:, 0, :], sel_raw[:, 2, :], ALU.add))
            made(dve.tensor_copy(sel[:, 3, :], sel_raw[:, 1, :]))
            made(dve.tensor_copy(pick[:, :, :], pick_raw[:, :, :]))
            made(dve.memset(mixw[:, :, :], 0.0))
            assert n == V_CONSTS, n

            def take_max(b, unit, p):
                dve.wait_ge(score_filled, 2 * b + unit + 1)
                dve.tensor_reduce(score_max[:, p, 2 * unit:2 * unit + 2, :],
                                  score_bank.rearrange("p m (j t) -> p m j t", j=4), AX.X, ALU.max)\
                   .then_inc(max_done, 1)

            def shifts(b, p):
                dve.wait_ge(max_done, 2 * b + 2)
                dve.tensor_scalar(shift[:, p, :, :], score_max[:, p, :, :], CLAMP, floor_max, ALU.min, ALU.max)\
                   .then_inc(shift_steps, 1)
                dve.wait_ge(shift_steps, 3 * b + 1)
                dve.tensor_scalar(shift_part[:, p, :, 0:HG], by_j(shift[:, p, :, :]), -1.0, None, ALU.mult)\
                   .then_inc(shift_steps, 1)
                dve.wait_ge(shift_steps, 3 * b + 2)
                dve.scalar_tensor_tensor(out=shift_part[:, p, :, HG:2 * HG], in0=by_j(shift[:, p, :, :]), scalar=-1.0,
                                         in1=shift_part[:, p, :, 0:HG].bitcast(F32),
                                         op0=ALU.mult, op1=ALU.subtract).then_inc(shift_steps, 1)

            def by_j(v):
                return v.rearrange("p m j -> p j m")

            def clamp(b, unit):
                dve.wait_ge(exp_done, HG * b + 2 * unit + 2)
                both = slice(2 * unit, 2 * unit + 2)
                dve.tensor_scalar(probs[:, both, :, :], probs[:, both, :, :], 1.0, TINY, ALU.min, ALU.max)\
                   .then_inc(clamp_done, 1)

            def normalise(b, par, s):
                dve.wait_ge(o_turned, b + 1)
                turned = att_bank.rearrange("p (h r) -> p h r", r=32)
                dve.reciprocal(sums_inv[:, :], turned[:, :, D]).then_inc(sums_ready, 1)
                dve.wait_ge(sums_ready, b + 1)
                dve.tensor_tensor(att[:, par, s, :].rearrange("p (h d) -> p h d", d=D), turned[:, :, 0:D],
                                  sums_inv[:, :].unsqueeze(2).to_broadcast([P, H, D]), ALU.mult)\
                   .then_inc(att_ready, 1)

            def low(name, g, no, par):
                part, col, s = (q_part[:, par], qb_col, q_high) if name == "q" else (k_part, kb_col, k_high)
                dve.wait_ge(s, g + 1)
                dve.scalar_tensor_tensor(out=part[:, 1, :], in0=stage_bank[no[name].bank], scalar=col[:, :],
                                         in1=part[:, 0, :].bitcast(F32), op0=ALU.add, op1=ALU.subtract)\
                   .then_inc(stage_copied[no[name].bank], 1)

            def v_copy(no, par):
                dve.wait_ge(stage_filled, no["v"].n + 1)
                dve.tensor_tensor(v_sb[:, par, :, :, 0:D],
                                  stage_bank[no["v"].bank].rearrange("p (s h d) -> p s h d", s=G, d=D),
                                  vb_row[:, :].rearrange("p (h d) -> p h d", d=D).unsqueeze(1)
                                  .to_broadcast([P, G, H, D]), ALU.add).then_inc(stage_copied[no["v"].bank], 1)

            def residual(name, g, no):
                dve.wait_ge(stage_filled, no[name].n + 1)
                if name == "wo":
                    dve.wait_ge(xbo_ready, g + 1)
                xg = xs[:, bass.ds(G * g, G), :]
                dve.tensor_tensor(xg, stage_bank[no[name].bank].rearrange("p (s c) -> p s c", s=G), xg, ALU.add)\
                   .then_inc(stage_copied[no[name].bank], 1)

            def token_low(g, par):
                dve.wait_ge(tok_high, g + 1)
                dve.tensor_tensor(pay[:, par, :, C // 2:C].bitcast(F16), tok[:, :, :],
                                  pay[:, par, :, 0:C // 2].bitcast(F16), ALU.subtract).then_inc(tok_low, 1)

            class Route:

                def __init__(self, g, at):
                    self.g, self.at = g, at

                def did(self, ins):
                    ins.then_inc(route, 1)
                    self.at += 1

                def wait(self, at):
                    dve.wait_ge(route, ROUTE * self.g + at)

            def each_mask(v):
                return v.unsqueeze(3).to_broadcast([P, G, TOP, E])

            def take_logits(no):
                at = no["logits"]
                dve.wait_ge(stage_filled, at.n + 1)
                dve.scalar_tensor_tensor(
                    out=lg[:, :, 8:8 + RD],
                    in0=stage_bank[at.bank][:, 0:16 * G].rearrange("p (s n) -> p s n", n=16)[:, :, 0:RD],
                    scalar=1.0 / WSCALE, in1=rb_row[:, :].unsqueeze(1).to_broadcast([P, G, RD]),
                    op0=ALU.mult, op1=ALU.add).then_inc(stage_copied[at.bank], 1)

            def choose(g, no):
                r = Route(g, 0)
                hold(dve, stage_copied[no["logits"].bank], no["logits"].at + 1)
                for s in range(G):
                    r.did(dve.max(lg[:, s, 0:8], lg[:, s, 10:10 + E]))
                hold(dve, route, ROUTE * g + G)
                for s in range(G):
                    r.did(dve.max_index(top_at[:, s, :], lg[:, s, 0:8], lg[:, s, 10:10 + E]))
                pairs = lg[:, :, 0:16].rearrange("p s (a r) -> p s a r", a=2)
                r.did(dve.tensor_tensor(dif[:, :, :, 0], pairs[:, :, :, 1], pairs[:, :, :, 0], ALU.subtract))
                r.did(dve.tensor_tensor(dif[:, :, :, 1], pairs[:, :, :, 0], pairs[:, :, :, 1], ALU.subtract))
                assert r.at == ROUTE_DIF
                r.wait(8)
                for_e = expert_no[:, :].unsqueeze(1).unsqueeze(1).to_broadcast([P, G, TOP, E])
                r.did(dve.tensor_tensor(mask[:, :, :, :], each_mask(top_at[:, :, 0:TOP]), for_e, ALU.is_equal))
                r.wait(11)
                r.did(dve.tensor_tensor(chosen[:, :, :], mask[:, :, 0, :], mask[:, :, 1, :], ALU.add))
                assert r.at == ROUTE_CHOSEN

            def place(g, par, no):
                r = Route(g, ROUTE_CHOSEN)
                at = no["rank"]
                dve.wait_ge(stage_filled, at.n + 1)
                ranks = stage_bank[at.bank]
                r.did(dve.tensor_tensor(pos[:, :, :], ranks[:, 0:E * G].rearrange("p (s e) -> p s e", s=G),
                                        count[:, :].unsqueeze(1).to_broadcast([P, G, E]), ALU.add))
                r.did(dve.tensor_tensor(pay[:, par, :, C + E:ROW].bitcast(I32), mask[:, :, 1, :],
                                        target0[:, :].unsqueeze(2).to_broadcast([P, G, E]), ALU.add))
                r.wait(14)
                dve.tensor_tensor(count[:, :], ranks[:, E * G:E * G + E], count[:, :], ALU.add)\
                   .then_inc(stage_copied[at.bank], 1)
                r.did(dve.tensor_scalar(target0[:, :], target0[:, :], float(TOP * GT), None, ALU.add))
                r.did(dve.tensor_tensor(mpos[:, :, :, :], mask[:, :, :, :],
                                        pos[:, :, :].unsqueeze(2).to_broadcast([P, G, TOP, E]), ALU.mult))
                r.wait(16)
                with nc.allow_low_precision(reason="row numbers are exact in float32"):
                    r.did(dve.tensor_reduce(slot_at[:, par, :, :], mpos[:, :, :, :], AX.X, ALU.add))
                assert r.at == ROUTE_PLACED

            def weigh(g, par):
                r = Route(g, ROUTE_PLACED)
                dve.wait_ge(dif_exped, g + 1)
                r.did(dve.tensor_scalar(dif_sum[:, :, :, :], dif_exp[:, :, :, :], 1.0, None, ALU.add))
                r.wait(18)
                r.did(dve.reciprocal(share[:, :, :, :], dif_sum[:, :, :, :]))
                r.wait(19)
                r.did(dve.scalar_tensor_tensor(out=wsh[:, :, :], in0=share[:, :, 0, :], scalar=1.0 / WSCALE,
                                               in1=share[:, :, 1, 0:1].to_broadcast([P, G, TOP]),
                                               op0=ALU.mult, op1=ALU.mult))
                r.did(dve.tensor_scalar(dense_w[:, bass.ds(G * g, G)], share[:, :, 1, 1], 1.0 / WSCALE, None, ALU.mult))
                r.did(dve.tensor_copy(mixw[:, :, E], share[:, :, 1, 1]))
                r.wait(20)
                r.did(dve.tensor_tensor(wmask[:, :, :, :], mask[:, :, :, :], each_mask(wsh[:, :, :]), ALU.mult))
                r.wait(23)
                r.did(dve.tensor_tensor(pay[:, par, :, C:C + E], wmask[:, :, 0, :], wmask[:, :, 1, :], ALU.add))
                r.did(dve.tensor_tensor(mixw[:, :, 0:E], wmask[:, :, 0, :], wmask[:, :, 1, :], ALU.add))
                assert r.at == ROUTE

            def prologue(no):
                low("q", 0, no, 0)
                low("k", 0, no, 0)
                v_copy(no, 0)
                dve.wait_ge(x_loaded, 16)
                take_max(0, 0, 0)
                take_max(0, 1, 0)
                shifts(0, 0)

            def body(g, par, half_g, no, pre, post):
                for s in range(G):
                    b = G * g + s
                    more = pre or s < G - 1
                    p1 = (s + 1) % 2
                    if more:
                        take_max(b + 1, 0, p1)
                    if s == 0 and pre:
                        ln(0, g + 1)
                    clamp(b, 0)
                    if s == 2 and post:
                        token_low(g - 1, 1 - par)
                    if more:
                        take_max(b + 1, 1, p1)
                        shifts(b + 1, p1)
                    if s == 1 and pre:
                        low("q", g + 1, no, 1 - par)
                    clamp(b, 1)
                    if s == 0 and post:
                        residual("wo", g - 1, no)
                    if s == 0 and pre:
                        low("k", g + 1, no, 1 - par)
                        norm(0, g + 1, xn, xn_ready)
                    if s == 1 and post:
                        norm(1, g - 1, tok, tok_ready)
                    if s == 1 and pre:
                        v_copy(no, 1 - par)
                    if s == 3 and post:
                        place(g - 1, 1 - par, no)
                        weigh(g - 1, 1 - par)
                    normalise(b, par, s)
                    if s == 0 and post:
                        ln(1, g - 1)
                    if s == 2 and post:
                        take_logits(no)
                        choose(g - 1, no)
                    if s == 3 and post:
                        residual("bias", g - 1, no)

            def tail(g, par, half_g, no):
                residual("wo", g, no)
                dve.wait_ge(stage_copied[no["wo"].bank], no["wo"].at + 1)
                ln(1, g)
                norm(1, g, tok, tok_ready)
                token_low(g, par)
                take_logits(no)
                choose(g, no)
                place(g, par, no)
                weigh(g, par)
                residual("bias", g, no)

            bodies(dve, prologue, body, tail)

            dve.wait_ge(ffn_loaded, 16 * 4)
            dve.tensor_scalar(b1_sb[:, :], b1_sb[:, :], WSCALE, None, ALU.mult).then_inc(consts_v, 1)
            dve.wait_ge(consts_v, V_CONSTS + 1)
            for i in range(2):
                dve.wait_ge(stage_copied[i], (STAGED + 1 - i) // 2)
            dve.tensor_copy(tab_pad[:, :], count[0:1, :]).then_inc(table, 1)
            steps = 0

            def did(ins):
                nonlocal steps
                steps += 1
                ins.then_inc(tab_steps, 1)
                dve.wait_ge(tab_steps, steps)

            NE = NT + 4
            did(dve.scalar_tensor_tensor(out=n_tok[:, :], in0=expert_no[0:1, :], scalar=-float(CAP),
                                         in1=count[0:1, :], op0=ALU.mult, op1=ALU.add))
            did(dve.tensor_scalar(n_i[:, :], n_tok[:, :], float(P - 1), None, ALU.add))
            did(dve.tensor_scalar(n_tiles_i[:, :], n_i[:, :], P.bit_length() - 1, None, ALU.logical_shift_right))
            did(dve.tensor_copy(n_tiles[:, :], n_tiles_i[:, :]))
            did(dve.tensor_tensor(cum_w[:, :, :], cum_mask[:, :, :],
                                  n_tiles[:, :].unsqueeze(1).to_broadcast([1, E, E]), ALU.mult))
            did(dve.tensor_reduce(cum[:, :], cum_w[:, :, :], AX.X, ALU.add))
            did(dve.tensor_tensor(past[:, :, :], tile_no[:, :].unsqueeze(2).to_broadcast([1, NE, E]),
                                  cum[:, :].unsqueeze(1).to_broadcast([1, NE, E]), ALU.is_ge))
            did(dve.tensor_reduce(tile_e[:, :], past[:, :, :], AX.X, ALU.add))
            did(dve.tensor_tensor(past_w[:, :, :], past[:, :, :],
                                  n_tiles[:, :].unsqueeze(1).to_broadcast([1, NE, E]), ALU.mult))
            did(dve.tensor_reduce(tile_s[:, :], past_w[:, :, :], AX.X, ALU.add))
            did(dve.tensor_tensor(tile_s[:, :], tile_no[:, :], tile_s[:, :], ALU.subtract))
            did(dve.tensor_scalar(tile_s[:, :], tile_s[:, :], float(P), None, ALU.mult))
            did(dve.scalar_tensor_tensor(out=tile_r[:, :], in0=tile_e[:, :], scalar=float(CAP), in1=tile_s[:, :],
                                         op0=ALU.mult, op1=ALU.add))
            did(dve.tensor_scalar(tab_row[:, :], tile_r[:, :], float(E * CAP), None, ALU.min))
            did(dve.tensor_scalar(tab_e[:, :], tile_e[:, :], float(E - 1), None, ALU.min))
            dve.memset(shift[:, 0, 0, 0:1], 0.0).then_inc(table, 1)

            def relu(k, j, bias):
                dve.wait_ge(hid_filled, k + 1)
                dve.wait_ge(y_filled, k + 1)
                for c in range(FC // 2, FC):
                    dve.tensor_scalar(hid[:, j % 2, c, :], hid_bank(j, c), bias(c), 0.0,
                                      ALU.add, ALU.max).then_inc(relu_v, 1)

            def dense_bias(c):
                return b1_sb[:, E * FC + c:E * FC + c + 1]

            def dense(k, j, it, more):
                if more > 0:
                    relu(k + 1, j + 1, dense_bias)
                dve.wait_ge(y_filled, k + 1 + FREE)
                xb = xs[:, bass.ds(k, 1), :].rearrange("p a c -> p (a c)")
                dve.scalar_tensor_tensor(out=xb, in0=y_bank[j % 2][:, 0:C], scalar=dense_w[:, bass.ds(k, 1)],
                                         in1=xb, op0=ALU.mult, op1=ALU.add).then_inc(y_ready, 1)

            dve.sem_inc(relu_v, FREE * FC // 2)
            dve.sem_inc(y_ready, FREE)
            relu(0, 0, dense_bias)
            tiles(dve, NB, dense)

            def expert(k, j, it, more):
                if more > 0:
                    e1 = dve.value_load(tab_e[0:1, bass.ds(k + 1, 1)], min_val=0, max_val=E - 1)
                    relu(NB + k + 1, j + 1, lambda c: b1_sb[:, bass.ds(e1 * FC + c, 1)])
                e = dve.value_load(tab_e[0:1, bass.ds(k, 1)], min_val=0, max_val=E - 1)
                dve.wait_ge(y_sent[j], 16 * it + 16)
                dve.tensor_copy(y_at[:, j:j + 1], row_sb[:, j, bass.ds(e + (C + E), 1)].bitcast(I32)).then_inc(y_target, 1)
                dve.wait_ge(y_filled, NB + k + 1 + FREE)
                dve.tensor_scalar(y_sb[:, j, :], y_bank[j % 2][:, 0:C], row_sb[:, j, bass.ds(e + C, 1)], None,
                                  ALU.mult).then_inc(y_ready, 1)

            e0 = dve.value_load(tab_e[0:1, 0:1], min_val=0, max_val=E - 1)
            relu(NB, 0, lambda c: b1_sb[:, bass.ds(e0 * FC + c, 1)])
            tiles(dve, NT, expert)

            for g in range(NG):
                dve.wait_ge(back_loaded[g % 2], 16 * (g // 2 + 1))
                xg, back = xs[:, G * g:G * g + G, :], y_back[:, g % 2, :, :]
                dve.tensor_tensor(xg, xg, back[:, :, 0:C], ALU.add).then_inc(sum1, 1)
                dve.wait_ge(sum1, g + 1)
                dve.tensor_tensor(xg, xg, back[:, :, C:2 * C], ALU.add).then_inc(sum2, 1)


_INS = ['x', 'ctx_768', 'L0_xattn_Wq', 'L0_xattn_bq', 'L0_xattn_Wk', 'L0_xattn_bk', 'L0_xattn_Wv', 'L0_xattn_bv',
        'L0_xattn_Wo', 'L0_xattn_bo', 'L0_ffn_Wr', 'L0_ffn_br', 'L0_ffn_Wg', 'L0_ffn_bg', 'L0_ffn_W1', 'L0_ffn_b1',
        'L0_ffn_W2', 'L0_ffn_b2', 'L0_ffn_D1', 'L0_ffn_d1b', 'L0_ffn_D2', 'L0_ffn_d2b']
_OUTS = [((32, 128, 128), 'float32')]


def kernel(**inputs):
    import numpy as _np
    import concourse.bacc as _bacc
    from concourse import mybir as _mybir
    from concourse.bass_utils import run_bass_kernel_spmd as _run

    nc = _bacc.Bacc("TRN2", target_bir_lowering=False, num_devices=1)
    arrays, args = {}, []
    for name in _INS:
        a = _np.ascontiguousarray(inputs[name])
        arrays[f"in_{name}_dram"] = a
        args.append(nc.dram_tensor(f"in_{name}_dram", a.shape, _mybir.dt.from_np(a.dtype), kind="ExternalInput").ap())
    for i, (shape, dtype) in enumerate(_OUTS):
        dt = _mybir.dt.from_np(_np.dtype(dtype))
        args.append(nc.dram_tensor(f"out_{i}_dram", shape, dt, kind="ExternalOutput").ap())
    cross_attention_moe(nc, *args)
    r = _run(nc, [arrays], core_ids=[0])
    got = tuple(r.results[0][f"out_{i}_dram"] for i in range(len(_OUTS)))
    return got[0]
```

```python
from contextlib import ExitStack

import concourse.bass as bass
from concourse import mybir

ALU = mybir.AluOpType
ACT = mybir.ActivationFunctionType
AX = mybir.AxisListType
F32 = mybir.dt.float32
F32R = mybir.dt.float32r
F16 = mybir.dt.float16
I32 = mybir.dt.int32
U32 = mybir.dt.uint32

P = 128
CLAMP = 10000.0
EPS = 1e-5
TINY_EXPONENT = 87.0
TINY = 1.6458115e-38
WSCALE = 16.0




def cross_attention_moe(nc, x, ctx_in, wq, bq, wk, bk, wv, bv, wo, bo, wr, br, wg, bg,
                        w1, b1, w2, b2, d1, d1b, d2, d2b, out):
    NB, _, C = x.shape
    CK = ctx_in.shape[2]
    H = 16
    D = C // H
    E = wg.shape[1]
    FF = w1.shape[2]
    FC = FF // P
    TOP = 2
    T = NB * P
    G = 4
    NG = NB // G
    GT = G * P
    HG = H // 4
    RD = E + 2
    ROW = C + 2
    CAP = T + P
    RB = 8
    NT = TOP * T // P + E
    ND = 20
    assert NT % RB == 0 and ND % 2 == 0 and FC * C == FF and NG == 8 and C == P and H * D == C
    q_scale = float(D) ** -0.5
    floor_max = -CLAMP + TINY_EXPONENT

    rows = nc.dram_tensor("routed_rows", (E * CAP + P, ROW), F32, kind="Internal").ap()
    expert_out = nc.dram_tensor("expert_out", (TOP * T, C), F32, kind="Internal").ap()
    x_v = x.rearrange("b s c -> s b c")
    out_v = out.rearrange("b s c -> s b c")
    ctx_v = ctx_in.rearrange("b s c -> s b c")
    w1_v = w1.rearrange("e d f -> d e f")
    w2_v = w2.rearrange("e (c p) d -> p e c d", p=P)
    d2_v = d2.rearrange("(c p) d -> p c d", p=P)
    b1_v = b1.rearrange("e (c p) -> p e c", p=P)
    d1b_v = d1b.rearrange("(c p) -> p c", p=P)

    with ExitStack() as stack:
        def sb(name, shape, dt=F32):
            return stack.enter_context(nc.sbuf_tensor(name, shape, dt))

        def sem(name):
            return stack.enter_context(nc.semaphore(name))

        wq_sb = sb("wq_sb", [P, C])
        wk_sb = sb("wk_sb", [CK, C])
        wv_sb = sb("wv_sb", [CK, C])
        wo_sb = sb("wo_sb", [P, C])
        qb_col = sb("qb_col", [P, 1])
        kb_col = sb("kb_col", [P, 1])
        vb_row = sb("vb_row", [P, C])
        ob_row = sb("ob_row", [P, C])
        wr_sb = sb("wr_sb", [P, RD])
        wr_part = sb("wr_part", [P, 2, RD], F16)
        rb_row = sb("rb_row", [P, RD])
        w1_raw = sb("w1_raw", [P, 2, FF])
        w1_part = sb("w1_part", [P, 2, (E + 1) * FF], F16)
        w2_sb = sb("w2_sb", [P, (E + 1) * FC * C])
        b1_sb = sb("b1_sb", [P, (E + 1) * FC])
        b2_sb = sb("b2_sb", [E + 1, C])
        ident = sb("ident", [P, P])
        ident16 = sb("ident16", [P, P], F16)
        sel = sb("sel", [P, 4, 4 * P], F32R)
        pick = sb("pick", [P, HG, P], F32R)
        before = sb("before", [P, P], F16)
        ones16 = sb("ones16", [P, P], F16)
        expert_no = sb("expert_no", [P, E])
        half = sb("half", [P, G])
        target = sb("target", [P, G, TOP])
        pad_rows = sb("pad_rows", [P, ROW])
        xs = sb("xs", [P, NB, C])
        tokT = sb("tokT", [P, 2, T], F16)
        dense_w = sb("dense_w", [P, NB])
        probs = sb("probs", [P, HG, 4, P])
        early = probs[:, :, :, :].rearrange("p m j t -> p (m j t)")
        sel_raw = early[:, 0:3 * 4 * P].rearrange("p (r n) -> p r n", r=3)
        pick_raw = early[:, 3 * 4 * P:3 * 4 * P + HG]
        ctx_sb = sb("ctx_sb", [P, 2, G, CK])
        ln_raw = sb("ln_raw", [P, 2, G, 6])
        ln_mv = sb("ln_mv", [P, 2, G, 2])
        ln_eps = sb("ln_eps", [P, 2, G])
        ln_rstd = sb("ln_rstd", [P, 2, G])
        xn = sb("xn", [P, G, C])
        xc = sb("xc", [P, G, C])
        xnT = sb("xnT", [P, GT])
        ctxT = sb("ctxT", [CK, GT])
        q_part = sb("q_part", [P, 2, 2, GT], F32R)
        k_part = sb("k_part", [P, 2, GT], F32R)
        k_rows = sb("k_rows", [P, 2, HG, GT], F32R)
        v_sb = sb("v_sb", [P, 2, G, H, 32])
        score_max = sb("score_max", [P, 2, HG, 4])
        shift = sb("shift", [P, 2, 4, HG])
        shift_part = sb("shift_part", [P, 2, 4, 32], F32R)
        q_diag = sb("q_diag", [P, 2, HG, 4, P], F32R)
        shift_diag = sb("shift_diag", [P, 2, 4, P], F32R)
        oT = sb("oT", [P, HG * P])
        sums_inv = sb("sums_inv", [P, H])
        att = sb("att", [P, 2, G, C])
        attT = sb("attT", [P, GT])
        tok = sb("tok", [P, G, C])
        pay = sb("pay", [P, 2, G, TOP, ROW])
        lg = sb("lg", [P, G, 24])
        lg_low = sb("lg_low", [P, G, RD])
        top_at = sb("top_at", [P, G, 8], U32)
        mask = sb("mask", [P, G, TOP, E])
        chosen = sb("chosen", [P, G + 1, E], F16)
        count = sb("count", [P, E])
        pos = sb("pos", [P, G, E])
        mpos = sb("mpos", [P, G, TOP, E])
        slot_at = sb("slot_at", [P, 2, G, TOP], I32)
        dif = sb("dif", [P, G, 2, 2])
        dif_exp = sb("dif_exp", [P, G, 2, 2])
        dif_sum = sb("dif_sum", [P, G, 2, 2])
        share = sb("share", [P, G, 2, 2])
        wsh = sb("wsh", [P, G, TOP])
        wmask = sb("wmask", [P, G, TOP, E])
        mixw = sb("mixw", [P, G, E + 1])
        mixT = sb("mixT", [E + 1, GT])
        cum_mask = sb("cum_mask", [1, E, E])
        tile_no = sb("tile_no", [1, NT])
        n_tok = sb("n_tok", [1, E])
        n_i = sb("n_i", [1, E], I32)
        n_tiles_i = sb("n_tiles_i", [1, E], I32)
        n_tiles = sb("n_tiles", [1, E])
        cum_w = sb("cum_w", [1, E, E])
        cum = sb("cum", [1, E])
        past = sb("past", [1, NT, E])
        past_w = sb("past_w", [1, NT, E])
        tile_e = sb("tile_e", [1, NT])
        tile_s = sb("tile_s", [1, NT])
        tile_r = sb("tile_r", [1, NT])
        tab_w = sb("tab_w", [1, NT], I32)
        tab_b = sb("tab_b", [1, NT], I32)
        tab_row = sb("tab_row", [1, NT], I32)
        tab_pad = sb("tab_pad", [1, E], I32)
        row_sb = sb("row_sb", [P, RB, ROW])
        tileT = sb("tileT", [P, 2, 2 * P], F16)
        late = v_sb[:, 1, :, :, :].rearrange("p s h d -> p (s h d)")
        hid = late[:, 0:2 * FC * P].rearrange("p (a c t) -> p a c t", a=2, c=FC)
        y_sb = late[:, 2 * FC * P:2 * FC * P + RB * C].rearrange("p (a c) -> p a c", a=RB)
        back = [v.rearrange("p (g s c) -> p g s c", s=G, c=TOP * C)[:, i] for v, n in (
            (v_sb[:, 0, :, :, :].rearrange("p s h d -> p (s h d)"), 2),
            (early, 2),
            (k_rows[:, :, :, :].rearrange("p a m t -> p (a m t)").bitcast(F32), 4)) for i in range(n)]
        assert len(back) == NG

        bank = stack.enter_context(nc.psum_tensor("bank", [P, 8, 512], F32))
        score_bank, stage_bank, att_bank = bank[:, 0:2, :], (bank[:, 5, :], bank[:, 6, :]), bank[:, 7, :]
        st_bank = (bank[:, 2, :], bank[:, 3, :], bank[:, 4, :], bank[:, 2, :])
        hid_bank, y_bank, turn_bank = (bank[:, 2, :], bank[:, 3, :]), (bank[:, 0, :], bank[:, 1, :]), \
            (bank[:, 4, :], bank[:, 7, :])

        qk_loaded = sem("qk_loaded")
        small_loaded = sem("small_loaded")
        x0_loaded = sem("x0_loaded")
        x_loaded = sem("x_loaded")
        ctx_loaded = [sem(f"ctx_loaded{i}") for i in range(2)]
        w1_loaded = [sem(f"w1_loaded{i}") for i in range(2)]
        ffn_loaded = sem("ffn_loaded")
        consts = sem("consts")
        v_padded = sem("v_padded")
        consts_s = sem("consts_s")
        consts_v = sem("consts_v")
        ln_stats = [sem("ln1_stats"), sem("ln2_stats")]
        ln_aggr = [sem("ln1_aggr"), sem("ln2_aggr")]
        ln_inv = [sem("ln1_inv"), sem("ln2_inv")]
        xn_ready = sem("xn_ready")
        centred = sem("centred")
        xbo_ready = sem("xbo_ready")
        stage_filled = sem("stage_filled")
        stage_copied = [sem(f"stage{i}_copied") for i in range(2)]
        diag_copied = sem("diag_copied")
        q_high = sem("q_high")
        k_high = sem("k_high")
        score_filled = sem("score_filled")
        max_done = sem("max_done")
        shift_steps = sem("shift_steps")
        st_filled = sem("st_filled")
        exp_done = sem("exp_done")
        clamp_done = sem("clamp_done")
        pv_done = sem("pv_done")
        o_copied = sem("o_copied")
        o_turned = sem("o_turned")
        sums_ready = sem("sums_ready")
        att_ready = sem("att_ready")
        tok_ready = sem("tok_ready")
        tok_high = sem("tok_high")
        tok_low = sem("tok_low")
        route = sem("route")
        dif_exped = sem("dif_exped")
        lg_steps = sem("lg_steps")
        scattered = [sem(f"scattered{i}") for i in range(2)]
        w1_high = sem("w1_high")
        w1_split = sem("w1_split")
        tab_steps = sem("tab_steps")
        table = sem("table")
        pads_written = sem("pads_written")
        hid_filled = sem("hid_filled")
        relu_done = sem("relu_done")
        y_filled = sem("y_filled")
        y_read = sem("y_read")
        row_loaded = [sem(f"row_loaded{i}") for i in range(RB)]
        tile_turned = sem("tile_turned")
        tile_copied = sem("tile_copied")
        y_sent = [sem(f"y_sent{i}") for i in range(RB)]
        back_loaded = [sem(f"back_loaded{i}") for i in range(NG)]
        sum1 = sem("sum1")
        sum2 = sem("sum2")
        stored = sem("stored")

        PRE = ["ctxT", "xT", "q", "k", "v", "kr0", "kr1", "kr2", "kr3", "rows2", "rows3", "turn3"]
        POST = ["attT", "wo", "tokT", "logits", "rank", "mixT", "bias"]
        GAPS = [
            {"a": ["attT"], "b": ["rows0"], "c": ["ctxT"], "e": ["turn0", "wo"]},
            {"a": ["k"], "b": ["rows1"], "c": ["kr0"], "d": ["xT"], "e": ["turn1", "q"]},
            {"a": ["kr1"], "b": ["v", "rows2"], "c": ["tokT"], "d": ["kr3"], "e": ["logits", "turn2"], "f": ["kr2"]},
            {"b": ["mixT", "rows3"], "c": ["rank"], "e": ["turn3"], "f": ["bias"]},
        ]
        NEEDS = {"q": "xT", "k": "ctxT", "v": "ctxT", "kr0": "k", "kr1": "k", "kr2": "k", "kr3": "k", "rows2": "q",
                 "wo": "attT", "logits": "tokT", "bias": "mixT"}
        FULL = [name for slot in GAPS for gap in sorted(slot) for name in slot[gap]]
        FIRST = [name for name in FULL if name not in POST]
        LAST = [name for name in FULL if name in POST or name in ("rows0", "rows1", "turn0", "turn1", "turn2")]
        AT_FIRST = len(PRE)
        AT_LOOP = AT_FIRST + len(FIRST)
        AT_LAST = AT_LOOP + len(FULL) * (NG - 2)
        AT_TAIL = AT_LAST + len(LAST)
        STAGED = AT_TAIL + len(POST)
        assert len(FULL) % 2 == 0
        FOR_QK, SMALL = 4, 10
        POOL_CONSTS, S_CONSTS, V_CONSTS = 27, 3, 14
        IDENT_AT = 8
        ROUTE, ROUTE_DIF, ROUTE_CHOSEN, ROUTE_WEIGHED = 25, 10, 12, 20
        SENT = 16 * TOP * G
        TAIL = ["attT", 0, "wo", 1, 2, "norm", 3, "low", 4, "tokT", 5, "logits", 6, "choose", 7, "weigh", 8, "rank",
                "counts", 9, "mixT", "ends", 10, "bias", "experts", 11, "starts", 12, "rows", 13]

        class Product:

            def __init__(self, base, loops):
                self.turn, self.bank = base, base % 2
                self.n = len(FULL) * loops + base
                self.at = len(FULL) // 2 * loops + base // 2

        def products(base, names, loops=0):
            return {name: Product(base + i, loops) for i, name in enumerate(names)}

        def bodies(eng, prologue, body, tail):
            prologue(products(0, PRE))
            body(0, 0, -1, products(AT_FIRST, FIRST), True, False)
            with eng.Fori(0, (NG - 2) // 2) as i:
                for u in range(2):
                    body(2 * i + 1 + u, (1 + u) % 2, i, products(AT_LOOP + len(FULL) * u, FULL, 2 * i), True, True)
            body(NG - 1, 1, (NG - 2) // 2, products(AT_LAST, LAST), False, True)
            tail(NG - 1, 1, (NG - 1) // 2, products(AT_TAIL, POST))

        def experts_of(s):
            return range(2 * s, 2 * s + 2 if s < G - 1 else E + 1)

        def in_gap(s, which, no):
            return [name for name in GAPS[s].get(which, []) if name in no]

        def hold(eng, s, value):
            eng.wait_ge(s, value)
            eng.nop(nofuse=True)

        def read_table(engine, values, most):
            return nc.values_load_multi_w_load_instructions(
                values, engines=[engine], min_val=0, max_val=most,
                skip_runtime_bounds_check_because="VectorE made the table, and clamps it")[1]

        block = stack.enter_context(nc.Block())

        @block.sync
        def _(sp):
            sp.dma_start(xs[:, 0:G, :], x_v[:, 0:G, :]).then_inc(x0_loaded, 16)
            sp.dma_start(ctx_sb[:, 0, :, :], ctx_v[:, 0:G, :]).then_inc(ctx_loaded[0], 16)

            def row(v, n=P):
                return v.rearrange("(a n) -> a n", a=1).to_broadcast([n, v.shape[0]])

            small = [(wq_sb[:, :], wq), (qb_col[:, :], bq.rearrange("(p a) -> p a", a=1)),
                     (wk_sb[:, :], wk), (kb_col[:, :], bk.rearrange("(p a) -> p a", a=1)),
                     (wv_sb[:, :], wv), (wo_sb[:, :], wo),
                     (vb_row[:, :], row(bv)), (ob_row[:, :], row(bo)), (wr_sb[:, 0:2], wr), (wr_sb[:, 2:RD], wg),
                     (rb_row[:, 0:2], row(br)), (rb_row[:, 2:RD], row(bg)),
                     (b2_sb[0:E, :], b2), (b2_sb[E:E + 1, :], row(d2b, 1))]
            assert len(small) == SMALL + FOR_QK
            for i, (dst, src) in enumerate(small):
                sp.dma_start(dst, src).then_inc(qk_loaded if i < FOR_QK else small_loaded, 16)
            sp.dma_start(ctx_sb[:, 1, :, :], ctx_v[:, G:2 * G, :]).then_inc(ctx_loaded[1], 16)
            sp.dma_start(xs[:, G:NB, :], x_v[:, G:NB, :]).then_inc(x_loaded, 16)
            sp.dma_start(w2_sb[:, 0:E * FC * C].rearrange("p (e c d) -> p e c d", e=E, c=FC), w2_v)\
              .then_inc(ffn_loaded, 16)
            sp.dma_start(w2_sb[:, E * FC * C:].rearrange("p (c d) -> p c d", c=FC), d2_v).then_inc(ffn_loaded, 16)
            with nc.allow_non_contiguous_dma(reason="hidden biases become columns"):
                sp.dma_start(b1_sb[:, 0:E * FC].rearrange("p (e c) -> p e c", e=E), b1_v).then_inc(ffn_loaded, 16)
                sp.dma_start(b1_sb[:, E * FC:], d1b_v).then_inc(ffn_loaded, 16)
            def load_w1(e):
                if e >= 2:
                    sp.wait_ge(w1_split, e - 1)
                sp.dma_start(w1_raw[:, e % 2, :], w1_v[:, e, :] if e < E else d1).then_inc(w1_loaded[e % 2], 16)

            def load_ctx(g, par, former):
                sp.wait_ge(stage_copied[former.bank], former.at + 1)
                sp.dma_start(ctx_sb[:, par, :, :], ctx_v[:, bass.ds(G * g, G), :]).then_inc(ctx_loaded[par], 16)

            load_w1(0)
            load_w1(1)
            load_ctx(2, 0, products(0, PRE)["ctxT"])
            load_ctx(3, 1, products(AT_FIRST, FIRST)["ctxT"])
            for e in range(2, E + 1):
                load_w1(e)
            with sp.Fori(0, (NG - 4) // 2) as i:
                for u in range(2):
                    load_ctx(2 * i + 4 + u, u, products(AT_LOOP + len(FULL) * u, FULL, 2 * i)["ctxT"])

            sp.wait_ge(table, 1)
            for r in read_table(mybir.EngineType.SP, tab_pad[0:1, :], E * CAP - P):
                sp.dma_start(rows[bass.ds(r, P), :], pad_rows[:, :]).then_inc(pads_written, 16)
            sp.wait_ge(pads_written, 16 * E)
            for par in range(2):
                sp.wait_ge(scattered[par], SENT * NG // 2 + 16)
            sp.wait_ge(table, 2)

            for j, r in enumerate(read_table(mybir.EngineType.SP, tab_row[0:1, 0:RB], E * CAP)):
                sp.dma_start(row_sb[:, j, :], rows[bass.ds(r, P), :]).then_inc(row_loaded[j], 16)
            with sp.Fori(1, NT // RB) as it:
                at = read_table(mybir.EngineType.SP, tab_row[0:1, bass.ds(RB * it, RB)], E * CAP)
                for j, r in enumerate(at):
                    sp.wait_ge(y_sent[j], 16 * it)
                    sp.dma_start(row_sb[:, j, :], rows[bass.ds(r, P), :]).then_inc(row_loaded[j], 16)

            for j in range(RB):
                sp.wait_ge(y_sent[j], 16 * NT // RB)
            back_v = expert_out.rearrange("(b p t) c -> p b (t c)", p=P, t=TOP)
            for g in range(NG):
                sp.dma_start(back[g], back_v[:, G * g:G * g + G, :]).then_inc(back_loaded[g], 16)
            for g in range(NG):
                sp.wait_ge(sum2, g + 1)
                sp.dma_start(out_v[:, G * g:G * g + G, :], xs[:, G * g:G * g + G, :]).then_inc(stored, 16)
            sp.wait_ge(stored, 16 * NG)

        @block.gpsimd
        def _(pool):
            n = 0

            def made(ins):
                nonlocal n
                n += 1
                ins.then_inc(consts, 1)

            made(pool.memset(ident[:, :], 0.0))
            made(pool.memset(half[:, :], -0.5))
            made(pool.memset(sel_raw[:, :, :], 0.0))
            made(pool.memset(pick_raw[:, :], 0.0))
            made(pool.memset(pad_rows[:, :], 0.0))
            made(pool.memset(cum_mask[:, :, :], 1.0))
            made(pool.memset(before[:, :], 1.0))
            pool.wait_ge(consts, n)
            made(pool.affine_select(out=ident[:, :], in_=ident[:, :], compare_op=ALU.not_equal, fill=1.0,
                                    base=0, pattern=[[-1, P]], channel_multiplier=1))
            assert n == IDENT_AT

            def rstd(which, g):
                hold(pool, ln_aggr[which], G * g + G)
                pool.tensor_scalar(ln_eps[:, which, :], ln_mv[:, which, :, 1], EPS, None, ALU.add)\
                    .then_inc(ln_inv[which], 1)
                pool.wait_ge(ln_inv[which], 2 * g + 1)
                pool.tensor_tensor(ln_rstd[:, which, :], ln_eps[:, which, :], half[:, :], ALU.pow)\
                    .then_inc(ln_inv[which], 1)

            rstd(0, 0)
            for r in range(3):
                v = sel_raw[:, r, :].rearrange("c (m j r d) -> c m j r d", m=HG, j=4, r=4)[:, :, :, r, :]
                made(pool.affine_select(out=v, in_=v, compare_op=ALU.not_equal, fill=1.0, base=0,
                                        pattern=[[-32, HG], [-8, 4], [-1, D]], channel_multiplier=1))
            for r in range(0, P, 32):
                for low in range(2):
                    pool.wait_ge(consts, n)
                    made(pool.affine_select(out=pick_raw[:, :], in_=pick_raw[:, :], compare_op=ALU.not_equal,
                                            fill=-1.0, base=-(r + HG * low), pattern=[[-1, HG]],
                                            channel_multiplier=1))
            made(pool.iota(expert_no[:, :], [[1, E]], base=0, channel_multiplier=0,
                           allow_small_or_imprecise_dtypes=True))
            made(pool.iota(target[:, :, :], [[TOP * P, G], [1, TOP]], base=0, channel_multiplier=TOP,
                           allow_small_or_imprecise_dtypes=True))
            made(pool.iota(count[:, :], [[CAP, E]], base=0, channel_multiplier=0,
                           allow_small_or_imprecise_dtypes=True))
            made(pool.iota(tile_no[:, :], [[1, NT]], base=0, channel_multiplier=0,
                           allow_small_or_imprecise_dtypes=True))
            made(pool.iota(pad_rows[:, C + 1:ROW].bitcast(I32), [[0, 1]], base=TOP * T, channel_multiplier=1))
            made(pool.affine_select(out=before[:, :], in_=before[:, :], compare_op=ALU.is_gt, fill=0.0,
                                    base=0, pattern=[[1, P]], channel_multiplier=-1))
            made(pool.affine_select(out=cum_mask[:, :, :], in_=cum_mask[:, :, :], compare_op=ALU.is_ge, fill=0.0,
                                    base=0, pattern=[[1, E], [-1, E]], channel_multiplier=0))
            made(pool.memset(ones16[:, :], 1.0))
            assert n == POOL_CONSTS, n
            v_all = v_sb[:, :, :, :, :].rearrange("p a s h d -> p (a s h) d")
            pool.memset(v_all[:, :, D:D + 1], 1.0).then_inc(v_padded, 1)
            pool.memset(v_all[:, :, D + 1:32], 0.0).then_inc(v_padded, 1)

            def add_bo(g):
                hold(pool, xn_ready, G * g + G)
                pool.tensor_tensor(xs[:, bass.ds(G * g, G), :], xs[:, bass.ds(G * g, G), :],
                                   ob_row[:, :].unsqueeze(1).to_broadcast([P, G, C]), ALU.add).then_inc(xbo_ready, 1)

            def scatter(g, par):
                hold(pool, route, ROUTE * g + ROUTE)
                for s in range(G):
                    for t in range(TOP):
                        pool.indirect_dma_start(
                            rows, bass.IndirectOffsetOnAxis(ap=slot_at[:, par, s, t:t + 1], axis=0),
                            pay[:, par, s, t, :], None, bounds_check=E * CAP + P - 1, oob_is_err=False)\
                            .then_inc(scattered[par], 16)

            pool.wait_ge(consts, POOL_CONSTS)
            for i in range(2):
                at = P // 2 * i
                pool.dma_start(rows[E * CAP + at:E * CAP + at + P // 2, :], pad_rows[at:at + P // 2, :])\
                    .then_inc(scattered[i], 16)

            def prologue(no):
                pool.wait_ge(small_loaded, 16 * SMALL)
                add_bo(0)

            def norm_x(g):
                pool.tensor_tensor(xc[:, :, :], xs[:, bass.ds(G * g, G), :],
                                   ln_mv[:, 0, :, 0:1].to_broadcast([P, G, C]), ALU.subtract).then_inc(centred, 1)
                pool.wait_ge(centred, g)
                pool.tensor_tensor(xn[:, :, :], xc[:, :, :],
                                   ln_rstd[:, 0, :].unsqueeze(2).to_broadcast([P, G, C]), ALU.mult).then_inc(xn_ready, G)

            def body(g, par, half_g, no, pre, post):
                if pre:
                    rstd(0, g + 1)
                    norm_x(g + 1)
                if post:
                    rstd(1, g - 1)
                if pre:
                    add_bo(g + 1)
                if post:
                    scatter(g - 1, 1 - par)

            def tail(g, par, half_g, no):
                rstd(1, g)
                scatter(g, par)

            bodies(pool, prologue, body, tail)

            with pool.Fori(0, NT // RB) as it:
                for j in range(RB):
                    hold(pool, y_read, RB * it + (j + 1 + ND))
                    pool.indirect_dma_start(
                        expert_out, bass.IndirectOffsetOnAxis(ap=row_sb[:, j, C + 1:ROW].bitcast(I32), axis=0),
                        y_sb[:, j, :], None, bounds_check=TOP * T - 1, oob_is_err=False).then_inc(y_sent[j], 16)

        class At:

            def __init__(self, number, parity):
                self.number, self.parity = number, parity % 2

            def __add__(self, more):
                return self.number + more

            def __sub__(self, less):
                return self.number - less

            def __mul__(self, by):
                return self.number * by

        def parity(k):
            return k.parity if isinstance(k, At) else k % 2

        def twice(v):
            return v.unsqueeze(2).to_broadcast([P, G, TOP, C])

        def expert_tiles(eng, step, engine=None, tab=None, most=0):
            with eng.Fori(0, NT // RB - 1) as it:
                at = read_table(engine, tab[0:1, bass.ds(RB * it, RB + 4)], most) if engine else [None] * (RB + 1)
                for j in range(RB):
                    step(RB * it + j, j, it, 2, at[j:j + 2])
            at = read_table(engine, tab[0:1, NT - RB:NT], most) if engine else [None] * RB
            for j in range(RB):
                step(NT - RB + j, j, NT // RB - 1, min(2, RB - 1 - j), at[j:j + 2])

        @block.scalar
        def _(act):
            act.wait_ge(consts, IDENT_AT)
            act.copy(ident16[:, :], ident[:, :]).then_inc(consts_s, 1)

            def scale_q():
                act.wait_ge(qk_loaded, 16 * FOR_QK)
                act.mul(wq_sb[:, :], wq_sb[:, :], q_scale).then_inc(consts_s, 1)
                act.mul(qb_col[:, :], qb_col[:, :], q_scale).then_inc(consts_s, 1)
                act.wait_ge(consts_s, S_CONSTS)

            def stage(name, g, no, par):
                if name in ("v", "wo", "logits", "rank", "bias"):
                    return
                act.wait_ge(stage_filled, no[name].n + 1)
                ps, copied = stage_bank[no[name].bank], stage_copied[no[name].bank]
                if name in ("q", "k"):
                    high, col, s = (q_part[:, par, 0, :], qb_col, q_high) if name == "q" \
                        else (k_part[:, 0, :], kb_col, k_high)
                    act.activation(high, ps, ACT.Identity, bias=col[:, :]).then_inc(s, 1)
                elif name[:4] in ("rows", "turn"):
                    p = (int(name[4]) + (name[:4] == "turn")) % 2
                    for j in range(4):
                        rows_j = slice(32 * j, 32 * j + 32)
                        if name[:4] == "rows":
                            dst, src = q_diag[rows_j, p, :, j, :], ps[rows_j, :].rearrange("p (m t) -> p m t", m=HG)
                        else:
                            dst, src = shift_diag[rows_j, p, j, :], ps[rows_j, 0:P]
                        act.copy(dst, src).then_inc(copied if j == 3 else diag_copied, 1)
                else:
                    if name == "tokT":
                        dst = tokT[:, :, bass.ds(g * GT, GT)].rearrange("p h (s t) -> p s h t", s=G)
                        src = ps.bitcast(F16).rearrange("p (s h t) -> p s h t", s=G, h=2)
                    else:
                        dst, src = {
                            "ctxT": lambda: (ctxT[:, :], ps[0:CK, :]),
                            "xT": lambda: (xnT[:, :], ps),
                            "kr": lambda: (k_rows[:, par, int(name[2]), :], ps),
                            "attT": lambda: (attT[:, :], ps),
                            "mixT": lambda: (mixT[:, :], ps[0:E + 1, :]),
                        }[name.rstrip("0123")]()
                    act.copy(dst, src).then_inc(copied, 1)

            def token_high(g, par, sent):
                act.wait_ge(scattered[par], sent + 16)
                act.wait_ge(tok_ready, G * g + G)
                act.copy(pay[:, par, :, :, 0:C // 2].bitcast(F16), twice(tok[:, :, :])).then_inc(tok_high, 1)

            def router_exp(g):
                act.wait_ge(route, ROUTE * g + ROUTE_DIF)
                act.activation(dif_exp[:, :, :, :], dif[:, :, :, :], ACT.Exp).then_inc(dif_exped, 1)

            def prologue(no):
                for name in PRE:
                    if name == "q":
                        scale_q()
                    if name == "rows2":
                        act.wait_ge(consts_v, V_CONSTS)
                    stage(name, 0, no, 0)

            def body(g, par, half_g, no, pre, post):
                for s in range(G):
                    b = G * g + s

                    def gap(which):
                        for name in in_gap(s, which, no):
                            stage(name, g + 1 if name in PRE else g - 1, no, 1 - par)

                    def exp(m):
                        act.wait_ge(st_filled, HG * b + m + 1)
                        if post or s > 0:
                            act.wait_ge(pv_done, 2 * b + m // 2 - 1)
                        act.activation(probs[:, m, :, :].rearrange("p j t -> p (j t)"), st_bank[m], ACT.Exp)\
                            .then_inc(exp_done, 1)

                    exp(0)
                    exp(1)
                    gap("a")
                    exp(2)
                    exp(3)
                    gap("b")
                    gap("c")
                    gap("d")
                    act.wait_ge(pv_done, 2 * b + 2)
                    act.copy(oT[:, :], att_bank).then_inc(o_copied, 1)
                    gap("e")
                    if s == 1 and post:
                        token_high(g - 1, 1 - par, SENT * half_g)
                    gap("f")
                    if s == 2 and post:
                        router_exp(g - 1)
                    if not post:
                        for e in experts_of(s):
                            act.wait_ge(w1_loaded[e % 2], 16 * (e // 2 + 1))
                            act.mul(w1_part[:, 0, e * FF:(e + 1) * FF], w1_raw[:, e % 2, :], WSCALE).then_inc(w1_high, 1)

            def relu(k, bias):
                act.wait_ge(hid_filled, k + 1)
                if not isinstance(k, int) or k >= 2:
                    act.wait_ge(y_filled, k - 1)
                for c in range(FC):
                    act.activation(hid[:, parity(k), c, :], hid_bank[parity(k)][:, c * P:(c + 1) * P], ACT.Relu,
                                   bias=bias[:, c:c + 1]).then_inc(relu_done, 1)

            dense_bias = b1_sb[:, E * FC:(E + 1) * FC]

            def tail(g, par, half_g, no):
                act.wait_ge(consts_v, V_CONSTS + 1)
                relu(0, dense_bias)
                for step in TAIL:
                    if isinstance(step, int):
                        relu(step + 1, dense_bias)
                    if step in POST:
                        stage(step, g, no, par)
                    if step == "norm":
                        token_high(g, par, SENT * half_g)
                    if step == "choose":
                        router_exp(g)

            bodies(act, prologue, body, tail)

            for k in range(TAIL[-1] + 1, ND - 1):
                relu(k + 1, dense_bias)

            def expert(k, j, it, more, at):
                if more > 0:
                    relu(At(ND + k + 1, j + 1), b1_sb[:, bass.ds(at[1], FC)])

            act.wait_ge(table, 2)
            at0 = act.value_load(tab_b[0:1, 0:1], min_val=0, max_val=(E - 1) * FC)
            relu(ND, b1_sb[:, bass.ds(at0, FC)])
            expert_tiles(act, expert, mybir.EngineType.Activation, tab_b, (E - 1) * FC)
            for k in range(ND, NB):
                relu(NT + k, dense_bias)

        @block.tensor
        def _(pe):
            pe.wait_ge(consts, IDENT_AT)

            def score(b, unit, s, par):
                t = slice(s * P, (s + 1) * P)
                for m in (2 * unit, 2 * unit + 1):
                    for j in range(4):
                        mm = pe.matmul(score_bank[:, m % 2, j * P:(j + 1) * P], q_diag[:, s % 2, m, j, :],
                                       k_rows[:, par, m, t], start=True, stop=True)
                mm.then_inc(score_filled, 1)

            def key_rows(no, unit):
                first, second = sorted((no[f"kr{m}"] for m in (2 * unit, 2 * unit + 1)), key=lambda at: at.turn)
                if first.bank != second.bank:
                    pe.wait_ge(stage_copied[first.bank], first.at + 1)
                pe.wait_ge(stage_copied[second.bank], second.at + 1)

            def scoreT(b, m, s, par, waits):
                t = slice(s * P, (s + 1) * P)
                if (m == 0 and waits) or m == 3:
                    pe.wait_ge(exp_done, HG * b + (m == 3))
                pe.matmul(st_bank[m], k_rows[:, par, m, t], q_diag[:, s % 2, m, :, :].rearrange("p j t -> p (j t)"),
                          start=True, stop=False)
                pe.matmul(st_bank[m], pick[:, m, :], shift_diag[:, s % 2, :, :].rearrange("p j t -> p (j t)"),
                          start=False, stop=True).then_inc(st_filled, 1)

            def values(b, unit, s, par, waits):
                pe.wait_ge(clamp_done, 2 * b + unit + 1)
                if unit == 0 and waits:
                    pe.wait_ge(att_ready, b)
                for m in (2 * unit, 2 * unit + 1):
                    for j in range(4):
                        mm = pe.matmul(att_bank[32 * j:32 * j + 32, m * P:(m + 1) * P],
                                       v_sb[:, par, s, 4 * m + j, :], probs[:, m, j, :],
                                       start=True, stop=True, tile_position=(0, 32 * j))
                mm.then_inc(pv_done, 1)

            def stage(name, g, no, par, ctx_at=None, turn_b=None):
                ps = stage_bank[no[name].bank]
                if not (isinstance(no[name].at, int) and no[name].at == 0):
                    pe.wait_ge(stage_copied[no[name].bank], no[name].at)
                if name in NEEDS:
                    need = no[NEEDS[name]]
                    pe.wait_ge(stage_copied[need.bank], need.at + 1)
                each = [slice(s * P, (s + 1) * P) for s in range(G)]
                if name == "ctxT":
                    pe.wait_ge(ctx_loaded[par], ctx_at)
                    for s, t in enumerate(each):
                        mm = pe.transpose(ps[0:CK, t], ctx_sb[:, par, s, :], ident[:, :])
                elif name == "xT":
                    pe.wait_ge(xn_ready, G * g + G)
                    for s, t in enumerate(each):
                        mm = pe.transpose(ps[:, t], xn[:, s, :], ident[:, :])
                elif name == "q":
                    mm = pe.matmul(ps, wq_sb[:, :], xnT[:, :], start=True, stop=True)
                elif name == "k":
                    mm = pe.matmul(ps, wk_sb[:, :], ctxT[:, :], start=True, stop=True)
                elif name == "v":
                    for t in each:
                        mm = pe.matmul(ps[:, t], ctxT[:, t], wv_sb[:, :], start=True, stop=True)
                elif name[:2] == "kr":
                    m = int(name[2])
                    for h in range(2):
                        mm = pe.matmul(ps, sel[:, 2 + h, m * P:(m + 1) * P], k_part[:, h, :],
                                       start=(h == 0), stop=(h == 1))
                elif name[:4] == "rows":
                    s1 = (int(name[4]) + 2) % G
                    par1 = par if s1 < 2 else 1 - par
                    for m in range(HG):
                        for h in range(2):
                            mm = pe.matmul(ps[:, m * P:(m + 1) * P], sel[:, h, m * P:(m + 1) * P],
                                           q_part[:, par1, h, s1 * P:(s1 + 1) * P], start=(h == 0), stop=(h == 1))
                elif name[:4] == "turn":
                    s1 = (int(name[4]) + 1) % G
                    pe.wait_ge(shift_steps, 3 * (turn_b + 1))
                    mm = pe.transpose(ps[:, 0:P], shift_part[:, s1 % 2, :, :].rearrange("p j r -> p (j r)").bitcast(F32),
                                      ident[:, :])
                elif name == "attT":
                    pe.wait_ge(att_ready, G * g + G)
                    for s, t in enumerate(each):
                        mm = pe.transpose(ps[:, t], att[:, par, s, :], ident[:, :])
                elif name == "wo":
                    for t in each:
                        mm = pe.matmul(ps[:, t], attT[:, t], wo_sb[:, :], start=True, stop=True)
                elif name == "tokT":
                    pe.wait_ge(tok_low, g + 1)
                    for s in range(G):
                        for h in range(2):
                            mm = pe.transpose(ps.bitcast(F16)[:, (2 * s + h) * P:(2 * s + h + 1) * P],
                                              pay[:, par, s, 0, h * C // 2:(h + 1) * C // 2].bitcast(F16),
                                              ident16[:, :])
                elif name == "logits":
                    for s in range(G):
                        t = bass.ds(g * GT + s * P, P)
                        pe.matmul(ps[:, 32 * s:32 * s + 2 * RD], tokT[:, 0, t],
                                  wr_part[:, :, :].rearrange("p w n -> p (w n)"), start=True, stop=False)
                        mm = pe.matmul(ps[:, 32 * s:32 * s + RD], tokT[:, 1, t], wr_part[:, 0, :],
                                       start=False, stop=True)
                elif name == "rank":
                    pe.wait_ge(route, ROUTE * g + ROUTE_CHOSEN)
                    pe.matmul(ps[:, 0:E * (G + 1)], before[:, :], chosen[:, :, :].rearrange("p s e -> p (s e)"),
                              start=True, stop=False)
                    for r in range(1, G + 1):
                        mm = pe.matmul(ps[:, E * r:E * (G + 1)], ones16[:, :],
                                       chosen[:, 0:G + 1 - r, :].rearrange("p s e -> p (s e)"),
                                       start=False, stop=(r == G))
                elif name == "mixT":
                    pe.wait_ge(route, ROUTE * g + ROUTE_WEIGHED)
                    for s, t in enumerate(each):
                        mm = pe.transpose(ps[0:E + 1, t], mixw[:, s, :], ident[:, :])
                elif name == "bias":
                    for t in each:
                        mm = pe.matmul(ps[:, t], mixT[:, t], b2_sb[:, :], start=True, stop=True)
                mm.then_inc(stage_filled, 1)

            def prologue(no):
                for name in PRE[:-1]:
                    if name == "q":
                        pe.wait_ge(consts_s, S_CONSTS)
                    if name == "v":
                        pe.wait_ge(small_loaded, 16 * SMALL)
                    if name == "kr0":
                        pe.wait_ge(consts_v, V_CONSTS)
                    stage(name, 0, no, 0, 16)
                pe.wait_ge(v_padded, 2)
                for name in ("kr2", "kr3", "rows2", "rows3"):
                    pe.wait_ge(stage_copied[no[name].bank], no[name].at + 1)
                score(0, 0, 0, 0)
                pe.wait_ge(max_done, 1)
                score(0, 1, 0, 0)
                stage("turn3", 0, no, 0, turn_b=0)
                pe.wait_ge(stage_copied[no["turn3"].bank], no["turn3"].at + 1)

            def body(g, par, half_g, no, pre, post):
                for s in range(G):
                    b = G * g + s
                    more = pre or s < G - 1
                    waits = post or s > 0
                    s1, par1 = (s + 1, par) if s < G - 1 else (0, 1 - par)

                    def gap(which):
                        for name in in_gap(s, which, no):
                            stage(name, g + 1 if name in PRE else g - 1, no, 1 - par, 16 * (half_g + 2), b + 1)

                    if more:
                        if s == G - 1:
                            key_rows(no, 0)
                        score(b + 1, 0, s1, par1)
                    for m in range(2):
                        scoreT(b, m, s, par, waits)
                    gap("a")
                    for m in range(2, 4):
                        scoreT(b, m, s, par, waits or m == 3)
                    gap("b")
                    if more:
                        if s == G - 1:
                            key_rows(no, 1)
                        pe.wait_ge(max_done, 2 * b + 3)
                        score(b + 1, 1, s1, par1)
                    gap("c")
                    values(b, 0, s, par, waits)
                    gap("d")
                    values(b, 1, s, par, waits)
                    gap("e")
                    pe.wait_ge(o_copied, b + 1)
                    for m in range(HG):
                        mm = pe.transpose(att_bank[:, m * P:(m + 1) * P], oT[:, m * P:(m + 1) * P], ident[:, :])
                    mm.then_inc(o_turned, 1)
                    gap("f")
                    if more:
                        turn_at = no[f"turn{s}"]
                        pe.wait_ge(stage_copied[turn_at.bank], turn_at.at + 1)

            def layer1(k, e, x_high, x_low):
                parts = [w1_part[:, w, bass.ds(e, FF)] for w in range(2)]
                for c in range(FC):
                    for i, (w, xp) in enumerate(((0, x_high), (0, x_low), (1, x_high))):
                        mm = pe.matmul(hid_bank[parity(k)][:, c * P:(c + 1) * P], parts[w][:, c * P:(c + 1) * P],
                                       xp, start=(i == 0), stop=(i == 2))
                mm.then_inc(hid_filled, 1)

            def layer2(k, e):
                if not isinstance(k, int) or k >= 2:
                    pe.wait_ge(y_read, k - 1)
                pe.wait_ge(relu_done, k * FC + FC)
                w2_e = w2_sb[:, bass.ds(e, FC * C)]
                for c in range(FC):
                    mm = pe.matmul(y_bank[parity(k)][:, 0:C], hid[:, parity(k), c, :], w2_e[:, c * C:(c + 1) * C],
                                   start=(c == 0), stop=(c == FC - 1))
                mm.then_inc(y_filled, 1)

            def dense_layer1(b, k):
                layer1(k, E * FF, tokT[:, 0, b * P:(b + 1) * P], tokT[:, 1, b * P:(b + 1) * P])

            def tail(g, par, half_g, no):
                pe.wait_ge(w1_split, E + 1)
                pe.wait_ge(ffn_loaded, 16 * 4)
                pe.wait_ge(exp_done, HG * NB)
                pe.wait_ge(max_done, 2 * NB)
                dense_layer1(0, 0)
                for step in TAIL:
                    if isinstance(step, int):
                        dense_layer1(step + 1, step + 1)
                        layer2(step, E * FF)
                    if step in POST:
                        stage(step, g, no, par)

            bodies(pe, prologue, body, tail)

            for k in range(TAIL[-1] + 1, ND - 1):
                dense_layer1(k + 1, k + 1)
                layer2(k, E * FF)

            def turn(k, j, it):
                pe.wait_ge(row_loaded[j % RB], 16 * it + 16)
                for h in range(2):
                    mm = pe.transpose(turn_bank[j % 2][:, 0:P].bitcast(F16)[:, h * P:(h + 1) * P],
                                      row_sb[:, j % RB, h * C // 2:(h + 1) * C // 2].bitcast(F16), ident16[:, :])
                mm.then_inc(tile_turned, 1)

            def expert_layer1(k, j, e):
                pe.wait_ge(tile_copied, k + 1)
                layer1(At(ND + k, j), e, tileT[:, j % 2, 0:P], tileT[:, j % 2, P:2 * P])

            def expert(k, j, it, more, at):
                if more > 0:
                    expert_layer1(k + 1, j + 1, at[1])
                else:
                    dense_layer1(ND, NT + ND)
                if more > 1:
                    turn(k + 2, j + 2, it + (j + 2) // RB)
                layer2(At(ND + k, j), at[0])

            pe.wait_ge(att_ready, NB)
            pe.wait_ge(table, 2)
            turn(0, 0, 0)
            turn(1, 1, 0)
            expert_layer1(0, 0, pe.value_load(tab_w[0:1, 0:1], min_val=0, max_val=(E - 1) * FF))
            layer2(ND - 1, E * FF)
            expert_tiles(pe, expert, mybir.EngineType.PE, tab_w, (E - 1) * FF)
            for k in range(ND, NB):
                if k + 1 < NB:
                    dense_layer1(k + 1, NT + k + 1)
                layer2(NT + k, E * FF)

        @block.vector
        def _(dve):
            def ln(which, g):
                for s in range(G):
                    dve.bn_stats(ln_raw[:, which, s, :], xs[:, bass.ds(G * g + s, 1), :].rearrange("p a c -> p (a c)"))\
                       .then_inc(ln_stats[which], 1)
                hold(dve, ln_stats[which], G * g + G)
                for s in range(G):
                    dve.bn_aggr(ln_mv[:, which, s, :], ln_raw[:, which, s, :]).then_inc(ln_aggr[which], 1)

            def norm(which, g, to, done):
                dve.wait_ge(ln_inv[which], 2 * g + 2)
                for s in range(G):
                    dve.tensor_scalar(to[:, s, :], xs[:, bass.ds(G * g + s, 1), :].rearrange("p a c -> p (a c)"),
                                      ln_mv[:, which, s, 0:1], ln_rstd[:, which, s:s + 1],
                                      ALU.subtract, ALU.mult).then_inc(done, 1)

            dve.wait_ge(x0_loaded, 16)
            ln(0, 0)
            n = 0

            def made(ins):
                nonlocal n
                n += 1
                ins.then_inc(consts_v, 1)

            made(dve.memset(shift_part[:, :, :, :].bitcast(F32), 0.0))
            made(dve.memset(shift_diag[:, :, :, :].bitcast(F32), 0.0))
            norm(0, 0, xn, xn_ready)
            made(dve.memset(q_diag[:, :, :, :, :].bitcast(F32), 0.0))
            dve.wait_ge(small_loaded, 16 * SMALL)
            dve.tensor_scalar(wr_sb[:, :], wr_sb[:, :], WSCALE, None, ALU.mult).then_inc(consts_v, 1)
            n += 1
            dve.wait_ge(consts_v, n)
            made(dve.tensor_copy(wr_part[:, 0, :], wr_sb[:, :]))
            dve.wait_ge(consts_v, n)
            made(dve.tensor_tensor(wr_part[:, 1, :], wr_sb[:, :], wr_part[:, 0, :], ALU.subtract))
            made(dve.tensor_scalar(b2_sb[0:E, :], b2_sb[0:E, :], WSCALE, None, ALU.mult))
            dve.wait_ge(consts, POOL_CONSTS)
            made(dve.tensor_tensor(sel[:, 0, :], sel_raw[:, 0, :], sel_raw[:, 1, :], ALU.add))
            made(dve.tensor_copy(sel[:, 1, :], sel_raw[:, 2, :]))
            made(dve.tensor_tensor(sel[:, 2, :], sel_raw[:, 0, :], sel_raw[:, 2, :], ALU.add))
            made(dve.tensor_copy(sel[:, 3, :], sel_raw[:, 1, :]))
            made(dve.tensor_copy(pick[:, :, :], pick_raw[:, :].unsqueeze(2).to_broadcast([P, HG, P])))
            made(dve.memset(mixw[:, :, :], 0.0))
            made(dve.memset(chosen[:, :, :], 0.0))
            assert n == V_CONSTS, n

            def w1_low(e):
                dve.wait_ge(w1_high, e + 1)
                dve.scalar_tensor_tensor(out=w1_part[:, 1, e * FF:(e + 1) * FF], in0=w1_raw[:, e % 2, :], scalar=WSCALE,
                                         in1=w1_part[:, 0, e * FF:(e + 1) * FF], op0=ALU.mult, op1=ALU.subtract)\
                   .then_inc(w1_split, 1)

            def take_max(b, unit, p):
                dve.wait_ge(score_filled, 2 * b + unit + 1)
                dve.tensor_reduce(score_max[:, p, 2 * unit:2 * unit + 2, :],
                                  score_bank.rearrange("p m (j t) -> p m j t", j=4), AX.X, ALU.max)\
                   .then_inc(max_done, 1)

            def shifts(b, p):
                dve.wait_ge(max_done, 2 * b + 2)
                dve.tensor_scalar(shift_part[:, p, :, 0:HG], by_j(score_max[:, p, :, :]), CLAMP, floor_max,
                                  ALU.min, ALU.max).then_inc(shift_steps, 1)
                dve.tensor_scalar(shift[:, p, :, :], by_j(score_max[:, p, :, :]), CLAMP, floor_max,
                                  ALU.min, ALU.max).then_inc(shift_steps, 1)
                dve.wait_ge(shift_steps, 3 * b + 2)
                dve.tensor_tensor(shift_part[:, p, :, HG:2 * HG], shift[:, p, :, :],
                                  shift_part[:, p, :, 0:HG].bitcast(F32), ALU.subtract).then_inc(shift_steps, 1)

            def by_j(v):
                return v.rearrange("p m j -> p j m")

            def clamp(b, unit):
                dve.wait_ge(exp_done, HG * b + 2 * unit + 2)
                both = slice(2 * unit, 2 * unit + 2)
                dve.tensor_scalar(probs[:, both, :, :], probs[:, both, :, :], 1.0, TINY, ALU.min, ALU.max)\
                   .then_inc(clamp_done, 1)

            def normalise(b, par, s):
                dve.wait_ge(o_turned, b + 1)
                turned = att_bank.rearrange("p (h r) -> p h r", r=32)
                dve.reciprocal(sums_inv[:, :], turned[:, :, D]).then_inc(sums_ready, 1)
                dve.wait_ge(sums_ready, b + 1)
                dve.tensor_tensor(att[:, par, s, :].rearrange("p (h d) -> p h d", d=D), turned[:, :, 0:D],
                                  sums_inv[:, :].unsqueeze(2).to_broadcast([P, H, D]), ALU.mult)\
                   .then_inc(att_ready, 1)

            def low(name, g, no, par):
                part, col, s = (q_part[:, par], qb_col, q_high) if name == "q" else (k_part, kb_col, k_high)
                dve.wait_ge(s, g + 1)
                dve.scalar_tensor_tensor(out=part[:, 1, :], in0=stage_bank[no[name].bank], scalar=col[:, :],
                                         in1=part[:, 0, :].bitcast(F32), op0=ALU.add, op1=ALU.subtract)\
                   .then_inc(stage_copied[no[name].bank], 1)

            def v_copy(no, par):
                dve.wait_ge(stage_filled, no["v"].n + 1)
                dve.tensor_tensor(v_sb[:, par, :, :, 0:D],
                                  stage_bank[no["v"].bank].rearrange("p (s h d) -> p s h d", s=G, d=D),
                                  vb_row[:, :].rearrange("p (h d) -> p h d", d=D).unsqueeze(1)
                                  .to_broadcast([P, G, H, D]), ALU.add).then_inc(stage_copied[no["v"].bank], 1)

            def residual(name, g, no):
                dve.wait_ge(stage_filled, no[name].n + 1)
                if name == "wo":
                    dve.wait_ge(xbo_ready, g + 1)
                xg = xs[:, bass.ds(G * g, G), :]
                dve.tensor_tensor(xg, stage_bank[no[name].bank].rearrange("p (s c) -> p s c", s=G), xg, ALU.add)\
                   .then_inc(stage_copied[no[name].bank], 1)

            def token_low(g, par):
                dve.wait_ge(tok_high, g + 1)
                dve.tensor_tensor(pay[:, par, :, :, C // 2:C].bitcast(F16), twice(tok[:, :, :]),
                                  pay[:, par, :, :, 0:C // 2].bitcast(F16), ALU.subtract).then_inc(tok_low, 1)

            class Route:

                def __init__(self, g, at):
                    self.g, self.at = g, at

                def did(self, ins):
                    ins.then_inc(route, 1)
                    self.at += 1

                def wait(self, at):
                    dve.wait_ge(route, ROUTE * self.g + at)

            def each_mask(v):
                return v.unsqueeze(3).to_broadcast([P, G, TOP, E])

            def take_logits(g, no):
                at = no["logits"]
                dve.wait_ge(stage_filled, at.n + 1)
                sums = stage_bank[at.bank][:, 0:32 * G].rearrange("p (s n) -> p s n", n=32)
                dve.scalar_tensor_tensor(out=lg_low[:, :, :], in0=sums[:, :, RD:2 * RD], scalar=1.0 / WSCALE,
                                         in1=rb_row[:, :].unsqueeze(1).to_broadcast([P, G, RD]),
                                         op0=ALU.mult, op1=ALU.add).then_inc(lg_steps, 1)
                dve.wait_ge(lg_steps, g + 1)
                dve.scalar_tensor_tensor(out=lg[:, :, 8:8 + RD], in0=sums[:, :, 0:RD], scalar=1.0 / WSCALE,
                                         in1=lg_low[:, :, :], op0=ALU.mult, op1=ALU.add)\
                   .then_inc(stage_copied[at.bank], 1)

            def choose(g, no):
                r = Route(g, 0)
                hold(dve, stage_copied[no["logits"].bank], no["logits"].at + 1)
                for s in range(G):
                    r.did(dve.max(lg[:, s, 0:8], lg[:, s, 10:10 + E]))
                hold(dve, route, ROUTE * g + G)
                for s in range(G):
                    r.did(dve.max_index(top_at[:, s, :], lg[:, s, 0:8], lg[:, s, 10:10 + E]))
                pairs = lg[:, :, 0:16].rearrange("p s (a r) -> p s a r", a=2)
                r.did(dve.tensor_tensor(dif[:, :, :, 0], pairs[:, :, :, 1], pairs[:, :, :, 0], ALU.subtract))
                r.did(dve.tensor_tensor(dif[:, :, :, 1], pairs[:, :, :, 0], pairs[:, :, :, 1], ALU.subtract))
                assert r.at == ROUTE_DIF
                r.wait(8)
                for_e = expert_no[:, :].unsqueeze(1).unsqueeze(1).to_broadcast([P, G, TOP, E])
                r.did(dve.tensor_tensor(mask[:, :, :, :], each_mask(top_at[:, :, 0:TOP]), for_e, ALU.is_equal))
                r.wait(11)
                r.did(dve.tensor_tensor(chosen[:, 0:G, :], mask[:, :, 0, :], mask[:, :, 1, :], ALU.add))
                assert r.at == ROUTE_CHOSEN

            def weigh(g, par):
                r = Route(g, ROUTE_CHOSEN)
                dve.wait_ge(dif_exped, g + 1)
                r.did(dve.tensor_scalar(dif_sum[:, :, :, :], dif_exp[:, :, :, :], 1.0, None, ALU.add))
                r.wait(13)
                r.did(dve.reciprocal(share[:, :, :, :], dif_sum[:, :, :, :]))
                r.wait(14)
                r.did(dve.scalar_tensor_tensor(out=wsh[:, :, :], in0=share[:, :, 0, :], scalar=1.0 / WSCALE,
                                               in1=share[:, :, 1, 0:1].to_broadcast([P, G, TOP]),
                                               op0=ALU.mult, op1=ALU.mult))
                r.did(dve.tensor_scalar(dense_w[:, bass.ds(G * g, G)], share[:, :, 1, 1], 1.0 / WSCALE, None, ALU.mult))
                r.did(dve.tensor_copy(mixw[:, :, E], share[:, :, 1, 1]))
                r.wait(15)
                r.did(dve.tensor_tensor(wmask[:, :, :, :], mask[:, :, :, :], each_mask(wsh[:, :, :]), ALU.mult))
                r.did(dve.tensor_copy(pay[:, par, :, :, C], wsh[:, :, :]))
                r.wait(18)
                r.did(dve.tensor_tensor(mixw[:, :, 0:E], wmask[:, :, 0, :], wmask[:, :, 1, :], ALU.add))
                assert r.at == ROUTE_WEIGHED

            def place(g, par, no):
                r = Route(g, ROUTE_WEIGHED)
                at = no["rank"]
                dve.wait_ge(stage_filled, at.n + 1)
                ranks = stage_bank[at.bank]
                r.did(dve.tensor_tensor(pos[:, :, :], ranks[:, 0:E * G].rearrange("p (s e) -> p s e", s=G),
                                        count[:, :].unsqueeze(1).to_broadcast([P, G, E]), ALU.add))
                r.did(dve.tensor_copy(pay[:, par, :, :, C + 1].bitcast(I32), target[:, :, :]))
                r.wait(22)
                dve.tensor_tensor(count[:, :], ranks[:, E * G:E * G + E], count[:, :], ALU.add)\
                   .then_inc(stage_copied[at.bank], 1)
                r.did(dve.tensor_scalar(target[:, :, :], target[:, :, :], float(TOP * GT), None, ALU.add))
                r.did(dve.tensor_tensor(mpos[:, :, :, :], mask[:, :, :, :],
                                        pos[:, :, :].unsqueeze(2).to_broadcast([P, G, TOP, E]), ALU.mult))
                r.wait(24)
                with nc.allow_low_precision(reason="row numbers are exact in float32"):
                    r.did(dve.tensor_reduce(slot_at[:, par, :, :], mpos[:, :, :, :], AX.X, ALU.add))
                assert r.at == ROUTE

            def prologue(no):
                low("q", 0, no, 0)
                low("k", 0, no, 0)
                v_copy(no, 0)
                dve.wait_ge(x_loaded, 16)
                take_max(0, 0, 0)
                take_max(0, 1, 0)
                shifts(0, 0)

            def body(g, par, half_g, no, pre, post):
                for s in range(G):
                    b = G * g + s
                    more = pre or s < G - 1
                    p1 = (s + 1) % 2
                    if s == 0:
                        if more:
                            take_max(b + 1, 0, p1)
                        clamp(b, 0)
                        clamp(b, 1)
                        if more:
                            take_max(b + 1, 1, p1)
                            shifts(b + 1, p1)
                        if pre:
                            ln(0, g + 1)
                        if post:
                            residual("wo", g - 1, no)
                        normalise(b, par, s)
                        if post:
                            ln(1, g - 1)
                    if s == 1:
                        if more:
                            take_max(b + 1, 0, p1)
                        clamp(b, 0)
                        if pre:
                            low("k", g + 1, no, 1 - par)
                        clamp(b, 1)
                        if more:
                            take_max(b + 1, 1, p1)
                            shifts(b + 1, p1)
                        if post:
                            norm(1, g - 1, tok, tok_ready)
                        if pre:
                            low("q", g + 1, no, 1 - par)
                        normalise(b, par, s)
                        if post:
                            token_low(g - 1, 1 - par)
                    if s == 2:
                        if more:
                            take_max(b + 1, 0, p1)
                        clamp(b, 0)
                        if pre:
                            v_copy(no, 1 - par)
                        clamp(b, 1)
                        if more:
                            take_max(b + 1, 1, p1)
                            shifts(b + 1, p1)
                        if post:
                            take_logits(g - 1, no)
                        if post:
                            choose(g - 1, no)
                        normalise(b, par, s)
                        if post:
                            weigh(g - 1, 1 - par)
                    if s == 3:
                        if more:
                            take_max(b + 1, 0, p1)
                        clamp(b, 0)
                        clamp(b, 1)
                        if more:
                            take_max(b + 1, 1, p1)
                            shifts(b + 1, p1)
                        if post:
                            place(g - 1, 1 - par, no)
                        normalise(b, par, s)
                        if post:
                            residual("bias", g - 1, no)
                    if not post:
                        for e in experts_of(s):
                            w1_low(e)

            def dense_y(b, k):
                dve.wait_ge(y_filled, k + 1)
                dve.scalar_tensor_tensor(out=xs[:, b, :], in0=y_bank[parity(k)][:, 0:C], scalar=dense_w[:, b:b + 1],
                                         in1=xs[:, b, :], op0=ALU.mult, op1=ALU.add).then_inc(y_read, 1)

            steps = 0

            def did(ins):
                nonlocal steps
                steps += 1
                ins.then_inc(tab_steps, 1)

            def table_counts(no):
                dve.wait_ge(stage_copied[no["rank"].bank], no["rank"].at + 1)
                dve.tensor_copy(tab_pad[:, :], count[0:1, :]).then_inc(table, 1)
                did(dve.scalar_tensor_tensor(out=n_tok[:, :], in0=expert_no[0:1, :], scalar=-float(CAP),
                                             in1=count[0:1, :], op0=ALU.mult, op1=ALU.add))
                dve.wait_ge(tab_steps, steps)
                did(dve.tensor_scalar(n_i[:, :], n_tok[:, :], float(P - 1), None, ALU.add))
                dve.wait_ge(tab_steps, steps)
                did(dve.tensor_scalar(n_tiles_i[:, :], n_i[:, :], P.bit_length() - 1, None, ALU.logical_shift_right))
                dve.wait_ge(tab_steps, steps)
                did(dve.tensor_copy(n_tiles[:, :], n_tiles_i[:, :]))

            def table_ends():
                dve.wait_ge(tab_steps, steps)
                did(dve.tensor_tensor(cum_w[:, :, :], cum_mask[:, :, :],
                                      n_tiles[:, :].unsqueeze(1).to_broadcast([1, E, E]), ALU.mult))
                dve.wait_ge(tab_steps, steps)
                did(dve.tensor_reduce(cum[:, :], cum_w[:, :, :], AX.X, ALU.add))

            def table_experts():
                dve.wait_ge(tab_steps, steps)
                did(dve.tensor_tensor(past[:, :, :], tile_no[:, :].unsqueeze(2).to_broadcast([1, NT, E]),
                                      cum[:, :].unsqueeze(1).to_broadcast([1, NT, E]), ALU.is_ge))
                dve.wait_ge(tab_steps, steps)
                did(dve.tensor_reduce(tile_e[:, :], past[:, :, :], AX.X, ALU.add))

            def table_starts():
                did(dve.tensor_tensor(past_w[:, :, :], past[:, :, :],
                                      n_tiles[:, :].unsqueeze(1).to_broadcast([1, NT, E]), ALU.mult))
                dve.wait_ge(tab_steps, steps)
                did(dve.tensor_reduce(tile_s[:, :], past_w[:, :, :], AX.X, ALU.add))

            def table_rows():
                did(dve.tensor_scalar(tab_w[:, :], tile_e[:, :], float(E - 1), float(FF), ALU.min, ALU.mult))
                did(dve.tensor_scalar(tab_b[:, :], tile_e[:, :], float(E - 1), float(FC), ALU.min, ALU.mult))
                dve.wait_ge(tab_steps, steps)
                did(dve.tensor_tensor(tile_s[:, :], tile_no[:, :], tile_s[:, :], ALU.subtract))
                dve.wait_ge(tab_steps, steps)
                did(dve.tensor_scalar(tile_s[:, :], tile_s[:, :], float(P), None, ALU.mult))
                dve.wait_ge(tab_steps, steps)
                did(dve.scalar_tensor_tensor(out=tile_r[:, :], in0=tile_e[:, :], scalar=float(CAP), in1=tile_s[:, :],
                                             op0=ALU.mult, op1=ALU.add))
                dve.wait_ge(tab_steps, steps)
                dve.tensor_scalar(tab_row[:, :], tile_r[:, :], float(E * CAP), None, ALU.min).then_inc(table, 1)

            def tail(g, par, half_g, no):
                dve.wait_ge(ffn_loaded, 16 * 4)
                dve.tensor_scalar(b1_sb[:, :], b1_sb[:, :], WSCALE, None, ALU.mult).then_inc(consts_v, 1)
                for step in TAIL:
                    if isinstance(step, int):
                        dense_y(step, step)
                    if step == "wo":
                        residual("wo", g, no)
                        dve.wait_ge(stage_copied[no["wo"].bank], no["wo"].at + 1)
                        ln(1, g)
                    if step == "norm":
                        norm(1, g, tok, tok_ready)
                    if step == "low":
                        token_low(g, par)
                    if step == "logits":
                        take_logits(g, no)
                        choose(g, no)
                    if step == "weigh":
                        weigh(g, par)
                    if step == "rank":
                        place(g, par, no)
                    if step == "bias":
                        residual("bias", g, no)
                    if step == "counts":
                        table_counts(no)
                    if step == "ends":
                        table_ends()
                    if step == "experts":
                        table_experts()
                    if step == "starts":
                        table_starts()
                    if step == "rows":
                        table_rows()

            bodies(dve, prologue, body, tail)

            for k in range(TAIL[-1] + 1, ND - 1):
                dense_y(k, k)

            def tile_copy(k, j):
                dve.wait_ge(tile_turned, k + 1)
                if not isinstance(k, int) or k >= 2:
                    dve.wait_ge(hid_filled, ND + k - 1)
                dve.tensor_copy(tileT[:, j % 2, :], turn_bank[j % 2][:, 0:P].bitcast(F16)).then_inc(tile_copied, 1)

            def expert(k, j, it, more, at):
                if more > 1:
                    tile_copy(k + 2, j)
                dve.wait_ge(y_filled, ND + k + 1)
                dve.tensor_scalar(y_sb[:, j, :], y_bank[j % 2][:, 0:C], row_sb[:, j, C:C + 1], None,
                                  ALU.mult).then_inc(y_read, 1)

            tile_copy(0, 0)
            tile_copy(1, 1)
            dense_y(ND - 1, ND - 1)
            expert_tiles(dve, expert)

            def add_back(g):
                dve.wait_ge(back_loaded[g], 16)
                dve.wait_ge(y_read, NT + max(ND, G * g + G))
                xg = xs[:, G * g:G * g + G, :]
                dve.tensor_tensor(xg, xg, back[g][:, :, 0:C], ALU.add).then_inc(sum1, 1)
                dve.wait_ge(sum1, g + 1)
                dve.tensor_tensor(xg, xg, back[g][:, :, C:2 * C], ALU.add).then_inc(sum2, 1)

            first = NB - (NG - 2)
            for k in range(ND, NB):
                dense_y(k, NT + k)
                if k >= first:
                    add_back(k - first)
            for g in range(NG - 2, NG):
                add_back(g)


_INS = ['x', 'ctx_768', 'L0_xattn_Wq', 'L0_xattn_bq', 'L0_xattn_Wk', 'L0_xattn_bk', 'L0_xattn_Wv', 'L0_xattn_bv',
        'L0_xattn_Wo', 'L0_xattn_bo', 'L0_ffn_Wr', 'L0_ffn_br', 'L0_ffn_Wg', 'L0_ffn_bg', 'L0_ffn_W1', 'L0_ffn_b1',
        'L0_ffn_W2', 'L0_ffn_b2', 'L0_ffn_D1', 'L0_ffn_d1b', 'L0_ffn_D2', 'L0_ffn_d2b']
_OUTS = [((32, 128, 128), 'float32')]


def kernel(**inputs):
    import numpy as _np
    import concourse.bacc as _bacc
    from concourse import mybir as _mybir
    from concourse.bass_utils import run_bass_kernel_spmd as _run

    nc = _bacc.Bacc("TRN2", target_bir_lowering=False, num_devices=1)
    arrays, args = {}, []
    for name in _INS:
        a = _np.ascontiguousarray(inputs[name])
        arrays[f"in_{name}_dram"] = a
        args.append(nc.dram_tensor(f"in_{name}_dram", a.shape, _mybir.dt.from_np(a.dtype), kind="ExternalInput").ap())
    for i, (shape, dtype) in enumerate(_OUTS):
        dt = _mybir.dt.from_np(_np.dtype(dtype))
        args.append(nc.dram_tensor(f"out_{i}_dram", shape, dt, kind="ExternalOutput").ap())
    cross_attention_moe(nc, *args)
    r = _run(nc, [arrays], core_ids=[0])
    got = tuple(r.results[0][f"out_{i}_dram"] for i in range(len(_OUTS)))
    return got[0]
```
